# Optimizing a Trainium2 kernel written in Bass

```python
import numpy as np
import jax
import jax.numpy as jnp

def _softmax(x, axis=-1):
    return jax.nn.softmax(x, axis=axis)

def _gelu(x):
    return jax.nn.gelu(x, approximate=True)

def _silu(x):
    return jax.nn.silu(x)

def _sigmoid(x):
    return jax.nn.sigmoid(x)

def _layernorm(x, axis=-1, eps=1e-05):
    m = jnp.mean(x, axis=axis, keepdims=True)
    v = jnp.var(x, axis=axis, keepdims=True)
    return (x - m) / jnp.sqrt(v + eps)

def _scatter_add(tgt, idx, src, axis=0):
    return tgt.at[idx].add(src)

def _segment_sum(src, seg, n):
    return jax.ops.segment_sum(src, seg, n)
kernel_name = 'mk_prb_d2_jaxref_r8_9050da'

def setup_inputs(seed: int=0):
    np.random.seed(seed)
    _w = jnp.asarray

    def _L0_attn_setup():
        import jax, jax.numpy as jnp
        import numpy as np
        N_HEADS = 32
        N_KV_HEADS = 8
        DIM = 512
        HEAD_DIM = DIM // N_HEADS
        N_REP = N_HEADS // N_KV_HEADS
        ROPE_THETA = 10000.0

        def _apply_rope(x):
            seq = x.shape[2]
            hd = x.shape[-1]
            inv_freq = 1.0 / ROPE_THETA ** (jnp.arange(0, hd, 2, dtype=jnp.float32) / hd)
            angles = jnp.arange(seq, dtype=jnp.float32)[:, None] * inv_freq[None, :]
            cos = jnp.cos(angles)[None, None]
            sin = jnp.sin(angles)[None, None]
            x1 = x[..., 0::2]
            x2 = x[..., 1::2]
            r1 = x1 * cos - x2 * sin
            r2 = x1 * sin + x2 * cos
            return jnp.stack([r1, r2], axis=-1).reshape(x.shape)
        key = jax.random.key(seed)
        k1, k2, k3 = jax.random.split(key, 3)
        bs, seq = (1, 256)
        x = jax.random.normal(k1, (bs, seq, DIM), dtype=jnp.float32)
        w_qkv = jax.random.normal(k2, (DIM, HEAD_DIM * (N_HEADS + 2 * N_KV_HEADS)), dtype=jnp.float32) * 0.02
        w_o = jax.random.normal(k3, (N_HEADS * HEAD_DIM, DIM), dtype=jnp.float32) * 0.02
        return {'x': x, 'w_qkv': w_qkv, 'w_o': w_o}
    _L0_attn_in = _L0_attn_setup()

    def _L0_ffn_setup():
        import jax, jax.numpy as jnp
        import numpy as np
        B, S, H, I, R = (4, 32, 512, 1792, 4)

        def _anemll_linear(x, w, su, sv):
            w_eff = w * (su @ sv)
            return jnp.einsum('bsh,oh->bso', x, w_eff)
        key = jax.random.key(seed)
        ks = jax.random.split(key, 10)
        sd = 0.02
        return {'x': jax.random.normal(ks[0], (B, S, H), dtype=jnp.float32), 'gate_w': jax.random.normal(ks[1], (I, H), dtype=jnp.float32) * sd, 'gate_su': jax.random.normal(ks[2], (I, R), dtype=jnp.float32) * 0.5, 'gate_sv': jax.random.normal(ks[3], (R, H), dtype=jnp.float32) * 0.5, 'up_w': jax.random.normal(ks[4], (I, H), dtype=jnp.float32) * sd, 'up_su': jax.random.normal(ks[5], (I, R), dtype=jnp.float32) * 0.5, 'up_sv': jax.random.normal(ks[6], (R, H), dtype=jnp.float32) * 0.5, 'down_w': jax.random.normal(ks[7], (H, I), dtype=jnp.float32) * sd, 'down_su': jax.random.normal(ks[8], (H, R), dtype=jnp.float32) * 0.5, 'down_sv': jax.random.normal(ks[9], (R, I), dtype=jnp.float32) * 0.5}
    _L0_ffn_in = _L0_ffn_setup()

    def _L1_attn_setup():
        import jax, jax.numpy as jnp
        import numpy as np
        HDC_DIM = 512
        N_HEADS = 4
        HEAD_DIM = HDC_DIM // N_HEADS

        def _ste_sign(w):
            alpha = jnp.mean(jnp.abs(w), axis=-1, keepdims=True)
            hard = alpha * jnp.sign(w)
            hard = jnp.where(hard == 0, alpha, hard)
            return jax.lax.stop_gradient(hard - w) + w
        key = jax.random.key(seed)
        kx, kq, kk, kv = jax.random.split(key, 4)
        B, T = (4, 256)
        x = jax.random.normal(kx, (B, T, HDC_DIM), dtype=jnp.float32)
        bv_q = jax.random.normal(kq, (N_HEADS, HEAD_DIM), dtype=jnp.float32) * 0.02
        bv_k = jax.random.normal(kk, (N_HEADS, HEAD_DIM), dtype=jnp.float32) * 0.02
        bv_v = jax.random.normal(kv, (N_HEADS, HEAD_DIM), dtype=jnp.float32) * 0.02
        return {'x': x, 'bv_q': bv_q, 'bv_k': bv_k, 'bv_v': bv_v}
    _L1_attn_in = _L1_attn_setup()

    def _L1_ffn_setup():
        import jax, jax.numpy as jnp
        import numpy as np
        DIM = 512
        HID = 1376
        R = 16
        SCALING = 32.0 / 16.0

        def _lora_linear(x, w, a, b):
            base = jnp.einsum('bsd,od->bso', x, w)
            low = jnp.einsum('bsr,or->bso', jnp.einsum('bsd,rd->bsr', x, a), b)
            return base + low * SCALING
        key = jax.random.key(seed)
        ks = jax.random.split(key, 10)
        s_in = 1.0 / np.sqrt(DIM)
        s_hid = 1.0 / np.sqrt(HID)
        return {'x': jax.random.normal(ks[0], (4, 256, DIM), jnp.float32), 'w1': jax.random.normal(ks[1], (HID, DIM), jnp.float32) * s_in, 'w3': jax.random.normal(ks[2], (HID, DIM), jnp.float32) * s_in, 'w2': jax.random.normal(ks[3], (DIM, HID), jnp.float32) * s_hid, 'lora_A1': jax.random.normal(ks[4], (R, DIM), jnp.float32) * s_in, 'lora_B1': jax.random.normal(ks[5], (HID, R), jnp.float32) * 0.02, 'lora_A3': jax.random.normal(ks[6], (R, DIM), jnp.float32) * s_in, 'lora_B3': jax.random.normal(ks[7], (HID, R), jnp.float32) * 0.02, 'lora_A2': jax.random.normal(ks[8], (R, HID), jnp.float32) * s_hid, 'lora_B2': jax.random.normal(ks[9], (DIM, R), jnp.float32) * 0.02}
    _L1_ffn_in = _L1_ffn_setup()
    _d = {'L0_attn_x': _L0_attn_in['x'], 'L0_attn_w_qkv': _L0_attn_in['w_qkv'], 'L0_attn_w_o': _L0_attn_in['w_o'], 'L0_ffn_gate_w': _L0_ffn_in['gate_w'], 'L0_ffn_gate_su': _L0_ffn_in['gate_su'], 'L0_ffn_gate_sv': _L0_ffn_in['gate_sv'], 'L0_ffn_up_w': _L0_ffn_in['up_w'], 'L0_ffn_up_su': _L0_ffn_in['up_su'], 'L0_ffn_up_sv': _L0_ffn_in['up_sv'], 'L0_ffn_down_w': _L0_ffn_in['down_w'], 'L0_ffn_down_su': _L0_ffn_in['down_su'], 'L0_ffn_down_sv': _L0_ffn_in['down_sv'], 'L1_attn_bv_q': _L1_attn_in['bv_q'], 'L1_attn_bv_k': _L1_attn_in['bv_k'], 'L1_attn_bv_v': _L1_attn_in['bv_v'], 'L1_ffn_w1': _L1_ffn_in['w1'], 'L1_ffn_w3': _L1_ffn_in['w3'], 'L1_ffn_w2': _L1_ffn_in['w2'], 'L1_ffn_lora_A1': _L1_ffn_in['lora_A1'], 'L1_ffn_lora_B1': _L1_ffn_in['lora_B1'], 'L1_ffn_lora_A3': _L1_ffn_in['lora_A3'], 'L1_ffn_lora_B3': _L1_ffn_in['lora_B3'], 'L1_ffn_lora_A2': _L1_ffn_in['lora_A2'], 'L1_ffn_lora_B2': _L1_ffn_in['lora_B2']}
    _x0 = _d['L0_attn_x']
    _d['L0_attn_x'] = jax.random.normal(jax.random.fold_in(jax.random.key(seed), 1), (2, 512, 512), dtype=_x0.dtype)
    del _x0
    return _d

def reference(L0_attn_x, L0_attn_w_qkv, L0_attn_w_o, L0_ffn_gate_w, L0_ffn_gate_su, L0_ffn_gate_sv, L0_ffn_up_w, L0_ffn_up_su, L0_ffn_up_sv, L0_ffn_down_w, L0_ffn_down_su, L0_ffn_down_sv, L1_attn_bv_q, L1_attn_bv_k, L1_attn_bv_v, L1_ffn_w1, L1_ffn_w3, L1_ffn_w2, L1_ffn_lora_A1, L1_ffn_lora_B1, L1_ffn_lora_A3, L1_ffn_lora_B3, L1_ffn_lora_A2, L1_ffn_lora_B2):

    def _L0_attn_ref(x, w_qkv, w_o):
        import jax, jax.numpy as jnp
        import numpy as np
        N_HEADS = 32
        N_KV_HEADS = 8
        DIM = 512
        HEAD_DIM = DIM // N_HEADS
        N_REP = N_HEADS // N_KV_HEADS
        ROPE_THETA = 10000.0

        def _apply_rope(x):
            seq = x.shape[2]
            hd = x.shape[-1]
            inv_freq = 1.0 / ROPE_THETA ** (jnp.arange(0, hd, 2, dtype=jnp.float32) / hd)
            angles = jnp.arange(seq, dtype=jnp.float32)[:, None] * inv_freq[None, :]
            cos = jnp.cos(angles)[None, None]
            sin = jnp.sin(angles)[None, None]
            x1 = x[..., 0::2]
            x2 = x[..., 1::2]
            r1 = x1 * cos - x2 * sin
            r2 = x1 * sin + x2 * cos
            return jnp.stack([r1, r2], axis=-1).reshape(x.shape)
        bs, seq, _ = x.shape
        qkv = x @ w_qkv
        q_sz = N_HEADS * HEAD_DIM
        kv_sz = N_KV_HEADS * HEAD_DIM
        xq = qkv[..., :q_sz].reshape(bs, seq, N_HEADS, HEAD_DIM).transpose(0, 2, 1, 3)
        xk = qkv[..., q_sz:q_sz + kv_sz].reshape(bs, seq, N_KV_HEADS, HEAD_DIM).transpose(0, 2, 1, 3)
        xv = qkv[..., q_sz + kv_sz:].reshape(bs, seq, N_KV_HEADS, HEAD_DIM).transpose(0, 2, 1, 3)
        xq = _apply_rope(xq)
        xk = _apply_rope(xk)
        keys = jnp.repeat(xk, N_REP, axis=1)
        values = jnp.repeat(xv, N_REP, axis=1)
        scale = 1.0 / jnp.sqrt(jnp.float32(HEAD_DIM))
        scores = jnp.einsum('bhsd,bhtd->bhst', xq, keys) * scale
        causal = jnp.tril(jnp.ones((seq, seq), dtype=bool))[None, None]
        scores = jnp.where(causal, scores, -jnp.inf)
        probs = jax.nn.softmax(scores, axis=-1)
        out = jnp.einsum('bhst,bhtd->bhsd', probs, values)
        out = out.transpose(0, 2, 1, 3).reshape(bs, seq, N_HEADS * HEAD_DIM)
        return out @ w_o

    def _L0_ffn_ref(x, gate_w, gate_su, gate_sv, up_w, up_su, up_sv, down_w, down_su, down_sv):
        import jax, jax.numpy as jnp
        import numpy as np
        B, S, H, I, R = (4, 32, 512, 1792, 4)

        def _anemll_linear(x, w, su, sv):
            w_eff = w * (su @ sv)
            return jnp.einsum('bsh,oh->bso', x, w_eff)
        a = _anemll_linear(x, gate_w, gate_su, gate_sv)
        b = _anemll_linear(x, up_w, up_su, up_sv)
        d = jax.nn.silu(a) * b
        return _anemll_linear(d, down_w, down_su, down_sv)

    def _L1_attn_ref(x, bv_q, bv_k, bv_v):
        import jax, jax.numpy as jnp
        import numpy as np
        HDC_DIM = 512
        N_HEADS = 4
        HEAD_DIM = HDC_DIM // N_HEADS

        def _ste_sign(w):
            alpha = jnp.mean(jnp.abs(w), axis=-1, keepdims=True)
            hard = alpha * jnp.sign(w)
            hard = jnp.where(hard == 0, alpha, hard)
            return jax.lax.stop_gradient(hard - w) + w
        B, T, D = x.shape
        H, HD = (N_HEADS, HEAD_DIM)
        scale = HD ** (-0.5)
        q_bind = _ste_sign(bv_q)
        k_bind = _ste_sign(bv_k)
        v_bind = _ste_sign(bv_v)
        xh = x.reshape(B, T, H, HD)
        Q = xh * q_bind
        K = xh * k_bind
        V = xh * v_bind
        scores = jnp.einsum('bthd,bshd->bhts', Q, K) * scale
        causal = jnp.tril(jnp.ones((T, T), dtype=bool))
        attn = jnp.where(causal, jax.nn.sigmoid(scores * 4.0), 0.0)
        out = jnp.einsum('bhts,bshd->bthd', attn, V)
        return out.reshape(B, T, D)

    def _L1_ffn_ref(x, w1, w3, w2, lora_A1, lora_B1, lora_A3, lora_B3, lora_A2, lora_B2):
        import jax, jax.numpy as jnp
        import numpy as np
        DIM = 512
        HID = 1376
        R = 16
        SCALING = 32.0 / 16.0

        def _lora_linear(x, w, a, b):
            base = jnp.einsum('bsd,od->bso', x, w)
            low = jnp.einsum('bsr,or->bso', jnp.einsum('bsd,rd->bsr', x, a), b)
            return base + low * SCALING
        h1 = _lora_linear(x, w1, lora_A1, lora_B1)
        h3 = _lora_linear(x, w3, lora_A3, lora_B3)
        g = jax.nn.silu(h1) * h3
        return _lora_linear(g, w2, lora_A2, lora_B2)
    x = L0_attn_x
    xn = _layernorm(x, axis=-1)
    x = x + _L0_attn_ref(xn, L0_attn_w_qkv, L0_attn_w_o) + _L0_ffn_ref(xn, L0_ffn_gate_w, L0_ffn_gate_su, L0_ffn_gate_sv, L0_ffn_up_w, L0_ffn_up_su, L0_ffn_up_sv, L0_ffn_down_w, L0_ffn_down_su, L0_ffn_down_sv)
    xn = _layernorm(x, axis=-1)
    x = x + _L1_attn_ref(xn, L1_attn_bv_q, L1_attn_bv_k, L1_attn_bv_v) + _L1_ffn_ref(xn, L1_ffn_w1, L1_ffn_w3, L1_ffn_w2, L1_ffn_lora_A1, L1_ffn_lora_B1, L1_ffn_lora_A3, L1_ffn_lora_B3, L1_ffn_lora_A2, L1_ffn_lora_B2)
    return x

_drawn_inputs = setup_inputs


def setup_inputs(seed=0):
    import zlib

    import numpy as np

    out = dict(_drawn_inputs(seed))
    spreads = {}
    factors = {}
    for name, (base, spread) in spreads.items():
        noise = np.random.default_rng([zlib.crc32(name.encode()), seed]).standard_normal(out[name].shape)
        drawn = base * np.exp(spread * noise) if base else spread * noise
        out[name] = jnp.asarray(drawn.astype(out[name].dtype))
    for name, factor in factors.items():
        out[name] = (out[name] * factor).astype(out[name].dtype)
    return out
```

```python
import concourse.bass as bass
from concourse import mybir
from contextlib import ExitStack
import numpy as np

F32 = mybir.dt.float32
F32R = mybir.dt.float32r
BF16 = mybir.dt.bfloat16
ALU = mybir.AluOpType
ACT = mybir.ActivationFunctionType
AXX = mybir.AxisListType.X

P = 128
B, S, D = 2, 512, 512
T = B * S
NT = T // P
NJ = S // P
NC = D // P
HEADS, KV, HD = 32, 8, 16
REP = HEADS // KV
FR = HD // 2
GROUPS = B * KV
STK = 3 * HD + 1
H1 = 4
EPS = 1e-5
NEG = -1.0e30
QW = (HEADS + 2 * KV) * HD
CH0, CH1 = 1792 // P, 11
S1_PIECES = [(0, 0, 4), (1, 0, 2), (1, 2, 2)] + [(i, h, 1) for i in (2, 3) for h in range(4)]
S2_PIECES = [(j, h, 1) for j in (0, 1) for h in range(4)] + [(2, 0, 2), (2, 2, 2), (3, 0, 4)]
S2_END = [4, 8, 10, 11]
STEPS = 16 * 14
G_STEPS = 14
VALUES_AT = [8, 11, 13, 14]
BLK = [0, 512, 896, 1152]
CAUSAL = 1280


class Env:
    pass


def three_pass(pe, out, w_hi, w_lo, m_hi, m_lo, first, last):
    pe.matmul(out, w_hi, m_hi, start=first, stop=False, skip_group_check=True)
    pe.matmul(out, w_lo, m_hi, start=False, stop=False, skip_group_check=True)
    return pe.matmul(out, w_hi, m_lo, start=False, stop=last, skip_group_check=True)


def f32(ap):
    return ap.bitcast(F32)


class Norm:

    def __init__(self, nc, ctx, tag, banks, ident, xT_hi, xT_lo, loaded, loads):
        sb = lambda n, s, d=F32: ctx.enter_context(nc.sbuf_tensor(f"{tag}_{n}", s, d))
        sem = lambda n: nc.alloc_semaphore(f"{tag}_{n}")
        self.x = sb("x", [P, NT, D])
        self.stats = sb("stats", [P, NT, 6])
        self.mv = sb("mv", [P, NT, 2])
        self.std = sb("std", [P, NT])
        self.rstd = sb("rstd", [P, NT])
        self.banks, self.ident, self.xT_hi, self.xT_lo = banks, ident, xT_hi, xT_lo
        self.loaded, self.loads = loaded, loads
        self.raw = sem("stats_raw")
        self.stat = sem("stats_ready")
        self.stdd = sem("std_ready")
        self.rst = sem("rstd_ready")
        self.normed = sem("normed")
        self.transposed = sem("transposed")
        self.hi = sem("xT_hi_ready")
        self.lo = sem("xT_lo_ready")

    def tile(self, t):
        return self.x[:, t, :]

    def load(self, eng, x_dram, t):
        eng.dma_start(self.x[:, t, :], x_dram[t * P:(t + 1) * P, :]).then_inc(self.loaded[t], 16)

    def dve_stats(self, dve, t):
        dve.wait_ge(self.loaded[t], self.loads)
        dve.bn_stats(self.stats[:, t, :], self.x[:, t, :]).then_inc(self.raw, 1)
        dve.wait_ge(self.raw, t + 1)
        dve.bn_aggr(self.mv[:, t, :], self.stats[:, t, :]).then_inc(self.stat, 1)

    def act_std(self, act, t):
        act.wait_ge(self.stat, t + 1)
        act.activation(self.std[:, t:t + 1], self.mv[:, t, 1:2], ACT.Sqrt, bias=EPS, scale=1.0).then_inc(self.stdd, 1)

    def dve_norm(self, dve, t):
        dve.wait_ge(self.stdd, t + 1)
        dve.reciprocal(self.rstd[:, t:t + 1], self.std[:, t:t + 1]).then_inc(self.rst, 1)
        dve.wait_ge(self.rst, t + 1)
        dve.tensor_scalar(self.tile(t), self.x[:, t, :], self.mv[:, t, 0:1], self.rstd[:, t:t + 1],
                          ALU.subtract, ALU.mult).then_inc(self.normed, 1)

    def pe_transpose(self, pe, t):
        pe.wait_ge(self.normed, t + 1)
        if t >= 2:
            pe.wait_ge(self.lo, t - 1)
        for c in range(NC):
            last = pe.transpose(self.banks[t % 2][:, c * P:(c + 1) * P], self.tile(t)[:, c * P:(c + 1) * P],
                                self.ident[:, :])
        last.then_inc(self.transposed, 1)

    def act_hi(self, act, t):
        act.wait_ge(self.transposed, t + 1)
        act.activation(self.xT_hi[:, :, t * P:(t + 1) * P],
                       self.banks[t % 2][:, :].rearrange("p (c s) -> p c s", c=NC), ACT.Copy).then_inc(self.hi, 1)

    def dve_lo(self, dve, t):
        dve.wait_ge(self.hi, t + 1)
        dve.tensor_tensor(self.xT_lo[:, :, t * P:(t + 1) * P],
                          self.banks[t % 2][:, :].rearrange("p (c s) -> p c s", c=NC),
                          f32(self.xT_hi[:, :, t * P:(t + 1) * P]), ALU.subtract).then_inc(self.lo, 1)


def stack_hi(act, stack, raw, loaded, done):
    act.wait_ge(loaded, 16)
    act.activation(stack[:, :], raw[:, :], ACT.Copy).then_inc(done, 1)


def stack_lo(dve, stack, raw, left, hi_done):
    dve.wait_ge(hi_done, 1)
    dve.tensor_tensor(stack[64:96, 0:left], raw[64:96, 0:left], f32(stack[64:96, 0:left]), ALU.subtract)
    dve.tensor_tensor(stack[32:64, left:], raw[32:64, left:], f32(stack[32:64, left:]), ALU.subtract)


class Up:
    def __init__(self, nc, ctx, tag, n, combine, banks, w_dram, xT_hi, xT_lo, lr, hid):
        sb = lambda nm, s, d=F32: ctx.enter_context(nc.sbuf_tensor(f"{tag}_{nm}", s, d))
        sem = lambda nm: nc.alloc_semaphore(f"{tag}_{nm}")
        self.n, self.combine, self.banks, self.w_dram = n, combine, banks, w_dram
        self.xT_hi, self.xT_lo, self.lr, self.hid = xT_hi, xT_lo, lr, hid
        self.w_raw = sb("w_raw", [P, 2, 2, NC, P])
        self.w_eff = sb("w_eff", [P, 2, NC, P])
        self.w_hi = sb("w_hi", [P, 2, 2, NC, P], F32R)
        self.w_lo = sb("w_lo", [P, 2, 2, NC, P], F32R)
        self.th = sb("tanh", [P, 2, S])
        self.ut = sb("gated", [P, 2, S])
        self.raw = [sem("w_raw0"), sem("w_raw1")]
        self.fac = sem("factor_mm")
        self.eff = [sem("gate_eff"), sem("up_eff")]
        self.whi = sem("w_hi_ready")
        self.wlo = sem("w_lo_ready")
        self.mm = sem("gate_up_mm")
        self.tanh = sem("tanh_ready")
        self.u = sem("gated_ready")
        self.h = sem("hidden_ready")

    def sp_load(self, sp, o):
        if o >= 2:
            sp.wait_ge(self.eff[1], o - 1)
        sp.dma_start(self.w_raw[:, o % 2], self.w_dram[o]).then_inc(self.raw[o % 2], 16)

    def pe_factor(self, pe, o, k):
        unit = 6 * o + k
        if k == 0 and o >= 2:
            pe.wait_ge(self.h, 2 * (o - 2) + 1)
        if k == 1 and o >= 2:
            pe.wait_ge(self.u, 2 * (o - 2) + 2)
        if k == 1 and o == 1:
            pe.wait_ge(self.eff[0], 1)
        unit = (0 if o == 0 else 6 * (o - 1) + 2) + k
        n = self.n * P
        for c in range(NC):
            last = pe.matmul(self.banks[unit % 3][:, c * P:(c + 1) * P],
                             self.lr[0:96, k * D + c * P:k * D + (c + 1) * P],
                             self.lr[0:96, 2 * D + k * n + o * P:2 * D + k * n + (o + 1) * P],
                             start=True, stop=True)
        last.then_inc(self.fac, 1)

    def factor_bank(self, o, k):
        return self.banks[((0 if o == 0 else 6 * (o - 1) + 2) + k) % 3]

    def dve_combine(self, dve, o, k):
        dve.wait_ge(self.fac, 2 * o + k + 1)
        dve.wait_ge(self.raw[o % 2], 16 * (o // 2 + 1))
        if o >= 1:
            dve.wait_ge(self.wlo, 2 * (o - 1) + k + 1)
        op0, scale, op1 = self.combine
        dve.scalar_tensor_tensor(out=self.w_eff[:, k].rearrange("p c m -> p (c m)"), in0=self.factor_bank(o, k)[:, :],
                                 scalar=scale, in1=self.w_raw[:, o % 2, k].rearrange("p c m -> p (c m)"),
                                 op0=op0, op1=op1).then_inc(self.eff[k], 1)

    def act_hi(self, act, o, k):
        act.wait_ge(self.eff[k], o + 1)
        if o >= 2:
            act.wait_ge(self.mm, 4 * (o - 1))
        act.activation(self.w_hi[:, o % 2, k], self.w_eff[:, k], ACT.Copy).then_inc(self.whi, 1)

    def pool_lo(self, pool, o, k):
        pool.wait_ge(self.whi, 2 * o + k + 1)
        pool.tensor_tensor(self.w_lo[:, o % 2, k], self.w_eff[:, k], f32(self.w_hi[:, o % 2, k]),
                           ALU.subtract).then_inc(self.wlo, 1)

    def pe_product(self, pe, o, b, k, c):
        more = o + 1 < self.n
        if c == 0:
            if b == 0:
                pe.wait_ge(self.wlo, 2 * o + k + 1)
            if (b, k) == (0, 0):
                if o >= 1:
                    pe.wait_ge(self.h, 2 * o)
                else:
                    pe.wait_ge(self.eff[1], 1)
            if (b, k) == (0, 1) and more:
                pe.wait_ge(self.eff[0], o + 2)
            if (b, k) == (1, 0) and more:
                pe.wait_ge(self.eff[1], o + 2)
            if (b, k) == (1, 1):
                pe.wait_ge(self.u, 2 * o + 1)
        last = three_pass(pe, self.product_bank(o, b, k)[:, :], self.w_hi[:, o % 2, k, c, :], self.w_lo[:, o % 2, k, c, :],
                          self.xT_hi[:, c, b * S:(b + 1) * S], self.xT_lo[:, c, b * S:(b + 1) * S],
                          c == 0, c == NC - 1)
        if c == NC - 1:
            last.then_inc(self.mm, 1)

    def pe_step(self, pe, o, r):
        if r in (0, 1) and o + 1 < self.n:
            self.pe_factor(pe, o + 1, r)
        self.pe_product(pe, o, r // 8, r // 4 % 2, r % 4)

    def dve_step(self, dve, o, r):
        if r == 0 and o >= 1:
            self.dve_hidden(dve, o - 1, 1)
        if r in (1, 2) and o + 1 < self.n:
            self.dve_combine(dve, o + 1, r - 1)
        if r in (5, 13):
            self.dve_gate(dve, o, r // 8)
        if r == 8:
            self.dve_hidden(dve, o, 0)

    def act_step(self, act, o, r):
        if r in (2, 3) and o + 1 < self.n:
            self.act_hi(act, o + 1, r - 2)
        if r in (4, 12):
            self.act_tanh(act, o, r // 8)

    def pool_step(self, pool, o, r):
        if r in (3, 4) and o + 1 < self.n:
            self.pool_lo(pool, o + 1, r - 3)

    def product_bank(self, o, b, k):
        return self.banks[(6 * o + 4 + 2 * b + k) % 3]

    def act_tanh(self, act, o, b):
        act.wait_ge(self.mm, 4 * o + 2 * b + 1)
        if o >= 1:
            act.wait_ge(self.u, 2 * (o - 1) + b + 1)
        act.activation(self.th[:, b, :], self.product_bank(o, b, 0)[:, :], ACT.Tanh, scale=0.5).then_inc(self.tanh, 1)

    def dve_gate(self, dve, o, b):
        dve.wait_ge(self.tanh, 2 * o + b + 1)
        if o >= 1:
            dve.wait_ge(self.h, 2 * (o - 1) + b + 1)
        dve.scalar_tensor_tensor(out=self.ut[:, b, :], in0=self.th[:, b, :], scalar=1.0,
                                 in1=self.product_bank(o, b, 0)[:, :], op0=ALU.add, op1=ALU.mult).then_inc(self.u, 1)

    def dve_hidden(self, dve, o, b):
        dve.wait_ge(self.mm, 4 * o + 2 * b + 2)
        dve.wait_ge(self.u, 2 * o + b + 1)
        dve.scalar_tensor_tensor(out=self.hid[:, o, b * S:(b + 1) * S], in0=self.ut[:, b, :], scalar=0.5,
                                 in1=self.product_bank(o, b, 1)[:, :], op0=ALU.mult, op1=ALU.mult).then_inc(self.h, 1)


class Down:
    def __init__(self, nc, ctx, tag, n, combine, banks, fac_banks, w_dram, lr, hid, res_dram, out_dram):
        sb = lambda nm, s, d=F32: ctx.enter_context(nc.sbuf_tensor(f"{tag}_{nm}", s, d))
        sem = lambda nm: nc.alloc_semaphore(f"{tag}_{nm}")
        self.n, self.combine, self.banks, self.fac_banks, self.w_dram = n, combine, banks, fac_banks, w_dram
        self.lr, self.hid, self.res_dram, self.out_dram = lr, hid, res_dram, out_dram
        self.half = [(0, (n + 1) // 2), ((n + 1) // 2, n)]
        m = (n + 1) // 2
        self.w_raw = sb("w_raw", [P, 2, D])
        self.w_eff = sb("w_eff", [P, D])
        self.w_hi = sb("w_hi", [P, n, D], F32R)
        self.w_lo = sb("w_lo", [P, n, D], F32R)
        self.h_hi = sb("h_hi", [P, 2, m, P], F32R)
        self.h_lo = sb("h_lo", [P, 2, m, P], F32R)
        self.res = sb("res", [P, 2, D])
        self.raw = [sem("w_raw0"), sem("w_raw1")]
        self.fac = sem("factor_mm")
        self.eff = sem("w_eff_ready")
        self.whi = sem("w_hi_ready")
        self.wlo = sem("w_lo_ready")
        self.hhi = sem("h_hi_ready")
        self.hlo = sem("h_lo_ready")
        self.mm = sem("down_mm")
        self.full, self.full_by = sem("tile_mm"), 1
        self.resin = [sem("res_in0"), sem("res_in1")]
        self.sum = sem("sum_ready")
        self.stored = [sem("stored0"), sem("stored1")]

    def sp_load(self, sp, o):
        if o >= 2:
            sp.wait_ge(self.eff, o - 1)
        sp.dma_start(self.w_raw[:, o % 2, :], self.w_dram[o * P:(o + 1) * P, :]).then_inc(self.raw[o % 2], 16)

    def pe_factor(self, pe, o):
        if o >= 2:
            pe.wait_ge(self.eff, o - 1)
        pe.matmul(self.fac_banks[o % 2][:, :], self.lr[0:96, o * P:(o + 1) * P],
                  self.lr[0:96, self.n * P:self.n * P + D], start=True, stop=True).then_inc(self.fac, 1)

    def dve_combine(self, dve, o):
        dve.wait_ge(self.fac, o + 1)
        dve.wait_ge(self.raw[o % 2], 16 * (o // 2 + 1))
        if o >= 1:
            dve.wait_ge(self.wlo, o)
        op0, scale, op1 = self.combine
        dve.scalar_tensor_tensor(out=self.w_eff[:, :], in0=self.fac_banks[o % 2][:, :], scalar=scale,
                                 in1=self.w_raw[:, o % 2, :], op0=op0, op1=op1).then_inc(self.eff, 1)

    def act_whi(self, act, o):
        act.wait_ge(self.eff, o + 1)
        act.activation(self.w_hi[:, o, :], self.w_eff[:, :], ACT.Copy).then_inc(self.whi, 1)

    def dve_wlo(self, dve, o):
        dve.wait_ge(self.whi, o + 1)
        dve.tensor_tensor(self.w_lo[:, o, :], self.w_eff[:, :], f32(self.w_hi[:, o, :]), ALU.subtract).then_inc(self.wlo, 1)

    def act_hhi(self, act, t, q):
        k = 2 * t + q
        o0, o1 = self.half[q]
        if k >= 2:
            act.wait_ge(self.mm, k - 1)
        act.activation(self.h_hi[:, k % 2, 0:o1 - o0, :], self.hid[:, o0:o1, t * P:(t + 1) * P],
                       ACT.Copy).then_inc(self.hhi, 1)

    def pool_hlo(self, pool, t, q):
        k = 2 * t + q
        o0, o1 = self.half[q]
        pool.wait_ge(self.hhi, k + 1)
        pool.tensor_tensor(self.h_lo[:, k % 2, 0:o1 - o0, :], self.hid[:, o0:o1, t * P:(t + 1) * P],
                           f32(self.h_hi[:, k % 2, 0:o1 - o0, :]), ALU.subtract).then_inc(self.hlo, 1)

    def pe_half(self, pe, t, q):
        k = 2 * t + q
        pe.wait_ge(self.hlo, k + 1)
        if q == 0 and t >= 2:
            pe.wait_ge(self.sum, t - 1)
        o0, o1 = self.half[q]
        for o in range(o0, o1):
            if t == 0:
                pe.wait_ge(self.wlo, o + 1)
            last = three_pass(pe, self.banks[t % 2][:, :], self.h_hi[:, k % 2, o - o0, :], self.h_lo[:, k % 2, o - o0, :],
                              self.w_hi[:, o, :], self.w_lo[:, o, :], o == 0, False)
        last.then_inc(self.mm, 1)

    def sp_res(self, sp, t):
        if t >= 2:
            sp.wait_ge(self.stored[t % 2], 16 * (t // 2))
        sp.dma_start(self.res[:, t % 2, :], self.res_dram[t * P:(t + 1) * P, :]).then_inc(self.resin[t % 2], 16)

    def dve_sum(self, dve, t):
        dve.wait_ge(self.full, self.full_by * (t + 1))
        dve.wait_ge(self.resin[t % 2], 16 * (t // 2 + 1))
        dve.tensor_tensor(self.res[:, t % 2, :], self.res[:, t % 2, :], self.banks[t % 2][:, :],
                          ALU.add).then_inc(self.sum, 1)

    def sp_store(self, sp, t):
        sp.wait_ge(self.sum, t + 1)
        sp.dma_start(self.out_dram[t * P:(t + 1) * P, :], self.res[:, t % 2, :]).then_inc(self.stored[t % 2], 16)

    def sp_stored(self, sp):
        for s in self.stored:
            sp.wait_ge(s, 16 * (NT // 2))


def qkv_stage(nc, e, d):
    with ExitStack() as ctx:
        sb = lambda n, s, dt=F32: ctx.enter_context(nc.sbuf_tensor(n, s, dt))
        sem = lambda n: nc.alloc_semaphore(n)
        norm = Norm(nc, ctx, "norm0", [e.bank[4], e.bank[5]], e.ident, e.xT_hi, e.xT_lo, e.x_loaded, 16)
        w_raw = sb("wqkv_raw", [P, NC, QW])
        w_hi = sb("wqkv_hi", [P, NC, QW], F32R)
        w_lo = sb("wqkv_lo", [P, NC, QW], F32R)
        cos = sb("cos", [P, S])
        sin = sb("sin", [P, S])
        prod = sb("rope_products", [P, 2, 4, S])
        rot = sb("rope_sum", [P, 2, 2, S])
        rot_hi = sb("rope_hi", [P, 2, 2, S], F32R)
        rot_lo = sb("rope_lo", [P, 2, 2, S], F32R)
        lr_raw = sb("lr0_raw", [96, e.lr0.shape[1]])
        lrd_raw = sb("lrd0_raw", [96, e.lrd0.shape[1]])
        w_loaded = [sem(f"wqkv_loaded{c}") for c in range(NC)]
        consts = sem("rope_tables_loaded")
        lr_in, lrd_in, lr_hi, lrd_hi = sem("lr0_loaded"), sem("lrd0_loaded"), sem("lr0_hi"), sem("lrd0_hi")
        w_hi_ready, w_lo_ready = sem("wqkv_hi_ready"), sem("wqkv_lo_ready")
        v_mm, v_ones = sem("v_mm"), sem("v_ones")
        pair_mm, products, summed, hi_ready, lo_ready = (sem("pair_mm"), sem("rope_prod_ready"), sem("rope_summed"),
                                                         sem("rope_hi_ready"), sem("rope_lo_ready"))
        stored = [sem("rope_stored0"), sem("rope_stored1")]
        pairs = [(b, k) for b in range(B) for k in range(3)]
        rows = [KV * FR, P, P]
        cols = [(4 * P, 4 * P + KV * FR), (0, 2 * P), (P, 3 * P)]

        with nc.Block() as block:
            @block.sync
            def _(sp):
                sp.dma_start(e.ident[:, :], d["ident"]).then_inc(e.ident_in, 16)
                for t in range(2):
                    norm.load(sp, d["x"], t)
                for c in range(NC):
                    sp.dma_start(w_raw[:, c, :], d["w_qkv"][c * P:(c + 1) * P, :]).then_inc(w_loaded[c], 16)
                for t in range(2, NT):
                    norm.load(sp, d["x"], t)
                sp.dma_start(cos[:, :], d["cos"]).then_inc(consts, 16)
                sp.dma_start(sin[:, :], d["sin"]).then_inc(consts, 16)
                sp.dma_start(lr_raw[:, :], d["lr0"]).then_inc(lr_in, 16)
                sp.dma_start(lrd_raw[:, :], d["lrd0"]).then_inc(lrd_in, 16)
                sp.dma_start(e.mask[:, :, :], d["mask"]).then_inc(e.mask_in, 16)
                sp.dma_start(e.identb[:, :], d["identb"]).then_inc(e.mask_in, 16)
                for n, (b, k) in enumerate(pairs):
                    sp.wait_ge(lo_ready, n + 1)
                    dst = [e.k_hi, e.k_lo] if k == 0 else [e.q_hi, e.q_lo]
                    h0, nh = (0, KV) if k == 0 else (16 * (k - 1), 16)
                    for part, src in enumerate((rot_hi, rot_lo)):
                        for r in range(2):
                            sp.dma_start(dst[part][b, r, :, h0:h0 + nh, :].rearrange("f h s -> h f s"),
                                         f32(src[0:rows[k], n % 2, r, :])).then_inc(stored[n % 2], 16)
                for s in stored:
                    sp.wait_ge(s, 64 * (len(pairs) // 2))

            @block.gpsimd
            def _(pool):
                for b in range(B):
                    pool.memset(e.v[:, b], 1.0).then_inc(v_ones, 1)
                for c in range(NC):
                    pool.wait_ge(w_hi_ready, c + 1)
                    pool.tensor_tensor(w_lo[:, c, :], w_raw[:, c, :], f32(w_hi[:, c, :]), ALU.subtract).then_inc(w_lo_ready, 1)
                for n, (b, k) in enumerate(pairs):
                    pool.wait_ge(products, 4 * (n + 1))
                    if n >= 2:
                        pool.wait_ge(lo_ready, n - 1)
                    R = rows[k]
                    pool.tensor_tensor(rot[0:R, n % 2, 0, :], prod[0:R, n % 2, 0, :], prod[0:R, n % 2, 1, :],
                                       ALU.subtract).then_inc(summed, 1)
                    pool.tensor_tensor(rot[0:R, n % 2, 1, :], prod[0:R, n % 2, 2, :], prod[0:R, n % 2, 3, :],
                                       ALU.add).then_inc(summed, 1)

            @block.scalar
            def _(act):
                for t in range(NT):
                    norm.act_std(act, t)
                    if t < NC:
                        act.wait_ge(w_loaded[t], 16)
                        act.activation(w_hi[:, t, :], w_raw[:, t, :], ACT.Copy).then_inc(w_hi_ready, 1)
                    if t >= 1:
                        norm.act_hi(act, t - 1)
                norm.act_hi(act, NT - 1)
                stack_hi(act, e.lr0, lr_raw, lr_in, lr_hi)
                stack_hi(act, e.lrd0, lrd_raw, lrd_in, lrd_hi)
                act.wait_ge(v_ones, B)
                for n, (b, k) in enumerate(pairs):
                    if k == 0:
                        act.wait_ge(v_mm, b + 1)
                        act.activation(e.v[:, b, :, :, 0:HD],
                                       e.bank[6 + b][:, :].rearrange("p (j g x) -> p j g x", j=NJ, g=KV), ACT.Copy)
                    act.wait_ge(summed, 2 * (n + 1))
                    if n >= 2:
                        act.wait_ge(stored[n % 2], 64 * (n // 2))
                    act.activation(rot_hi[0:rows[k], n % 2], rot[0:rows[k], n % 2], ACT.Copy).then_inc(hi_ready, 1)

            @block.vector
            def _(dve):
                norm.dve_stats(dve, 0)
                for t in range(NT):
                    if t + 1 < NT:
                        norm.dve_stats(dve, t + 1)
                    norm.dve_norm(dve, t)
                    if t >= 1:
                        norm.dve_lo(dve, t - 1)
                norm.dve_lo(dve, NT - 1)
                dve.wait_ge(consts, 32)

                def rest(n):
                    R = rows[pairs[n][1]]
                    dve.wait_ge(hi_ready, n + 1)
                    dve.tensor_tensor(rot_lo[0:R, n % 2], rot[0:R, n % 2], f32(rot_hi[0:R, n % 2]),
                                      ALU.subtract).then_inc(lo_ready, 1)

                for n, (b, k) in enumerate(pairs):
                    dve.wait_ge(pair_mm, n + 1)
                    if n >= 2:
                        dve.wait_ge(summed, 2 * (n - 1))
                    R = rows[k]
                    scale = 1.0 if k == 0 else HD ** -0.5
                    for m, (src, table) in enumerate(((0, cos), (1, sin), (0, sin), (1, cos))):
                        dve.scalar_tensor_tensor(out=prod[0:R, n % 2, m, :], in0=e.bank[2 * (n % 2) + src][0:R, :],
                                                 scalar=scale, in1=table[0:R, :], op0=ALU.mult,
                                                 op1=ALU.mult).then_inc(products, 1)
                    if n >= 1:
                        rest(n - 1)
                rest(len(pairs) - 1)
                stack_lo(dve, e.lr0, lr_raw, 2 * D, lr_hi)
                stack_lo(dve, e.lrd0, lrd_raw, CH0 * P, lrd_hi)

            @block.tensor
            def _(pe):
                pe.wait_ge(e.ident_in, 16)

                def products_of(b):
                    pe.wait_ge(norm.lo, NJ * (b + 1))
                    if b == 0:
                        pe.wait_ge(w_lo_ready, NC)
                    for n in range(3 * b, 3 * b + 3):
                        k = pairs[n][1]
                        if n >= 2:
                            pe.wait_ge(products, 4 * (n - 1))
                        for r in range(2):
                            c0 = cols[k][r]
                            for c in range(NC):
                                last = three_pass(pe, e.bank[2 * (n % 2) + r][0:rows[k], :], w_hi[:, c, c0:c0 + rows[k]],
                                                  w_lo[:, c, c0:c0 + rows[k]], e.xT_hi[:, c, b * S:(b + 1) * S],
                                                  e.xT_lo[:, c, b * S:(b + 1) * S], c == 0, c == NC - 1)
                        last.then_inc(pair_mm, 1)
                    for j in range(NJ):
                        tok = slice(b * S + j * P, b * S + (j + 1) * P)
                        for c in range(NC):
                            last = three_pass(pe, e.bank[6 + b][:, j * P:(j + 1) * P], e.xT_hi[:, c, tok], e.xT_lo[:, c, tok],
                                              w_hi[:, c, 5 * P:6 * P], w_lo[:, c, 5 * P:6 * P], c == 0, c == NC - 1)
                    last.then_inc(v_mm, 1)

                for t in range(NT):
                    norm.pe_transpose(pe, t)
                for b in range(B):
                    products_of(b)


def attention_stage(nc, e, d):
    with ExitStack() as ctx:
        sb = lambda n, s, dt=F32: ctx.enter_context(nc.sbuf_tensor(n, s, dt))
        sem = lambda n: nc.alloc_semaphore(n)
        up = Up(nc, ctx, "up0", CH0, (ALU.mult, 1.0, ALU.mult), e.bank[0:3], d["w_gate_up0"], e.xT_hi, e.xT_lo, e.lr0, e.hid)
        qst = sb("q_stack", [64 + STK, 2, REP, S], F32R)
        kst = sb("k_stack", [64 + STK, 2, S], F32R)
        pt = sb("probs", [P, 2, REP, S])
        rmax = sb("row_max", [P, REP, NJ])
        negm = sb("minus_max", [P, REP * NJ])
        negrow = sb("minus_max_rows", [REP * NJ, P], F32R)
        att = sb("att_T", [P, 2, S])
        ones = sem("k_ones")
        stk = [sem(f"stack_loaded{n}") for n in range(4)]
        s1_mm, reduced, neg_done = sem("max_scores_mm"), sem("maxima"), sem("minus_max_ready")
        neg_mm, neg_copied, neg_row = sem("minus_max_mm"), sem("minus_max_copied"), sem("minus_max_row")
        s2_mm, exp_done, masked, pv_mm, att_out = (sem("scores_mm"), sem("exp_done"), sem("masked"), sem("pv_mm"),
                                                   sem("att_out"))
        att_stored = [sem("att_stored0"), sem("att_stored1")]
        LOADS = 16 * 6

        def rows_of(g):
            return 64 * (g % 2), (g // 2) % 2

        with nc.Block() as block:
            @block.sync
            def _(sp):
                def load_stack(g):
                    b, kv = g // KV, g % KV
                    r, slot = rows_of(g)
                    if g >= 4:
                        sp.wait_ge(s2_mm, 11 * (g - 3))
                    qh, ql, kh, kl = (x[b].rearrange("r f h s -> (r f) h s") for x in (e.q_hi, e.q_lo, e.k_hi, e.k_lo))
                    qs = lambda x: x[:, REP * kv:REP * (kv + 1), :]
                    for part, (q, k) in enumerate(((qh, kh), (qh, kl), (ql, kh))):
                        at = slice(r + part * HD, r + (part + 1) * HD)
                        sp.dma_start(f32(qst[at, slot, :, :]), qs(q)).then_inc(stk[g % 4], 16)
                        sp.dma_start(f32(kst[at, slot, :]), k[:, kv, :]).then_inc(stk[g % 4], 16)

                sp.wait_ge(ones, 4)
                load_stack(0)
                up.sp_load(sp, 0)
                load_stack(1)
                up.sp_load(sp, 1)
                load_stack(2)
                for g in range(GROUPS):
                    if g + 2 < CH0:
                        up.sp_load(sp, g + 2)
                    if g + 3 < GROUPS:
                        load_stack(g + 3)
                    if g >= 1:
                        sp.wait_ge(att_out, g)
                        sp.dma_start(e.att_dram[(g - 1) // KV, (g - 1) % KV], att[:, (g - 1) % 2, :]).then_inc(att_stored[(g - 1) % 2], 16)
                sp.wait_ge(att_out, GROUPS)
                sp.dma_start(e.att_dram[B - 1, KV - 1], att[:, (GROUPS - 1) % 2, :]).then_inc(att_stored[(GROUPS - 1) % 2], 16)
                for s in att_stored:
                    sp.wait_ge(s, 16 * (GROUPS // 2))

            @block.gpsimd
            def _(pool):
                for g in range(4):
                    r, slot = rows_of(g)
                    pool.memset(f32(kst[r:r + STK, slot, :]), 1.0).then_inc(ones, 1)
                for k in range(2):
                    up.pool_lo(pool, 0, k)

                def mask_keys(g, j):
                    jj = NJ * g + j
                    pool.wait_ge(exp_done, 11 * g + S2_END[j])
                    diag = pt[:, jj % 2, :, 0:P]
                    pool.affine_select(out=diag, in_=diag, compare_op=ALU.is_ge, fill=0.0, base=0,
                                       pattern=[[0, REP], [1, P]], channel_multiplier=-1).then_inc(masked, 1)

                for step in range(STEPS):
                    g, s = step // G_STEPS, step % G_STEPS
                    up.pool_step(pool, step // 16, step % 16)
                    for j in range(NJ):
                        if s == S2_END[j] + 1:
                            mask_keys(g, j)

            @block.scalar
            def _(act):
                def minus_max_row(g):
                    r, slot = rows_of(g)
                    act.wait_ge(neg_mm, g + 1)
                    if g >= 1:
                        act.wait_ge(neg_row, 16 * g)
                    act.activation(negrow[:, :], e.bank[4][0:REP * NJ, 0:P], ACT.Copy).then_inc(neg_copied, 1)
                    act.wait_ge(neg_copied, g + 1)
                    if g >= 4:
                        act.wait_ge(s2_mm, 11 * (g - 3))
                    act.dma_start(f32(qst[r + STK - 1:r + STK, slot]).rearrange("o h (i s) -> o (h i) s", i=NJ),
                                  f32(negrow[:, :])).then_inc(neg_row, 16)

                def exp_piece(g, n):
                    j, h, nh = S2_PIECES[n]
                    n += 11 * g
                    jj = NJ * g + j
                    act.wait_ge(s2_mm, n + 1)
                    if jj >= 2:
                        act.wait_ge(pv_mm, jj - 1)
                    w = S - j * P
                    act.activation(pt[:, jj % 2, h:h + nh, 0:w],
                                   e.bank[5 + n % 2][:, 0:nh * w].rearrange("p (h s) -> p h s", h=nh),
                                   ACT.Exp).then_inc(exp_done, 1)

                for k in range(2):
                    up.act_hi(act, 0, k)
                minus_max_row(0)
                for step in range(STEPS):
                    g, s = step // G_STEPS, step % G_STEPS
                    up.act_step(act, step // 16, step % 16)
                    if 1 <= s <= 11:
                        exp_piece(g, s - 1)
                    if s == 13 and g + 1 < GROUPS:
                        minus_max_row(g + 1)

            @block.vector
            def _(dve):
                def maxima(g, p):
                    i, h, nh = S1_PIECES[p]
                    dve.wait_ge(s1_mm, 11 * g + p + 1)
                    if p == 0 and g >= 1:
                        dve.wait_ge(neg_done, g)
                    w = (i + 1) * P
                    dve.reduce_max(rmax[:, h:h + nh, i:i + 1],
                                   e.bank[3 + p % 2][:, 0:nh * w].rearrange("p (h t) -> p h t", h=nh),
                                   axis=AXX).then_inc(reduced, 1)

                def negate(g):
                    dve.wait_ge(reduced, 11 * (g + 1))
                    if g >= 1:
                        dve.wait_ge(neg_mm, g)
                    dve.tensor_scalar(negm[:, :], rmax[:, :, :].rearrange("p h i -> p (h i)"), -1.0, None,
                                      ALU.mult).then_inc(neg_done, 1)

                def evacuate(g):
                    dve.wait_ge(pv_mm, NJ * (g + 1))
                    if g >= 2:
                        dve.wait_ge(att_stored[g % 2], 16 * (g // 2))
                    dve.tensor_copy(att[:, g % 2, :], e.bank[7][:, :]).then_inc(att_out, 1)

                for k in range(2):
                    up.dve_combine(dve, 0, k)
                for p in range(11):
                    maxima(0, p)
                negate(0)
                for step in range(STEPS):
                    g, s = step // G_STEPS, step % G_STEPS
                    up.dve_step(dve, step // 16, step % 16)
                    if g + 1 < GROUPS:
                        if s < 11:
                            maxima(g + 1, s)
                        if s == 11:
                            negate(g + 1)
                    if s == 2 and g >= 1:
                        evacuate(g - 1)
                up.dve_hidden(dve, CH0 - 1, 1)
                evacuate(GROUPS - 1)

            @block.tensor
            def _(pe):
                pe.wait_ge(e.mask_in, 32)

                def max_scores(g, p):
                    r, slot = rows_of(g)
                    if p == 0:
                        pe.wait_ge(stk[g % 4], LOADS * (g // 4 + 1))
                    K = slice(r, r + STK - 1)
                    i, h, nh = S1_PIECES[p]
                    if p >= 2:
                        pe.wait_ge(reduced, 11 * g + p - 1)
                    elif p == 0 and g >= 1:
                        pe.wait_ge(reduced, 11 * g)
                    elif p == 1 and g >= 1:
                        pe.wait_ge(neg_copied, g)
                    w = (i + 1) * P
                    bank = e.bank[3 + p % 2]
                    for n in range(nh):
                        pe.matmul(bank[:, n * w:(n + 1) * w], qst[K, slot, h + n, i * P:(i + 1) * P], kst[K, slot, 0:w],
                                  start=(n == 0), stop=False, skip_group_check=True)
                    diag = bank[:, 0:nh * w].rearrange("p (h t) -> p h t", h=nh)[:, :, i * P:(i + 1) * P]
                    pe.matmul(diag, e.identb[:, :], e.mask[:, 0:nh, :], start=False, stop=True,
                              skip_group_check=True).then_inc(s1_mm, 1)

                def minus_max(g):
                    pe.wait_ge(neg_done, g + 1)
                    pe.transpose(e.bank[4][0:REP * NJ, 0:P], negm[:, :], e.ident[:, :]).then_inc(neg_mm, 1)

                def scores(g, n):
                    r, slot = rows_of(g)
                    j, h, nh = S2_PIECES[n]
                    if n == 0:
                        pe.wait_ge(neg_row, 16 * (g + 1))
                    K = slice(r, r + STK)
                    n += 11 * g
                    if n >= 2:
                        pe.wait_ge(exp_done, n - 1)
                    w = S - j * P
                    pe.matmul(e.bank[5 + n % 2][:, 0:nh * w], kst[K, slot, j * P:(j + 1) * P],
                              qst[K, slot, h:h + nh, j * P:], start=True, stop=True).then_inc(s2_mm, 1)

                def values(g, j):
                    jj = NJ * g + j
                    pe.wait_ge(masked, jj + 1)
                    if j == 0 and g >= 1:
                        pe.wait_ge(att_out, g)
                    b, kv = g // KV, g % KV
                    for h in range(REP):
                        last = pe.matmul(e.bank[7][32 * h:32 * (h + 1), j * P:], e.v[:, b, j, kv, :],
                                         pt[:, jj % 2, h, 0:S - j * P], start=(j == 0), stop=(j == NJ - 1),
                                         skip_group_check=True)
                    last.then_inc(pv_mm, 1)

                for k in range(2):
                    up.pe_factor(pe, 0, k)
                for p in range(11):
                    max_scores(0, p)
                minus_max(0)
                for step in range(STEPS):
                    g, s = step // G_STEPS, step % G_STEPS
                    up.pe_step(pe, step // 16, step % 16)
                    if g + 1 < GROUPS:
                        if s < 11:
                            max_scores(g + 1, s)
                        if s == 12:
                            minus_max(g + 1)
                    if 1 <= s <= 11:
                        scores(g, s - 1)
                    for j in range(NJ):
                        if s == VALUES_AT[j]:
                            values(g, j)
                        if g >= 1 and s == VALUES_AT[j] - G_STEPS:
                            values(g - 1, j)
                values(GROUPS - 1, NJ - 1)


def down0_stage(nc, e, d):
    with ExitStack() as ctx:
        sb = lambda n, s, dt=F32: ctx.enter_context(nc.sbuf_tensor(n, s, dt))
        sem = lambda n: nc.alloc_semaphore(n)
        down = Down(nc, ctx, "down0", CH0, (ALU.mult, 1.0, ALU.mult), e.bank[0:2], e.bank[2:4], d["w_down0"], e.lrd0, e.hid,
                    d["x"], e.x1_dram)
        att = sb("att_dense", [P, NC, T])
        den = sb("den", [HEADS, B, S])
        rden = sb("rden", [HEADS, B, S])
        sel = sb("head_rows", [HEADS, NC, P])
        wo_hi = sb("wo_hi", [P, NC, D], F32R)
        wo_lo = sb("wo_lo", [P, NC, D], F32R)
        a_hi = sb("att_hi", [P, NC, P], F32R)
        a_lo = sb("att_lo", [P, NC, P], F32R)
        att_in, den_in, sel_in, wo_in = sem("att_in"), sem("den_in"), sem("sel_in"), [sem("wo_in0"), sem("wo_in1")]
        wo_hi_s, wo_lo_s = sem("wo_hi_ready"), sem("wo_lo_ready")
        rden_s, bc_mm, att_n = sem("rden_ready"), sem("broadcast_mm"), sem("att_normalised")
        a_hi_s, a_lo_s, o_mm = sem("att_hi_ready"), sem("att_lo_ready"), sem("att_out_mm")
        NH = CH0

        with nc.Block() as block:
            @block.sync
            def _(sp):
                down.sp_load(sp, 0)
                down.sp_load(sp, 1)
                for b in range(B):
                    sp.dma_start(den[:, b, :], e.att_dram[b].rearrange("g (h r) s -> (g h) r s", h=REP)[:, HD, :]).then_inc(den_in, 16)
                sp.dma_start(sel[:, :, :], d["head_rows"]).then_inc(sel_in, 16)
                for b in range(B):
                    for c in range(NC):
                        for k in range(2):
                            sp.dma_start(att[64 * k:64 * (k + 1), c, b * S:(b + 1) * S],
                                         e.att_dram[b, 2 * c + k].rearrange("(h r) s -> h r s", h=REP)[:, 0:HD, :]).then_inc(att_in, 16)
                down.sp_res(sp, 0)
                down.sp_res(sp, 1)
                for o in range(2, CH0):
                    down.sp_load(sp, o)
                for c in range(NC):
                    o = CH0 + c
                    sp.wait_ge(down.eff, CH0) if c < 2 else sp.wait_ge(wo_lo_s, c - 1)
                    sp.dma_start(down.w_raw[:, o % 2, :], d["w_o"][c * P:(c + 1) * P, :]).then_inc(wo_in[c % 2], 16)
                for t in range(NT):
                    down.sp_store(sp, t)
                    if t + 2 < NT:
                        down.sp_res(sp, t + 2)
                down.sp_stored(sp)

            @block.gpsimd
            def _(pool):
                for t in range(NT):
                    for q in range(2):
                        down.pool_hlo(pool, t, q)
                    pool.wait_ge(a_hi_s, t + 1)
                    pool.tensor_tensor(a_lo[:, :, :], att[:, :, t * P:(t + 1) * P], f32(a_hi[:, :, :]), ALU.subtract).then_inc(a_lo_s, 1)

            @block.scalar
            def _(act):
                for q in range(2):
                    down.act_hhi(act, 0, q)
                for o in range(CH0):
                    down.act_whi(act, o)
                for c in range(NC):
                    act.wait_ge(wo_in[c % 2], 16 * (c // 2 + 1))
                    act.activation(wo_hi[:, c, :], down.w_raw[:, (CH0 + c) % 2, :], ACT.Copy).then_inc(wo_hi_s, 1)
                for t in range(NT):
                    act.wait_ge(att_n, 4 * (t // NJ + 1))
                    if t >= 1:
                        act.wait_ge(down.full, t)
                    act.activation(a_hi[:, :, :], att[:, :, t * P:(t + 1) * P], ACT.Copy).then_inc(a_hi_s, 1)
                    if t + 1 < NT:
                        for q in range(2):
                            down.act_hhi(act, t + 1, q)

            @block.vector
            def _(dve):
                for o in range(CH0):
                    down.dve_combine(dve, o)
                    down.dve_wlo(dve, o)
                    if o in (3, 8):
                        b = 0 if o == 3 else 1
                        dve.wait_ge(den_in, 32)
                        dve.reciprocal(rden[:, b, :], den[:, b, :]).then_inc(rden_s, 1)
                for c in range(NC):
                    dve.wait_ge(wo_hi_s, c + 1)
                    dve.tensor_tensor(wo_lo[:, c, :], down.w_raw[:, (CH0 + c) % 2, :], f32(wo_hi[:, c, :]),
                                      ALU.subtract).then_inc(wo_lo_s, 1)
                dve.wait_ge(att_in, 16 * B * NC * 2)
                for n in range(B * NC):
                    b, c = n // NC, n % NC
                    dve.wait_ge(bc_mm, n + 1)
                    dve.tensor_tensor(att[:, c, b * S:(b + 1) * S], att[:, c, b * S:(b + 1) * S], e.bank[4 + n % 2][:, :],
                                      ALU.mult).then_inc(att_n, 1)
                for t in range(NT):
                    down.dve_sum(dve, t)

            @block.tensor
            def _(pe):
                for o in range(2):
                    down.pe_factor(pe, o)
                pe.wait_ge(down.hlo, 1)
                for o in range(CH0):
                    if o == down.half[1][0]:
                        pe.wait_ge(down.hlo, 2)
                    if o + 2 < CH0:
                        down.pe_factor(pe, o + 2)
                    pe.wait_ge(down.wlo, o + 1)
                    q = o >= down.half[1][0]
                    k = o - down.half[q][0]
                    last = three_pass(pe, down.banks[0][:, :], down.h_hi[:, int(q), k, :], down.h_lo[:, int(q), k, :],
                                      down.w_hi[:, o, :], down.w_lo[:, o, :], o == 0, False)
                    if o + 1 in (down.half[0][1], CH0):
                        last.then_inc(down.mm, 1)
                pe.wait_ge(sel_in, 16)
                for n in range(B * NC):
                    b, c = n // NC, n % NC
                    if b == 0 and c == 0:
                        pe.wait_ge(rden_s, 1)
                    if b == 1 and c == 0:
                        pe.wait_ge(rden_s, 2)
                    if n >= 2:
                        pe.wait_ge(att_n, n - 1)
                    pe.matmul(e.bank[4 + n % 2][:, :], sel[:, c, :], rden[:, b, :], start=True, stop=True).then_inc(bc_mm, 1)
                pe.wait_ge(wo_lo_s, NC)
                for t in range(NT):
                    if t >= 1:
                        for q in range(2):
                            down.pe_half(pe, t, q)
                    pe.wait_ge(a_lo_s, t + 1)
                    for c in range(NC):
                        last = three_pass(pe, down.banks[t % 2][:, :], a_hi[:, c, :], a_lo[:, c, :], wo_hi[:, c, :],
                                          wo_lo[:, c, :], False, c == NC - 1)
                    last.then_inc(down.full, 1)


def sigmoid_stage(nc, e, d):
    with ExitStack() as ctx:
        sb = lambda n, s, dt=F32: ctx.enter_context(nc.sbuf_tensor(n, s, dt))
        sem = lambda n: nc.alloc_semaphore(n)
        norm = Norm(nc, ctx, "norm1", [e.bank[4], e.bank[5]], e.ident, e.xT_hi, e.xT_lo, e.x_loaded, 32)
        xk_hi = sb("xk_hi", [P, H1, T], F32R)
        xk_lo = sb("xk_lo", [P, H1, T], F32R)
        bv = sb("bv", [3 * 32, P])
        babs, bsum, bsgn, bzero, bhard, bdif, bind = (sb(f"bind_{n}", [3 * 32, P]) for n in
                                                     ("abs", "sum", "sign", "zero", "hard", "dif", "out"))
        alpha = sb("alpha", [3 * 32, 1])
        cols = sb("bind_cols", [P, 2 * 32])
        qk = sb("qk_cols", [P, H1])
        vrow = sb("v_rows", [P, D])
        lr_raw = sb("lr1_raw", [96, e.lr1.shape[1]])
        lr_in, lr_hi = sem("lr1_loaded"), sem("lr1_hi")
        bv_in, bstep, b_t, b_cols, vrow_st, vrow_in = (sem("bv_in"), sem("bind_steps"), sem("bind_transposed"),
                                                       sem("bind_cols_ready"), sem("v_row_stored"), sem("v_row_in"))
        v_lo_s, v_hi_s, v_s = sem("v1_lo_ready"), sem("v1_hi_ready"), sem("v1_ready")
        k_hi_s, k_lo_s, k_s = sem("xk_hi_ready"), sem("xk_lo_ready"), sem("xk_scaled")
        sc_mm, th_s, a_s = sem("scores1_mm"), sem("tanh1"), sem("weights1")
        xk = sb("xk_scaled", [P, 2, S])
        vt = sb("v1_scaled", [P, 2, D])
        units = [(b, h) for b in range(B) for h in range(H1)]

        with nc.Block() as block:
            @block.sync
            def _(sp):
                for t in range(2):
                    norm.load(sp, e.x1_dram, t)
                sp.dma_start(bv[:, :], d["binders"]).then_inc(bv_in, 16)
                for t in range(2, NT):
                    norm.load(sp, e.x1_dram, t)
                sp.dma_start(lr_raw[:, :], d["lr1"]).then_inc(lr_in, 16)
                sp.wait_ge(bstep, 8)
                sp.dma_start(e.vrow_dram, bind[64:64 + H1, :]).then_inc(vrow_st, 16)
                sp.wait_ge(vrow_st, 16)
                sp.dma_start(vrow[:, :], e.vrow_dram.rearrange("h p -> (h p)").partition_broadcast(P)).then_inc(vrow_in, 16)
                sp.wait_ge(vrow_in, 16)

            @block.gpsimd
            def _(pool):
                pool.wait_ge(vrow_in, 16)
                for t in range(NT):
                    pool.wait_ge(norm.normed, t + 1)
                    if t >= 2:
                        pool.wait_ge(v_lo_s, t - 1)
                    pool.tensor_tensor(vt[:, t % 2, :], norm.tile(t), vrow[:, :], ALU.mult).then_inc(v_s, 1)

            @block.scalar
            def _(act):
                for t in range(NT):
                    norm.act_std(act, t)
                    if t >= 1:
                        norm.act_hi(act, t - 1)
                norm.act_hi(act, NT - 1)
                stack_hi(act, e.lr1, lr_raw, lr_in, lr_hi)
                for n, (b, h) in enumerate(units):
                    act.wait_ge(k_s, n + 1)
                    act.activation(xk_hi[:, h, b * S:(b + 1) * S], xk[:, n % 2, :], ACT.Copy).then_inc(k_hi_s, 1)
                    act.wait_ge(v_s, n + 1)
                    act.activation(e.v_hi[:, n, :], vt[:, n % 2, :], ACT.Copy).then_inc(v_hi_s, 1)
                for n, (b, h) in enumerate(units):
                    for j in range(NJ):
                        m = NJ * n + j
                        w = S - j * P
                        act.wait_ge(sc_mm, m + 1)
                        act.activation(e.aT[:, n, BLK[j]:BLK[j] + w], e.bank[m % 4][:, 0:w], ACT.Tanh,
                                       scale=2.0 * P ** -0.5).then_inc(th_s, 1)

            @block.vector
            def _(dve):
                steps = [0]

                def step(ins):
                    ins.then_inc(bstep, 1)
                    steps[0] += 1
                    dve.wait_ge(bstep, steps[0])

                norm.dve_stats(dve, 0)
                for t in range(NT):
                    if t + 1 < NT:
                        norm.dve_stats(dve, t + 1)
                    norm.dve_norm(dve, t)
                    if t >= 1:
                        norm.dve_lo(dve, t - 1)
                    if t == 1:
                        dve.wait_ge(bv_in, 16)
                        step(dve.tensor_scalar(bsgn[:, :], bv[:, :], 0.0, 2.0, ALU.is_ge, ALU.mult))
                        step(dve.tensor_scalar(bzero[:, :], bsgn[:, :], -1.0, None, ALU.add))
                        step(dve.tensor_tensor(babs[:, :], bv[:, :], bzero[:, :], ALU.mult))
                        step(dve.reduce_sum(alpha[:, :], babs[:, :], axis=AXX))
                        step(dve.tensor_scalar(bsum[:, :], bzero[:, :], alpha[:, 0:1], None, ALU.mult))
                        step(dve.tensor_scalar(bhard[:, :], bsum[:, :], 1.0 / P, None, ALU.mult))
                        step(dve.tensor_tensor(bdif[:, :], bhard[:, :], bv[:, :], ALU.subtract))
                        step(dve.tensor_tensor(bind[:, :], bdif[:, :], bv[:, :], ALU.add))
                norm.dve_lo(dve, NT - 1)
                dve.wait_ge(b_t, 1)
                step(dve.tensor_copy(cols[:, :], e.bank[6][:, 0:2 * 32]))
                dve.tensor_tensor(qk[:, :], cols[:, 0:H1], cols[:, 32:32 + H1], ALU.mult).then_inc(b_cols, 1)
                dve.wait_ge(b_cols, 1)
                for n, (b, h) in enumerate(units):
                    tok = slice(b * S, (b + 1) * S)
                    if n >= 2:
                        dve.wait_ge(k_lo_s, n - 1)
                    dve.tensor_tensor(xk[:, n % 2, :], f32(e.xT_hi[:, h, tok]), f32(e.xT_lo[:, h, tok]), ALU.add).then_inc(bstep, 1)
                    steps[0] += 1
                    dve.wait_ge(bstep, steps[0])
                    dve.tensor_scalar(xk[:, n % 2, :], xk[:, n % 2, :], qk[:, h:h + 1], None, ALU.mult).then_inc(k_s, 1)
                    dve.wait_ge(k_hi_s, n + 1)
                    dve.tensor_tensor(xk_lo[:, h, tok], xk[:, n % 2, :], f32(xk_hi[:, h, tok]), ALU.subtract).then_inc(k_lo_s, 1)
                    dve.wait_ge(v_hi_s, n + 1)
                    dve.tensor_tensor(e.v_lo[:, n, :], vt[:, n % 2, :], f32(e.v_hi[:, n, :]), ALU.subtract).then_inc(v_lo_s, 1)
                stack_lo(dve, e.lr1, lr_raw, 2 * D, lr_hi)
                for n in range(len(units)):
                    dve.wait_ge(th_s, NJ * (n + 1))
                    dve.tensor_scalar(e.aT[:, n, :], e.aT[:, n, :], 1.0, 0.5, ALU.add, ALU.mult).then_inc(a_s, 1)

            @block.tensor
            def _(pe):
                for t in range(NT):
                    norm.pe_transpose(pe, t)
                pe.wait_ge(bstep, 8)
                pe.transpose(e.bank[6][:, 0:64], bind[0:64, :], e.ident[0:64, 0:64]).then_inc(b_t, 1)
                for n, (b, h) in enumerate(units):
                    pe.wait_ge(k_lo_s, n + 1)
                    for j in range(NJ):
                        m = NJ * n + j
                        w = S - j * P
                        if m >= 4:
                            pe.wait_ge(th_s, m - 3)
                        keys = slice(b * S + j * P, b * S + (j + 1) * P)
                        qs = slice(b * S + j * P, (b + 1) * S)
                        three_pass(pe, e.bank[m % 4][:, 0:w], xk_hi[:, h, keys], xk_lo[:, h, keys], e.xT_hi[:, h, qs],
                                   e.xT_lo[:, h, qs], True, True).then_inc(sc_mm, 1)


def up1_stage(nc, e, d):
    with ExitStack() as ctx:
        sem = lambda n: nc.alloc_semaphore(n)
        up = Up(nc, ctx, "up1", CH1, (ALU.mult, 2.0, ALU.add), e.bank[0:3], d["w_gate_up1"], e.xT_hi, e.xT_lo, e.lr1, e.hid1)
        with nc.Block() as block:
            @block.sync
            def _(sp):
                for o in range(CH1):
                    up.sp_load(sp, o)

            @block.gpsimd
            def _(pool):
                for n in range(B * H1):
                    for j in range(NJ):
                        diag = e.aT[:, n, BLK[j]:BLK[j] + P]
                        pool.affine_select(out=diag, in_=diag, compare_op=ALU.is_ge, fill=0.0, base=0,
                                           pattern=[[1, P]], channel_multiplier=-1)
                    if n == 0:
                        for k in range(2):
                            up.pool_lo(pool, 0, k)
                    if n + 1 < CH1:
                        for k in range(2):
                            up.pool_lo(pool, n + 1, k)
                for o in range(B * H1 + 1, CH1):
                    for k in range(2):
                        up.pool_lo(pool, o, k)

            @block.scalar
            def _(act):
                for k in range(2):
                    up.act_hi(act, 0, k)
                for o in range(CH1):
                    for r in range(16):
                        up.act_step(act, o, r)

            @block.vector
            def _(dve):
                for k in range(2):
                    up.dve_combine(dve, 0, k)
                for o in range(CH1):
                    for r in range(16):
                        up.dve_step(dve, o, r)
                up.dve_hidden(dve, CH1 - 1, 1)

            @block.tensor
            def _(pe):
                for k in range(2):
                    up.pe_factor(pe, 0, k)
                for o in range(CH1):
                    for r in range(16):
                        up.pe_step(pe, o, r)


def down1_stage(nc, e, d, out):
    with ExitStack() as ctx:
        sb = lambda n, s, dt=F32: ctx.enter_context(nc.sbuf_tensor(n, s, dt))
        sem = lambda n: nc.alloc_semaphore(n)
        lrd1 = sb("lrd1", [96, CH1 * P + D], F32R)
        with ExitStack() as early:
            raw = early.enter_context(nc.sbuf_tensor("lrd1_raw", [96, CH1 * P + D], F32))
            lr_in, lr_hi = sem("lrd1_loaded"), sem("lrd1_hi")
            with nc.Block() as block:
                @block.sync
                def _(sp):
                    sp.dma_start(raw[:, :], d["lrd1"]).then_inc(lr_in, 16)

                @block.scalar
                def _(act):
                    stack_hi(act, lrd1, raw, lr_in, lr_hi)

                @block.vector
                def _(dve):
                    stack_lo(dve, lrd1, raw, CH1 * P, lr_hi)

        down = Down(nc, ctx, "down1", CH1, (ALU.mult, 2.0, ALU.add), e.bank[0:2], e.bank[2:4], d["w_down1"], lrd1, e.hid1,
                    e.x1_dram, out)
        NA = 3
        a_hi = sb("a1_hi", [P, NA, S], F32R)
        a_lo = sb("a1_lo", [P, NA, S], F32R)
        a_hi_s, a_lo_s, a_mm = sem("a1_hi_ready"), sem("a1_lo_ready"), sem("a1_mm")
        NU = NT * H1
        down.full, down.full_by = a_mm, H1

        def cols_of(u):
            t, h = u // H1, u % H1
            b, i = t // NJ, t % NJ
            n = b * H1 + h
            return [e.aT[:, n, BLK[j] + (i - j) * P:BLK[j] + (i - j + 1) * P] for j in range(i + 1)]

        before = [sum((v // H1) % NJ + 1 for v in range(u)) for u in range(NU + 1)]

        with nc.Block() as block:
            @block.sync
            def _(sp):
                down.sp_load(sp, 0)
                down.sp_load(sp, 1)
                down.sp_res(sp, 0)
                down.sp_res(sp, 1)
                for o in range(2, CH1):
                    down.sp_load(sp, o)
                for t in range(NT):
                    down.sp_store(sp, t)
                    if t + 2 < NT:
                        down.sp_res(sp, t + 2)
                down.sp_stored(sp)

            @block.gpsimd
            def _(pool):
                for t in range(NT):
                    for q in range(2):
                        down.pool_hlo(pool, t, q)

            @block.scalar
            def _(act):
                for q in range(2):
                    down.act_hhi(act, 0, q)
                for o in range(CH1):
                    down.act_whi(act, o)
                for t in range(NT):
                    for u in range(t * H1, (t + 1) * H1):
                        if u >= NA:
                            act.wait_ge(a_mm, u - NA + 1)
                        for j, a in enumerate(cols_of(u)):
                            act.activation(a_hi[:, u % NA, j * P:(j + 1) * P], a, ACT.Copy).then_inc(a_hi_s, 1)
                    if t + 1 < NT:
                        for q in range(2):
                            down.act_hhi(act, t + 1, q)

            @block.vector
            def _(dve):
                for o in range(CH1):
                    down.dve_combine(dve, o)
                    down.dve_wlo(dve, o)
                for t in range(NT):
                    for u in range(t * H1, (t + 1) * H1):
                        for j, a in enumerate(cols_of(u)):
                            dve.wait_ge(a_hi_s, before[u] + j + 1)
                            dve.tensor_tensor(a_lo[:, u % NA, j * P:(j + 1) * P], a,
                                              f32(a_hi[:, u % NA, j * P:(j + 1) * P]), ALU.subtract).then_inc(a_lo_s, 1)
                    if t >= 1:
                        down.dve_sum(dve, t - 1)
                down.dve_sum(dve, NT - 1)

            @block.tensor
            def _(pe):
                for o in range(2):
                    down.pe_factor(pe, o)
                pe.wait_ge(down.hlo, 1)
                for o in range(CH1):
                    if o == down.half[1][0]:
                        pe.wait_ge(down.hlo, 2)
                    if o + 2 < CH1:
                        down.pe_factor(pe, o + 2)
                    pe.wait_ge(down.wlo, o + 1)
                    q = o >= down.half[1][0]
                    k = o - down.half[q][0]
                    last = three_pass(pe, down.banks[0][:, :], down.h_hi[:, int(q), k, :], down.h_lo[:, int(q), k, :],
                                      down.w_hi[:, o, :], down.w_lo[:, o, :], o == 0, False)
                    if o + 1 in (down.half[0][1], CH1):
                        last.then_inc(down.mm, 1)
                for t in range(NT):
                    if t >= 1:
                        for q in range(2):
                            down.pe_half(pe, t, q)
                    b, i = t // NJ, t % NJ
                    for u in range(t * H1, (t + 1) * H1):
                        h = u % H1
                        pe.wait_ge(a_lo_s, before[u + 1])
                        for j in range(i + 1):
                            last = three_pass(pe, down.banks[t % 2][:, h * P:(h + 1) * P],
                                              a_hi[:, u % NA, j * P:(j + 1) * P], a_lo[:, u % NA, j * P:(j + 1) * P],
                                              e.v_hi[:, b * NJ + j, h * P:(h + 1) * P], e.v_lo[:, b * NJ + j, h * P:(h + 1) * P],
                                              False, h == H1 - 1 and j == i)
                        last.then_inc(a_mm, 1)


def build(nc, d, out):
    e = Env()
    with ExitStack() as ctx:
        def holder(stack, side):
            return lambda n, s, dt=F32: stack.enter_context(nc.sbuf_tensor(n, s, dt, side=side))

        sb = holder(ctx, "left")
        sem = lambda n: nc.alloc_semaphore(n)
        dram = lambda n, s: nc.dram_tensor(n, s, F32, kind="Internal").ap()
        e.bank = [ctx.enter_context(nc.psum_tensor(f"bank{n}", [P, 512], F32)) for n in range(8)]
        e.ident = sb("ident", [P, P])
        e.ident_in, e.mask_in = sem("ident_in"), sem("mask_in")
        e.x_loaded = [sem(f"x_loaded{t}") for t in range(NT)]
        e.q_hi, e.q_lo = dram("q_hi", (B, 2, FR, HEADS, S)), dram("q_lo", (B, 2, FR, HEADS, S))
        e.k_hi, e.k_lo = dram("k_hi", (B, 2, FR, KV, S)), dram("k_lo", (B, 2, FR, KV, S))
        e.att_dram = dram("att", (B, KV, P, S))
        e.x1_dram = dram("x1", (T, D))
        e.vrow_dram = dram("v_row", (H1, P))
        with ExitStack() as to_down0, ExitStack() as hidden0:
            e.lrd0 = holder(to_down0, "right")("lrd0", [96, CH0 * P + D], F32R)
            with ExitStack() as to_up0:
                sb0 = holder(to_up0, "right")
                e.lr0 = sb0("lr0", [96, 2 * D + 2 * CH0 * P], F32R)
                e.mask = sb0("mask", [P, REP, P], BF16)
                e.identb = sb0("identb", [P, P], BF16)
                e.v = sb0("v_ones", [P, B, NJ, KV, 32])
                e.xT_hi = sb0("x0T_hi", [P, NC, T], F32R)
                e.xT_lo = sb0("x0T_lo", [P, NC, T], F32R)
                qkv_stage(nc, e, d)
                e.hid = holder(hidden0, "left")("hidden0", [P, CH0, T])
                attention_stage(nc, e, d)
            down0_stage(nc, e, d)
        with ExitStack() as to_down1, ExitStack() as hidden1:
            sb1 = holder(to_down1, "right")
            e.v_hi = sb1("v1_hi", [P, NT, D], F32R)
            e.v_lo = sb1("v1_lo", [P, NT, D], F32R)
            e.aT = sb1("weights1_T", [P, B * H1, CAUSAL])
            with ExitStack() as to_up1:
                sb2 = holder(to_up1, "right")
                e.lr1 = sb2("lr1", [96, 2 * D + 2 * CH1 * P], F32R)
                e.xT_hi = sb2("x1T_hi", [P, NC, T], F32R)
                e.xT_lo = sb2("x1T_lo", [P, NC, T], F32R)
                sigmoid_stage(nc, e, d)
                e.hid1 = holder(hidden1, "left")("hidden1", [P, CH1, T])
                up1_stage(nc, e, d)
            down1_stage(nc, e, d, out)


def _stacked(left, right):
    a = np.zeros((96, left.shape[1] + right.shape[1]), left.dtype)
    for g in range(3):
        a[32 * g:32 * g + left.shape[0], :left.shape[1]] = left
        a[32 * g:32 * g + left.shape[0], left.shape[1]:] = right
    return a


def _chunked(gate, up, n):
    a = np.zeros((2, n * P, D), gate.dtype)
    a[0, :gate.shape[0]] = gate
    a[1, :up.shape[0]] = up
    return np.ascontiguousarray(a.reshape(2, n, P, NC, P).transpose(1, 4, 0, 3, 2))


def _rope_tables():
    inv = (np.float32(1.0) / np.float32(10000.0) ** (np.arange(0, HD, 2, dtype=np.float32) / np.float32(HD))).astype(np.float32)
    angle = (np.arange(S, dtype=np.float32)[:, None] * inv[None, :]).astype(np.float32)
    rep = lambda a: np.ascontiguousarray(np.tile(a.astype(np.float32).T, (P // FR, 1)))
    return rep(np.cos(angle)), rep(np.sin(angle))


def _padded(a, shape):
    out = np.zeros(shape, a.dtype)
    out[tuple(slice(0, n) for n in a.shape)] = a
    return out


def kernel(**inputs):
    import ml_dtypes
    import concourse.bacc as _bacc
    from concourse.bass_utils import run_bass_kernel_spmd as _run

    i = {k: np.asarray(v) for k, v in inputs.items()}
    wq = i["L0_attn_w_qkv"]
    q = wq[:, :HEADS * HD].reshape(D, HEADS, FR, 2)
    k = wq[:, HEADS * HD:(HEADS + KV) * HD].reshape(D, KV, FR, 2)
    w_qkv = np.concatenate([q[..., 0].reshape(D, -1), q[..., 1].reshape(D, -1), k[..., 0].reshape(D, -1),
                            k[..., 1].reshape(D, -1), wq[:, (HEADS + KV) * HD:]], axis=1)
    bind = np.zeros((96, P), np.float32)
    for n, name in enumerate(("q", "k", "v")):
        bind[32 * n:32 * n + H1] = i[f"L1_attn_bv_{name}"]
    cos, sin = _rope_tables()
    after = np.arange(P)[None, :] > np.arange(P)[:, None]
    mask = np.where(after, np.float32(NEG), np.float32(0.0))
    heads = np.zeros((HEADS, NC, P), np.float32)
    for c in range(NC):
        for p in range(P):
            heads[c * (P // HD) + p // HD, c, p] = 1.0
    cat = lambda *a: np.concatenate(a, axis=1)
    n1 = CH1 * P
    arrays = {
        "x": np.ascontiguousarray(i["L0_attn_x"].reshape(T, D)),
        "w_qkv": np.ascontiguousarray(w_qkv),
        "w_o": np.ascontiguousarray(i["L0_attn_w_o"]),
        "cos": cos, "sin": sin, "head_rows": heads,
        "ident": np.eye(P, dtype=np.float32),
        "identb": np.eye(P).astype(ml_dtypes.bfloat16),
        "mask": np.ascontiguousarray(np.broadcast_to(mask[:, None, :], (P, REP, P))).astype(ml_dtypes.bfloat16),
        "w_gate_up0": _chunked(i["L0_ffn_gate_w"], i["L0_ffn_up_w"], CH0),
        "w_gate_up1": _chunked(i["L1_ffn_w1"], i["L1_ffn_w3"], CH1),
        "w_down0": np.ascontiguousarray(i["L0_ffn_down_w"].T),
        "w_down1": _padded(i["L1_ffn_w2"].T, (n1, D)),
        "lr0": _stacked(cat(i["L0_ffn_gate_sv"], i["L0_ffn_up_sv"]), cat(i["L0_ffn_gate_su"].T, i["L0_ffn_up_su"].T)),
        "lrd0": _stacked(i["L0_ffn_down_sv"], i["L0_ffn_down_su"].T),
        "lr1": _stacked(cat(i["L1_ffn_lora_A1"], i["L1_ffn_lora_A3"]),
                        cat(_padded(i["L1_ffn_lora_B1"].T, (16, n1)), _padded(i["L1_ffn_lora_B3"].T, (16, n1)))),
        "lrd1": _stacked(_padded(i["L1_ffn_lora_A2"], (16, n1)), i["L1_ffn_lora_B2"].T),
        "binders": bind,
    }
    nc = _bacc.Bacc("TRN2", target_bir_lowering=False, num_devices=1)
    d = {n: nc.dram_tensor(f"in_{n}", a.shape, mybir.dt.from_np(a.dtype), kind="ExternalInput").ap() for n, a in arrays.items()}
    out = nc.dram_tensor("out", (T, D), F32, kind="ExternalOutput").ap()
    build(nc, d, out)
    r = _run(nc, [{f"in_{n}": a for n, a in arrays.items()}], core_ids=[0])
    return r.results[0]["out"].reshape(B, S, D)
```

```python
import concourse.bass as bass
from concourse import mybir
from contextlib import ExitStack
import numpy as np

F32 = mybir.dt.float32
F32R = mybir.dt.float32r
BF16 = mybir.dt.bfloat16
ALU = mybir.AluOpType
ACT = mybir.ActivationFunctionType
AXX = mybir.AxisListType.X

P = 128
B, S, D = 2, 512, 512
T = B * S
NT = T // P
NJ = S // P
NC = D // P
HEADS, KV, HD = 32, 8, 16
REP = HEADS // KV
FR = HD // 2
GROUPS = B * KV
STK = 3 * HD + 1
H1 = 4
EPS = 1e-5
NEG = -1.0e30
QW = (HEADS + 2 * KV) * HD
CH0, CH1 = 1792 // P, 11
S1_PIECES = [(0, 0, 4), (1, 0, 2), (1, 2, 2)] + [(i, h, 1) for i in (2, 3) for h in range(4)]
S2_PIECES = [(j, h, 1) for j in (0, 1) for h in range(4)] + [(2, 0, 2), (2, 2, 2), (3, 0, 4)]
S2_END = [4, 8, 10, 11]
STEPS = 16 * 14
G_STEPS = 14
VALUES_AT = [8, 11, 13, 14]
BLK = [0, 512, 896, 1152]
CAUSAL = 1280


class Env:
    pass


def three_pass(pe, out, w_hi, w_lo, m_hi, m_lo, first, last):
    pe.matmul(out, w_hi, m_hi, start=first, stop=False, skip_group_check=True)
    pe.matmul(out, w_lo, m_hi, start=False, stop=False, skip_group_check=True)
    return pe.matmul(out, w_hi, m_lo, start=False, stop=last, skip_group_check=True)


def f32(ap):
    return ap.bitcast(F32)


class Norm:

    def __init__(self, nc, ctx, tag, banks, ident, xT_hi, xT_lo, loaded, loads):
        sb = lambda n, s, d=F32: ctx.enter_context(nc.sbuf_tensor(f"{tag}_{n}", s, d))
        sem = lambda n: nc.alloc_semaphore(f"{tag}_{n}")
        self.x = sb("x", [P, NT, D])
        self.stats = sb("stats", [P, NT, 6])
        self.mv = sb("mv", [P, NT, 2])
        self.std = sb("std", [P, NT])
        self.rstd = sb("rstd", [P, NT])
        self.banks, self.ident, self.xT_hi, self.xT_lo = banks, ident, xT_hi, xT_lo
        self.loaded, self.loads = loaded, loads
        self.raw = sem("stats_raw")
        self.stat = sem("stats_ready")
        self.stdd = sem("std_ready")
        self.rst = sem("rstd_ready")
        self.normed = sem("normed")
        self.transposed = sem("transposed")
        self.hi = sem("xT_hi_ready")
        self.lo = sem("xT_lo_ready")

    def tile(self, t):
        return self.x[:, t, :]

    def load(self, eng, x_dram, t):
        eng.dma_start(self.x[:, t, :], x_dram[t * P:(t + 1) * P, :]).then_inc(self.loaded[t], 16)

    def dve_stats(self, dve, t):
        dve.wait_ge(self.loaded[t], self.loads)
        dve.bn_stats(self.stats[:, t, :], self.x[:, t, :]).then_inc(self.raw, 1)
        dve.wait_ge(self.raw, t + 1)
        dve.bn_aggr(self.mv[:, t, :], self.stats[:, t, :]).then_inc(self.stat, 1)

    def act_std(self, act, t):
        act.wait_ge(self.stat, t + 1)
        act.activation(self.std[:, t:t + 1], self.mv[:, t, 1:2], ACT.Sqrt, bias=EPS, scale=1.0).then_inc(self.stdd, 1)

    def dve_norm(self, dve, t):
        dve.wait_ge(self.stdd, t + 1)
        dve.reciprocal(self.rstd[:, t:t + 1], self.std[:, t:t + 1]).then_inc(self.rst, 1)
        dve.wait_ge(self.rst, t + 1)
        dve.tensor_scalar(self.tile(t), self.x[:, t, :], self.mv[:, t, 0:1], self.rstd[:, t:t + 1],
                          ALU.subtract, ALU.mult).then_inc(self.normed, 1)

    def pe_transpose(self, pe, t):
        pe.wait_ge(self.normed, t + 1)
        if t >= 2:
            pe.wait_ge(self.lo, t - 1)
        for c in range(NC):
            last = pe.transpose(self.banks[t % 2][:, c * P:(c + 1) * P], self.tile(t)[:, c * P:(c + 1) * P],
                                self.ident[:, :])
        last.then_inc(self.transposed, 1)

    def act_hi(self, act, t):
        act.wait_ge(self.transposed, t + 1)
        act.activation(self.xT_hi[:, :, t * P:(t + 1) * P],
                       self.banks[t % 2][:, :].rearrange("p (c s) -> p c s", c=NC), ACT.Copy).then_inc(self.hi, 1)

    def dve_lo(self, dve, t):
        dve.wait_ge(self.hi, t + 1)
        dve.tensor_tensor(self.xT_lo[:, :, t * P:(t + 1) * P],
                          self.banks[t % 2][:, :].rearrange("p (c s) -> p c s", c=NC),
                          f32(self.xT_hi[:, :, t * P:(t + 1) * P]), ALU.subtract).then_inc(self.lo, 1)


def stack_hi(act, stack, raw, loaded, done):
    act.wait_ge(loaded, 16)
    act.activation(stack[:, :], raw[:, :], ACT.Copy).then_inc(done, 1)


def stack_lo(dve, stack, raw, left, hi_done):
    dve.wait_ge(hi_done, 1)
    dve.tensor_tensor(stack[64:96, 0:left], raw[64:96, 0:left], f32(stack[64:96, 0:left]), ALU.subtract)
    dve.tensor_tensor(stack[32:64, left:], raw[32:64, left:], f32(stack[32:64, left:]), ALU.subtract)


class Up:
    def __init__(self, nc, ctx, tag, n, combine, banks, w_dram, xT_hi, xT_lo, lr, hid):
        sb = lambda nm, s, d=F32: ctx.enter_context(nc.sbuf_tensor(f"{tag}_{nm}", s, d))
        sem = lambda nm: nc.alloc_semaphore(f"{tag}_{nm}")
        self.n, self.combine, self.banks, self.w_dram = n, combine, banks, w_dram
        self.xT_hi, self.xT_lo, self.lr, self.hid = xT_hi, xT_lo, lr, hid
        self.w_raw = sb("w_raw", [P, 2, 2, NC, P])
        self.w_eff = sb("w_eff", [P, 2, NC, P])
        self.w_hi = sb("w_hi", [P, 2, 2, NC, P], F32R)
        self.w_lo = sb("w_lo", [P, 2, 2, NC, P], F32R)
        self.th = sb("tanh", [P, 2, S])
        self.ut = sb("gated", [P, 2, S])
        self.raw = [sem("w_raw0"), sem("w_raw1")]
        self.fac = sem("factor_mm")
        self.eff = [sem("gate_eff"), sem("up_eff")]
        self.whi = sem("w_hi_ready")
        self.wlo = sem("w_lo_ready")
        self.mm = sem("gate_up_mm")
        self.tanh = sem("tanh_ready")
        self.u = sem("gated_ready")
        self.h = sem("hidden_ready")

    def sp_load(self, sp, o):
        if o >= 2:
            sp.wait_ge(self.eff[1], o - 1)
        sp.dma_start(self.w_raw[:, o % 2], self.w_dram[o]).then_inc(self.raw[o % 2], 16)

    def pe_factor(self, pe, o, k):
        unit = 6 * o + k
        if k == 0 and o >= 2:
            pe.wait_ge(self.h, 2 * (o - 2) + 1)
        if k == 1 and o >= 2:
            pe.wait_ge(self.u, 2 * (o - 2) + 2)
        if k == 1 and o == 1:
            pe.wait_ge(self.eff[0], 1)
        unit = (0 if o == 0 else 6 * (o - 1) + 2) + k
        n = self.n * P
        for c in range(NC):
            last = pe.matmul(self.banks[unit % 3][:, c * P:(c + 1) * P],
                             self.lr[0:96, k * D + c * P:k * D + (c + 1) * P],
                             self.lr[0:96, 2 * D + k * n + o * P:2 * D + k * n + (o + 1) * P],
                             start=True, stop=True)
        last.then_inc(self.fac, 1)

    def factor_bank(self, o, k):
        return self.banks[((0 if o == 0 else 6 * (o - 1) + 2) + k) % 3]

    def dve_combine(self, dve, o, k):
        dve.wait_ge(self.fac, 2 * o + k + 1)
        dve.wait_ge(self.raw[o % 2], 16 * (o // 2 + 1))
        if o >= 1:
            dve.wait_ge(self.wlo, 2 * (o - 1) + k + 1)
        op0, scale, op1 = self.combine
        dve.scalar_tensor_tensor(out=self.w_eff[:, k].rearrange("p c m -> p (c m)"), in0=self.factor_bank(o, k)[:, :],
                                 scalar=scale, in1=self.w_raw[:, o % 2, k].rearrange("p c m -> p (c m)"),
                                 op0=op0, op1=op1).then_inc(self.eff[k], 1)

    def act_hi(self, act, o, k):
        act.wait_ge(self.eff[k], o + 1)
        if o >= 2:
            act.wait_ge(self.mm, 4 * (o - 1))
        act.activation(self.w_hi[:, o % 2, k], self.w_eff[:, k], ACT.Copy).then_inc(self.whi, 1)

    def pool_lo(self, pool, o, k):
        pool.wait_ge(self.whi, 2 * o + k + 1)
        pool.tensor_tensor(self.w_lo[:, o % 2, k], self.w_eff[:, k], f32(self.w_hi[:, o % 2, k]),
                           ALU.subtract).then_inc(self.wlo, 1)

    def pe_product(self, pe, o, b, k, c):
        more = o + 1 < self.n
        if c == 0:
            if b == 0:
                pe.wait_ge(self.wlo, 2 * o + k + 1)
            if (b, k) == (0, 0):
                if o >= 1:
                    pe.wait_ge(self.h, 2 * o)
                else:
                    pe.wait_ge(self.eff[1], 1)
            if (b, k) == (0, 1) and more:
                pe.wait_ge(self.eff[0], o + 2)
            if (b, k) == (1, 0) and more:
                pe.wait_ge(self.eff[1], o + 2)
            if (b, k) == (1, 1):
                pe.wait_ge(self.u, 2 * o + 1)
        last = three_pass(pe, self.product_bank(o, b, k)[:, :], self.w_hi[:, o % 2, k, c, :], self.w_lo[:, o % 2, k, c, :],
                          self.xT_hi[:, c, b * S:(b + 1) * S], self.xT_lo[:, c, b * S:(b + 1) * S],
                          c == 0, c == NC - 1)
        if c == NC - 1:
            last.then_inc(self.mm, 1)

    def pe_step(self, pe, o, r):
        if r in (0, 1) and o + 1 < self.n:
            self.pe_factor(pe, o + 1, r)
        self.pe_product(pe, o, r // 8, r // 4 % 2, r % 4)

    def dve_step(self, dve, o, r):
        if r == 0 and o >= 1:
            self.dve_hidden(dve, o - 1, 1)
        if r in (1, 2) and o + 1 < self.n:
            self.dve_combine(dve, o + 1, r - 1)
        if r in (5, 13):
            self.dve_gate(dve, o, r // 8)
        if r == 8:
            self.dve_hidden(dve, o, 0)

    def act_step(self, act, o, r):
        if r in (2, 3) and o + 1 < self.n:
            self.act_hi(act, o + 1, r - 2)
        if r in (4, 12):
            self.act_tanh(act, o, r // 8)

    def pool_step(self, pool, o, r):
        if r in (3, 4) and o + 1 < self.n:
            self.pool_lo(pool, o + 1, r - 3)

    def product_bank(self, o, b, k):
        return self.banks[(6 * o + 4 + 2 * b + k) % 3]

    def act_tanh(self, act, o, b):
        act.wait_ge(self.mm, 4 * o + 2 * b + 1)
        if o >= 1:
            act.wait_ge(self.u, 2 * (o - 1) + b + 1)
        act.activation(self.th[:, b, :], self.product_bank(o, b, 0)[:, :], ACT.Tanh, scale=0.5).then_inc(self.tanh, 1)

    def dve_gate(self, dve, o, b):
        dve.wait_ge(self.tanh, 2 * o + b + 1)
        if o >= 1:
            dve.wait_ge(self.h, 2 * (o - 1) + b + 1)
        dve.scalar_tensor_tensor(out=self.ut[:, b, :], in0=self.th[:, b, :], scalar=1.0,
                                 in1=self.product_bank(o, b, 0)[:, :], op0=ALU.add, op1=ALU.mult).then_inc(self.u, 1)

    def dve_hidden(self, dve, o, b):
        dve.wait_ge(self.mm, 4 * o + 2 * b + 2)
        dve.wait_ge(self.u, 2 * o + b + 1)
        dve.scalar_tensor_tensor(out=self.hid[:, o, b * S:(b + 1) * S], in0=self.ut[:, b, :], scalar=0.5,
                                 in1=self.product_bank(o, b, 1)[:, :], op0=ALU.mult, op1=ALU.mult).then_inc(self.h, 1)


class Down:
    def __init__(self, nc, ctx, tag, n, combine, bank, w_dram, lr, hid):
        sb = lambda nm, s, d=F32: ctx.enter_context(nc.sbuf_tensor(f"{tag}_{nm}", s, d))
        sem = lambda nm: nc.alloc_semaphore(f"{tag}_{nm}")
        self.n, self.combine, self.bank, self.w_dram, self.lr, self.hid = n, combine, bank, w_dram, lr, hid
        self.w_raw = sb("w_raw", [P, 2, D])
        self.w_eff = sb("w_eff", [P, D])
        self.w_hi = sb("w_hi", [P, n, D], F32R)
        self.w_lo = sb("w_lo", [P, n, D], F32R)
        self.h_hi = sb("h_hi", [P, 2, S], F32R)
        self.h_lo = sb("h_lo", [P, 2, S], F32R)
        self.raw = [sem("w_raw0"), sem("w_raw1")]
        self.fac = sem("factor_mm")
        self.eff = sem("w_eff_ready")
        self.whi = sem("w_hi_ready")
        self.wlo = sem("w_lo_ready")
        self.hhi = sem("h_hi_ready")
        self.hlo = sem("h_lo_ready")
        self.mm = sem("down_mm")
        self.full = sem("tile_mm")
        self.sum = sem("sum_ready")
        self.stored = sem("stored")

    def acc(self, t):
        return self.bank[t]

    def sp_load(self, sp, o):
        if o >= 2:
            sp.wait_ge(self.eff, o - 1)
        sp.dma_start(self.w_raw[:, o % 2, :], self.w_dram[o * P:(o + 1) * P, :]).then_inc(self.raw[o % 2], 16)

    def pe_factor(self, pe, o):
        if o >= 2:
            pe.wait_ge(self.eff, o - 1)
        pe.matmul(self.bank[4 + o % 2][:, :], self.lr[0:96, o * P:(o + 1) * P],
                  self.lr[0:96, self.n * P:self.n * P + D], start=True, stop=True).then_inc(self.fac, 1)

    def dve_combine(self, dve, o):
        dve.wait_ge(self.fac, o + 1)
        dve.wait_ge(self.raw[o % 2], 16 * (o // 2 + 1))
        if o >= 1:
            dve.wait_ge(self.wlo, o)
        op0, scale, op1 = self.combine
        dve.scalar_tensor_tensor(out=self.w_eff[:, :], in0=self.bank[4 + o % 2][:, :], scalar=scale,
                                 in1=self.w_raw[:, o % 2, :], op0=op0, op1=op1).then_inc(self.eff, 1)

    def act_whi(self, act, o):
        act.wait_ge(self.eff, o + 1)
        act.activation(self.w_hi[:, o, :], self.w_eff[:, :], ACT.Copy).then_inc(self.whi, 1)

    def dve_wlo(self, dve, o):
        dve.wait_ge(self.whi, o + 1)
        dve.tensor_tensor(self.w_lo[:, o, :], self.w_eff[:, :], f32(self.w_hi[:, o, :]), ALU.subtract).then_inc(self.wlo, 1)

    def act_hhi(self, act, b, o):
        k = self.n * b + o
        if k >= 2:
            act.wait_ge(self.mm, k - 1)
        act.activation(self.h_hi[:, k % 2, :], self.hid[:, o, b * S:(b + 1) * S], ACT.Copy).then_inc(self.hhi, 1)

    def pool_hlo(self, pool, b, o):
        k = self.n * b + o
        pool.wait_ge(self.hhi, k + 1)
        pool.tensor_tensor(self.h_lo[:, k % 2, :], self.hid[:, o, b * S:(b + 1) * S], f32(self.h_hi[:, k % 2, :]),
                           ALU.subtract).then_inc(self.hlo, 1)

    def pe_chunk(self, pe, b, o, last_of_tile):
        k = self.n * b + o
        if b == 0 and o + 2 < self.n:
            self.pe_factor(pe, o + 2)
        pe.wait_ge(self.hlo, k + 1)
        if b == 0:
            pe.wait_ge(self.wlo, o + 1)
        for i in range(NJ):
            own = slice(i * P, (i + 1) * P)
            last = three_pass(pe, self.acc(NJ * b + i)[:, :], self.h_hi[:, k % 2, own], self.h_lo[:, k % 2, own],
                              self.w_hi[:, o, :], self.w_lo[:, o, :], o == 0, last_of_tile)
            if last_of_tile:
                last.then_inc(self.full, 1)
        if not last_of_tile:
            last.then_inc(self.mm, 1)


def qkv_stage(nc, e, d):
    with ExitStack() as ctx:
        sb = lambda n, s, dt=F32: ctx.enter_context(nc.sbuf_tensor(n, s, dt))
        sem = lambda n: nc.alloc_semaphore(n)
        norm = Norm(nc, ctx, "norm0", [e.bank[4], e.bank[5]], e.ident, e.xT_hi, e.xT_lo, e.x_loaded, 16)
        w_raw = sb("wqkv_raw", [P, NC, QW])
        w_hi = sb("wqkv_hi", [P, NC, QW], F32R)
        w_lo = sb("wqkv_lo", [P, NC, QW], F32R)
        cos = sb("cos", [P, S])
        sin = sb("sin", [P, S])
        prod = sb("rope_products", [P, 2, 4, S])
        rot = sb("rope_sum", [P, 2, 2, S])
        rot_hi = sb("rope_hi", [P, 2, 2, S], F32R)
        rot_lo = sb("rope_lo", [P, 2, 2, S], F32R)
        lr_raw = sb("lr0_raw", [96, e.lr0.shape[1]])
        lrd_raw = sb("lrd0_raw", [96, e.lrd0.shape[1]])
        w_loaded = [sem(f"wqkv_loaded{c}") for c in range(NC)]
        consts = sem("rope_tables_loaded")
        lr_in, lrd_in, lr_hi, lrd_hi = sem("lr0_loaded"), sem("lrd0_loaded"), sem("lr0_hi"), sem("lrd0_hi")
        w_hi_ready, w_lo_ready = sem("wqkv_hi_ready"), sem("wqkv_lo_ready")
        v_mm, v_ones = sem("v_mm"), sem("v_ones")
        pair_mm, products, summed, hi_ready, lo_ready = (sem("pair_mm"), sem("rope_prod_ready"), sem("rope_summed"),
                                                         sem("rope_hi_ready"), sem("rope_lo_ready"))
        stored = [sem("rope_stored0"), sem("rope_stored1")]
        pairs = [(b, k) for b in range(B) for k in range(3)]
        rows = [KV * FR, P, P]
        cols = [(4 * P, 4 * P + KV * FR), (0, 2 * P), (P, 3 * P)]

        with nc.Block() as block:
            @block.sync
            def _(sp):
                sp.dma_start(e.ident[:, :], d["ident"]).then_inc(e.ident_in, 16)
                for t in range(2):
                    norm.load(sp, d["x"], t)
                for c in range(NC):
                    sp.dma_start(w_raw[:, c, :], d["w_qkv"][c * P:(c + 1) * P, :]).then_inc(w_loaded[c], 16)
                for t in range(2, NT):
                    norm.load(sp, d["x"], t)
                sp.dma_start(cos[:, :], d["cos"]).then_inc(consts, 16)
                sp.dma_start(sin[:, :], d["sin"]).then_inc(consts, 16)
                sp.dma_start(lr_raw[:, :], d["lr0"]).then_inc(lr_in, 16)
                sp.dma_start(lrd_raw[:, :], d["lrd0"]).then_inc(lrd_in, 16)
                sp.dma_start(e.mask[:, :, :], d["mask"]).then_inc(e.mask_in, 16)
                sp.dma_start(e.identb[:, :], d["identb"]).then_inc(e.mask_in, 16)
                for n, (b, k) in enumerate(pairs):
                    sp.wait_ge(lo_ready, n + 1)
                    dst = [e.k_hi, e.k_lo] if k == 0 else [e.q_hi, e.q_lo]
                    h0, nh = (0, KV) if k == 0 else (16 * (k - 1), 16)
                    for part, src in enumerate((rot_hi, rot_lo)):
                        for r in range(2):
                            sp.dma_start(dst[part][b, r, :, h0:h0 + nh, :].rearrange("f h s -> h f s"),
                                         f32(src[0:rows[k], n % 2, r, :])).then_inc(stored[n % 2], 16)
                for s in stored:
                    sp.wait_ge(s, 64 * (len(pairs) // 2))

            @block.gpsimd
            def _(pool):
                for b in range(B):
                    pool.memset(e.v[:, b], 1.0).then_inc(v_ones, 1)
                for c in range(NC):
                    pool.wait_ge(w_hi_ready, c + 1)
                    pool.tensor_tensor(w_lo[:, c, :], w_raw[:, c, :], f32(w_hi[:, c, :]), ALU.subtract).then_inc(w_lo_ready, 1)
                for n, (b, k) in enumerate(pairs):
                    pool.wait_ge(products, 4 * (n + 1))
                    if n >= 2:
                        pool.wait_ge(lo_ready, n - 1)
                    R = rows[k]
                    pool.tensor_tensor(rot[0:R, n % 2, 0, :], prod[0:R, n % 2, 0, :], prod[0:R, n % 2, 1, :],
                                       ALU.subtract).then_inc(summed, 1)
                    pool.tensor_tensor(rot[0:R, n % 2, 1, :], prod[0:R, n % 2, 2, :], prod[0:R, n % 2, 3, :],
                                       ALU.add).then_inc(summed, 1)

            @block.scalar
            def _(act):
                for t in range(NT):
                    norm.act_std(act, t)
                    if t < NC:
                        act.wait_ge(w_loaded[t], 16)
                        act.activation(w_hi[:, t, :], w_raw[:, t, :], ACT.Copy).then_inc(w_hi_ready, 1)
                    if t >= 1:
                        norm.act_hi(act, t - 1)
                norm.act_hi(act, NT - 1)
                stack_hi(act, e.lr0, lr_raw, lr_in, lr_hi)
                stack_hi(act, e.lrd0, lrd_raw, lrd_in, lrd_hi)
                act.wait_ge(v_ones, B)
                for n, (b, k) in enumerate(pairs):
                    if k == 0:
                        act.wait_ge(v_mm, b + 1)
                        act.activation(e.v[:, b, :, :, 0:HD],
                                       e.bank[6 + b][:, :].rearrange("p (j g x) -> p j g x", j=NJ, g=KV), ACT.Copy)
                    act.wait_ge(summed, 2 * (n + 1))
                    if n >= 2:
                        act.wait_ge(stored[n % 2], 64 * (n // 2))
                    act.activation(rot_hi[0:rows[k], n % 2], rot[0:rows[k], n % 2], ACT.Copy).then_inc(hi_ready, 1)

            @block.vector
            def _(dve):
                norm.dve_stats(dve, 0)
                for t in range(NT):
                    if t + 1 < NT:
                        norm.dve_stats(dve, t + 1)
                    norm.dve_norm(dve, t)
                    if t >= 1:
                        norm.dve_lo(dve, t - 1)
                norm.dve_lo(dve, NT - 1)
                dve.wait_ge(consts, 32)

                def rest(n):
                    R = rows[pairs[n][1]]
                    dve.wait_ge(hi_ready, n + 1)
                    dve.tensor_tensor(rot_lo[0:R, n % 2], rot[0:R, n % 2], f32(rot_hi[0:R, n % 2]),
                                      ALU.subtract).then_inc(lo_ready, 1)

                for n, (b, k) in enumerate(pairs):
                    dve.wait_ge(pair_mm, n + 1)
                    if n >= 2:
                        dve.wait_ge(summed, 2 * (n - 1))
                    R = rows[k]
                    scale = 1.0 if k == 0 else HD ** -0.5
                    for m, (src, table) in enumerate(((0, cos), (1, sin), (0, sin), (1, cos))):
                        dve.scalar_tensor_tensor(out=prod[0:R, n % 2, m, :], in0=e.bank[2 * (n % 2) + src][0:R, :],
                                                 scalar=scale, in1=table[0:R, :], op0=ALU.mult,
                                                 op1=ALU.mult).then_inc(products, 1)
                    if n >= 1:
                        rest(n - 1)
                rest(len(pairs) - 1)
                stack_lo(dve, e.lr0, lr_raw, 2 * D, lr_hi)
                stack_lo(dve, e.lrd0, lrd_raw, CH0 * P, lrd_hi)

            @block.tensor
            def _(pe):
                pe.wait_ge(e.ident_in, 16)

                def products_of(b):
                    pe.wait_ge(norm.lo, NJ * (b + 1))
                    if b == 0:
                        pe.wait_ge(w_lo_ready, NC)
                    for n in range(3 * b, 3 * b + 3):
                        k = pairs[n][1]
                        if n >= 2:
                            pe.wait_ge(products, 4 * (n - 1))
                        for r in range(2):
                            c0 = cols[k][r]
                            for c in range(NC):
                                last = three_pass(pe, e.bank[2 * (n % 2) + r][0:rows[k], :], w_hi[:, c, c0:c0 + rows[k]],
                                                  w_lo[:, c, c0:c0 + rows[k]], e.xT_hi[:, c, b * S:(b + 1) * S],
                                                  e.xT_lo[:, c, b * S:(b + 1) * S], c == 0, c == NC - 1)
                        last.then_inc(pair_mm, 1)
                    for j in range(NJ):
                        tok = slice(b * S + j * P, b * S + (j + 1) * P)
                        for c in range(NC):
                            last = three_pass(pe, e.bank[6 + b][:, j * P:(j + 1) * P], e.xT_hi[:, c, tok], e.xT_lo[:, c, tok],
                                              w_hi[:, c, 5 * P:6 * P], w_lo[:, c, 5 * P:6 * P], c == 0, c == NC - 1)
                    last.then_inc(v_mm, 1)

                for t in range(NT):
                    norm.pe_transpose(pe, t)
                for b in range(B):
                    products_of(b)


def attention_stage(nc, e, d):
    with ExitStack() as ctx:
        sb = lambda n, s, dt=F32: ctx.enter_context(nc.sbuf_tensor(n, s, dt))
        sem = lambda n: nc.alloc_semaphore(n)
        up = Up(nc, ctx, "up0", CH0, (ALU.mult, 1.0, ALU.mult), e.bank[0:3], d["w_gate_up0"], e.xT_hi, e.xT_lo, e.lr0, e.hid)
        qst = sb("q_stack", [64 + STK, 2, REP, S], F32R)
        kst = sb("k_stack", [64 + STK, 2, S], F32R)
        pt = sb("probs", [P, 2, REP, S])
        rmax = sb("row_max", [P, REP, NJ])
        negm = sb("minus_max", [P, REP * NJ])
        negrow = sb("minus_max_rows", [REP * NJ, P], F32R)
        att = sb("att_T", [P, 2, S])
        ones = sem("k_ones")
        stk = [sem(f"stack_loaded{n}") for n in range(4)]
        s1_mm, reduced, neg_done = sem("max_scores_mm"), sem("maxima"), sem("minus_max_ready")
        neg_mm, neg_copied, neg_row = sem("minus_max_mm"), sem("minus_max_copied"), sem("minus_max_row")
        s2_mm, exp_done, masked, pv_mm, att_out = (sem("scores_mm"), sem("exp_done"), sem("masked"), sem("pv_mm"),
                                                   sem("att_out"))
        att_stored = [sem("att_stored0"), sem("att_stored1")]
        LOADS = 16 * 6

        def rows_of(g):
            return 64 * (g % 2), (g // 2) % 2

        with nc.Block() as block:
            @block.sync
            def _(sp):
                def load_stack(g):
                    b, kv = g // KV, g % KV
                    r, slot = rows_of(g)
                    if g >= 4:
                        sp.wait_ge(s2_mm, 11 * (g - 3))
                    qh, ql, kh, kl = (x[b].rearrange("r f h s -> (r f) h s") for x in (e.q_hi, e.q_lo, e.k_hi, e.k_lo))
                    qs = lambda x: x[:, REP * kv:REP * (kv + 1), :]
                    for part, (q, k) in enumerate(((qh, kh), (qh, kl), (ql, kh))):
                        at = slice(r + part * HD, r + (part + 1) * HD)
                        sp.dma_start(f32(qst[at, slot, :, :]), qs(q)).then_inc(stk[g % 4], 16)
                        sp.dma_start(f32(kst[at, slot, :]), k[:, kv, :]).then_inc(stk[g % 4], 16)

                sp.wait_ge(ones, 4)
                load_stack(0)
                up.sp_load(sp, 0)
                load_stack(1)
                up.sp_load(sp, 1)
                load_stack(2)
                for g in range(GROUPS):
                    if g + 2 < CH0:
                        up.sp_load(sp, g + 2)
                    if g + 3 < GROUPS:
                        load_stack(g + 3)
                    if g >= 1:
                        sp.wait_ge(att_out, g)
                        sp.dma_start(e.att_dram[(g - 1) // KV, (g - 1) % KV], att[:, (g - 1) % 2, :]).then_inc(att_stored[(g - 1) % 2], 16)
                sp.wait_ge(att_out, GROUPS)
                sp.dma_start(e.att_dram[B - 1, KV - 1], att[:, (GROUPS - 1) % 2, :]).then_inc(att_stored[(GROUPS - 1) % 2], 16)
                for s in att_stored:
                    sp.wait_ge(s, 16 * (GROUPS // 2))

            @block.gpsimd
            def _(pool):
                for g in range(4):
                    r, slot = rows_of(g)
                    pool.memset(f32(kst[r:r + STK, slot, :]), 1.0).then_inc(ones, 1)
                for k in range(2):
                    up.pool_lo(pool, 0, k)

                def mask_keys(g, j):
                    jj = NJ * g + j
                    pool.wait_ge(exp_done, 11 * g + S2_END[j])
                    diag = pt[:, jj % 2, :, 0:P]
                    pool.affine_select(out=diag, in_=diag, compare_op=ALU.is_ge, fill=0.0, base=0,
                                       pattern=[[0, REP], [1, P]], channel_multiplier=-1).then_inc(masked, 1)

                for step in range(STEPS):
                    g, s = step // G_STEPS, step % G_STEPS
                    up.pool_step(pool, step // 16, step % 16)
                    for j in range(NJ):
                        if s == S2_END[j] + 1:
                            mask_keys(g, j)

            @block.scalar
            def _(act):
                def minus_max_row(g):
                    r, slot = rows_of(g)
                    act.wait_ge(neg_mm, g + 1)
                    if g >= 1:
                        act.wait_ge(neg_row, 16 * g)
                    act.activation(negrow[:, :], e.bank[4][0:REP * NJ, 0:P], ACT.Copy).then_inc(neg_copied, 1)
                    act.wait_ge(neg_copied, g + 1)
                    if g >= 4:
                        act.wait_ge(s2_mm, 11 * (g - 3))
                    act.dma_start(f32(qst[r + STK - 1:r + STK, slot]).rearrange("o h (i s) -> o (h i) s", i=NJ),
                                  f32(negrow[:, :])).then_inc(neg_row, 16)

                def exp_piece(g, n):
                    j, h, nh = S2_PIECES[n]
                    n += 11 * g
                    jj = NJ * g + j
                    act.wait_ge(s2_mm, n + 1)
                    if jj >= 2:
                        act.wait_ge(pv_mm, jj - 1)
                    w = S - j * P
                    act.activation(pt[:, jj % 2, h:h + nh, 0:w],
                                   e.bank[5 + n % 2][:, 0:nh * w].rearrange("p (h s) -> p h s", h=nh),
                                   ACT.Exp).then_inc(exp_done, 1)

                for k in range(2):
                    up.act_hi(act, 0, k)
                minus_max_row(0)
                for step in range(STEPS):
                    g, s = step // G_STEPS, step % G_STEPS
                    up.act_step(act, step // 16, step % 16)
                    if 1 <= s <= 11:
                        exp_piece(g, s - 1)
                    if s == 13 and g + 1 < GROUPS:
                        minus_max_row(g + 1)

            @block.vector
            def _(dve):
                def maxima(g, p):
                    i, h, nh = S1_PIECES[p]
                    dve.wait_ge(s1_mm, 11 * g + p + 1)
                    if p == 0 and g >= 1:
                        dve.wait_ge(neg_done, g)
                    w = (i + 1) * P
                    dve.reduce_max(rmax[:, h:h + nh, i:i + 1],
                                   e.bank[3 + p % 2][:, 0:nh * w].rearrange("p (h t) -> p h t", h=nh),
                                   axis=AXX).then_inc(reduced, 1)

                def negate(g):
                    dve.wait_ge(reduced, 11 * (g + 1))
                    if g >= 1:
                        dve.wait_ge(neg_mm, g)
                    dve.tensor_scalar(negm[:, :], rmax[:, :, :].rearrange("p h i -> p (h i)"), -1.0, None,
                                      ALU.mult).then_inc(neg_done, 1)

                def evacuate(g):
                    dve.wait_ge(pv_mm, NJ * (g + 1))
                    if g >= 2:
                        dve.wait_ge(att_stored[g % 2], 16 * (g // 2))
                    dve.tensor_copy(att[:, g % 2, :], e.bank[7][:, :]).then_inc(att_out, 1)

                for k in range(2):
                    up.dve_combine(dve, 0, k)
                for p in range(11):
                    maxima(0, p)
                negate(0)
                for step in range(STEPS):
                    g, s = step // G_STEPS, step % G_STEPS
                    up.dve_step(dve, step // 16, step % 16)
                    if g + 1 < GROUPS:
                        if s < 11:
                            maxima(g + 1, s)
                        if s == 11:
                            negate(g + 1)
                    if s == 2 and g >= 1:
                        evacuate(g - 1)
                up.dve_hidden(dve, CH0 - 1, 1)
                evacuate(GROUPS - 1)

            @block.tensor
            def _(pe):
                pe.wait_ge(e.mask_in, 32)

                def max_scores(g, p):
                    r, slot = rows_of(g)
                    if p == 0:
                        pe.wait_ge(stk[g % 4], LOADS * (g // 4 + 1))
                    K = slice(r, r + STK - 1)
                    i, h, nh = S1_PIECES[p]
                    if p >= 2:
                        pe.wait_ge(reduced, 11 * g + p - 1)
                    elif p == 0 and g >= 1:
                        pe.wait_ge(reduced, 11 * g)
                    elif p == 1 and g >= 1:
                        pe.wait_ge(neg_copied, g)
                    w = (i + 1) * P
                    bank = e.bank[3 + p % 2]
                    for n in range(nh):
                        pe.matmul(bank[:, n * w:(n + 1) * w], qst[K, slot, h + n, i * P:(i + 1) * P], kst[K, slot, 0:w],
                                  start=(n == 0), stop=False, skip_group_check=True)
                    diag = bank[:, 0:nh * w].rearrange("p (h t) -> p h t", h=nh)[:, :, i * P:(i + 1) * P]
                    pe.matmul(diag, e.identb[:, :], e.mask[:, 0:nh, :], start=False, stop=True,
                              skip_group_check=True).then_inc(s1_mm, 1)

                def minus_max(g):
                    pe.wait_ge(neg_done, g + 1)
                    pe.transpose(e.bank[4][0:REP * NJ, 0:P], negm[:, :], e.ident[:, :]).then_inc(neg_mm, 1)

                def scores(g, n):
                    r, slot = rows_of(g)
                    j, h, nh = S2_PIECES[n]
                    if n == 0:
                        pe.wait_ge(neg_row, 16 * (g + 1))
                    K = slice(r, r + STK)
                    n += 11 * g
                    if n >= 2:
                        pe.wait_ge(exp_done, n - 1)
                    w = S - j * P
                    pe.matmul(e.bank[5 + n % 2][:, 0:nh * w], kst[K, slot, j * P:(j + 1) * P],
                              qst[K, slot, h:h + nh, j * P:], start=True, stop=True).then_inc(s2_mm, 1)

                def values(g, j):
                    jj = NJ * g + j
                    pe.wait_ge(masked, jj + 1)
                    if j == 0 and g >= 1:
                        pe.wait_ge(att_out, g)
                    b, kv = g // KV, g % KV
                    for h in range(REP):
                        last = pe.matmul(e.bank[7][32 * h:32 * (h + 1), j * P:], e.v[:, b, j, kv, :],
                                         pt[:, jj % 2, h, 0:S - j * P], start=(j == 0), stop=(j == NJ - 1),
                                         skip_group_check=True)
                    last.then_inc(pv_mm, 1)

                for k in range(2):
                    up.pe_factor(pe, 0, k)
                for p in range(11):
                    max_scores(0, p)
                minus_max(0)
                for step in range(STEPS):
                    g, s = step // G_STEPS, step % G_STEPS
                    up.pe_step(pe, step // 16, step % 16)
                    if g + 1 < GROUPS:
                        if s < 11:
                            max_scores(g + 1, s)
                        if s == 12:
                            minus_max(g + 1)
                    if 1 <= s <= 11:
                        scores(g, s - 1)
                    for j in range(NJ):
                        if s == VALUES_AT[j]:
                            values(g, j)
                        if g >= 1 and s == VALUES_AT[j] - G_STEPS:
                            values(g - 1, j)
                values(GROUPS - 1, NJ - 1)


def down0_stage(nc, e, d):
    with ExitStack() as ctx:
        sb = lambda n, s, dt=F32: ctx.enter_context(nc.sbuf_tensor(n, s, dt))
        sem = lambda n: nc.alloc_semaphore(n)
        down = Down(nc, ctx, "down0", CH0, (ALU.mult, 1.0, ALU.mult), e.bank, d["w_down0"], e.lrd0, e.hid)
        res = sb("res", [P, NT, D])
        att = sb("att_dense", [P, NC, T])
        den = sb("den", [HEADS, B, S])
        rden = sb("rden", [HEADS, B, S])
        sel = sb("head_rows", [HEADS, NC, P])
        wo_hi = sb("wo_hi", [P, NC, D], F32R)
        wo_lo = sb("wo_lo", [P, NC, D], F32R)
        a_hi = sb("att_hi", [P, 2, S], F32R)
        a_lo = sb("att_lo", [P, 2, S], F32R)
        att_in, den_in, sel_in, wo_in = sem("att_in"), sem("den_in"), sem("sel_in"), [sem("wo_in0"), sem("wo_in1")]
        wo_hi_s, wo_lo_s, res_in = sem("wo_hi_ready"), sem("wo_lo_ready"), sem("res_in")
        rden_s, bc_mm, att_n = sem("rden_ready"), sem("broadcast_mm"), sem("att_normalised")
        a_hi_s, a_lo_s, o_mm = sem("att_hi_ready"), sem("att_lo_ready"), sem("att_out_mm")
        UNITS = [(b, c) for b in range(B) for c in range(NC)]

        with nc.Block() as block:
            @block.sync
            def _(sp):
                down.sp_load(sp, 0)
                down.sp_load(sp, 1)
                for b in range(B):
                    sp.dma_start(den[:, b, :], e.att_dram[b].rearrange("g (h r) s -> (g h) r s", h=REP)[:, HD, :]).then_inc(den_in, 16)
                sp.dma_start(sel[:, :, :], d["head_rows"]).then_inc(sel_in, 16)
                for b, c in UNITS:
                    for k in range(2):
                        sp.dma_start(att[64 * k:64 * (k + 1), c, b * S:(b + 1) * S],
                                     e.att_dram[b, 2 * c + k].rearrange("(h r) s -> h r s", h=REP)[:, 0:HD, :]).then_inc(att_in, 16)
                for o in range(2, CH0):
                    down.sp_load(sp, o)
                    if o == 4:
                        sp.dma_start(res[:, :, :], d["x"].rearrange("(t p) n -> p t n", p=P)).then_inc(res_in, 16)
                for c in range(NC):
                    o = CH0 + c
                    if c < 2:
                        sp.wait_ge(down.eff, o - 1)
                    else:
                        sp.wait_ge(wo_lo_s, c - 1)
                    sp.dma_start(down.w_raw[:, o % 2, :], d["w_o"][c * P:(c + 1) * P, :]).then_inc(wo_in[c % 2], 16)
                for t in range(NT):
                    sp.wait_ge(down.sum, t + 1)
                    sp.dma_start(e.x1_dram[t * P:(t + 1) * P, :], res[:, t, :]).then_inc(down.stored, 16)
                sp.wait_ge(down.stored, 16 * NT)

            @block.gpsimd
            def _(pool):
                for b in range(B):
                    for o in range(CH0):
                        down.pool_hlo(pool, b, o)
                    for c in range(NC):
                        n = NC * b + c
                        pool.wait_ge(a_hi_s, n + 1)
                        pool.tensor_tensor(a_lo[:, n % 2, :], att[:, c, b * S:(b + 1) * S], f32(a_hi[:, n % 2, :]),
                                           ALU.subtract).then_inc(a_lo_s, 1)

            @block.scalar
            def _(act):
                for b in range(B):
                    for o in range(CH0):
                        down.act_hhi(act, b, o)
                        if b == 0:
                            down.act_whi(act, o)
                    for c in range(NC):
                        if b == 0:
                            act.wait_ge(wo_in[c % 2], 16 * (c // 2 + 1))
                            act.activation(wo_hi[:, c, :], down.w_raw[:, (CH0 + c) % 2, :], ACT.Copy).then_inc(wo_hi_s, 1)
                        n = NC * b + c
                        act.wait_ge(att_n, n + 1)
                        if n >= 2:
                            pb, pc = UNITS[n - 2]
                            if pc < NC - 1:
                                act.wait_ge(o_mm, (NC - 1) * pb + pc + 1)
                            else:
                                act.wait_ge(down.full, NJ * (pb + 1))
                        act.activation(a_hi[:, n % 2, :], att[:, c, b * S:(b + 1) * S], ACT.Copy).then_inc(a_hi_s, 1)

            @block.vector
            def _(dve):
                def normalise(n):
                    b, c = UNITS[n]
                    dve.wait_ge(bc_mm, n + 1)
                    dve.tensor_tensor(att[:, c, b * S:(b + 1) * S], att[:, c, b * S:(b + 1) * S], e.bank[6 + n % 2][:, :],
                                      ALU.mult).then_inc(att_n, 1)

                for o in range(CH0):
                    down.dve_combine(dve, o)
                    down.dve_wlo(dve, o)
                    if o in (2, 5):
                        dve.wait_ge(den_in, 32)
                        b = o // 4
                        dve.reciprocal(rden[:, b, :], den[:, b, :]).then_inc(rden_s, 1)
                    if o == 6:
                        dve.wait_ge(att_in, 16 * len(UNITS) * 2)
                    if o >= 6:
                        normalise(o - 6)
                for c in range(NC):
                    dve.wait_ge(wo_hi_s, c + 1)
                    dve.tensor_tensor(wo_lo[:, c, :], down.w_raw[:, (CH0 + c) % 2, :], f32(wo_hi[:, c, :]),
                                      ALU.subtract).then_inc(wo_lo_s, 1)
                dve.wait_ge(res_in, 16)
                for t in range(NT):
                    dve.wait_ge(down.full, t + 1)
                    dve.tensor_tensor(res[:, t, :], res[:, t, :], down.acc(t)[:, :], ALU.add).then_inc(down.sum, 1)

            @block.tensor
            def _(pe):
                for o in range(2):
                    down.pe_factor(pe, o)
                for b in range(B):
                    for o in range(CH0):
                        down.pe_chunk(pe, b, o, False)
                        if b == 0 and o >= 5 and o - 5 < len(UNITS):
                            n = o - 5
                            ub, c = UNITS[n]
                            if n == 0:
                                pe.wait_ge(sel_in, 16)
                            if c == 0:
                                pe.wait_ge(rden_s, ub + 1)
                            if n >= 2:
                                pe.wait_ge(att_n, n - 1)
                            pe.matmul(e.bank[6 + n % 2][:, :], sel[:, c, :], rden[:, ub, :], start=True, stop=True).then_inc(bc_mm, 1)
                    for c in range(NC):
                        n = NC * b + c
                        pe.wait_ge(a_lo_s, n + 1)
                        if b == 0:
                            pe.wait_ge(wo_lo_s, c + 1)
                        for i in range(NJ):
                            own = slice(i * P, (i + 1) * P)
                            last = three_pass(pe, down.acc(NJ * b + i)[:, :], a_hi[:, n % 2, own], a_lo[:, n % 2, own],
                                              wo_hi[:, c, :], wo_lo[:, c, :], False, c == NC - 1)
                            if c == NC - 1:
                                last.then_inc(down.full, 1)
                        if c < NC - 1:
                            last.then_inc(o_mm, 1)


def sigmoid_stage(nc, e, d):
    with ExitStack() as ctx:
        sb = lambda n, s, dt=F32: ctx.enter_context(nc.sbuf_tensor(n, s, dt))
        sem = lambda n: nc.alloc_semaphore(n)
        norm = Norm(nc, ctx, "norm1", [e.bank[4], e.bank[5]], e.ident, e.xT_hi, e.xT_lo, e.x_loaded, 32)
        xk_hi = sb("xk_hi", [P, H1, T], F32R)
        xk_lo = sb("xk_lo", [P, H1, T], F32R)
        bv = sb("bv", [3 * 32, P])
        babs, bsum, bsgn, bzero, bhard, bdif, bind = (sb(f"bind_{n}", [3 * 32, P]) for n in
                                                     ("abs", "sum", "sign", "zero", "hard", "dif", "out"))
        alpha = sb("alpha", [3 * 32, 1])
        cols = sb("bind_cols", [P, 2 * 32])
        qk = sb("qk_cols", [P, H1])
        vrow = sb("v_rows", [P, D])
        lr_raw = sb("lr1_raw", [96, e.lr1.shape[1]])
        lr_in, lr_hi = sem("lr1_loaded"), sem("lr1_hi")
        bv_in, bstep, b_t, b_cols, vrow_st, vrow_in = (sem("bv_in"), sem("bind_steps"), sem("bind_transposed"),
                                                       sem("bind_cols_ready"), sem("v_row_stored"), sem("v_row_in"))
        v_lo_s, v_hi_s, v_s = sem("v1_lo_ready"), sem("v1_hi_ready"), sem("v1_ready")
        k_hi_s, k_lo_s, k_s = sem("xk_hi_ready"), sem("xk_lo_ready"), sem("xk_scaled")
        sc_mm, th_s, a_s = sem("scores1_mm"), sem("tanh1"), sem("weights1")
        xk = sb("xk_scaled", [P, 2, S])
        vt = sb("v1_scaled", [P, 2, D])
        units = [(b, h) for b in range(B) for h in range(H1)]

        with nc.Block() as block:
            @block.sync
            def _(sp):
                for t in range(2):
                    norm.load(sp, e.x1_dram, t)
                sp.dma_start(bv[:, :], d["binders"]).then_inc(bv_in, 16)
                for t in range(2, NT):
                    norm.load(sp, e.x1_dram, t)
                sp.dma_start(lr_raw[:, :], d["lr1"]).then_inc(lr_in, 16)
                sp.wait_ge(bstep, 8)
                sp.dma_start(e.vrow_dram, bind[64:64 + H1, :]).then_inc(vrow_st, 16)
                sp.wait_ge(vrow_st, 16)
                sp.dma_start(vrow[:, :], e.vrow_dram.rearrange("h p -> (h p)").partition_broadcast(P)).then_inc(vrow_in, 16)
                sp.wait_ge(vrow_in, 16)

            @block.gpsimd
            def _(pool):
                pool.wait_ge(vrow_in, 16)
                for t in range(NT):
                    pool.wait_ge(norm.normed, t + 1)
                    if t >= 2:
                        pool.wait_ge(v_lo_s, t - 1)
                    pool.tensor_tensor(vt[:, t % 2, :], norm.tile(t), vrow[:, :], ALU.mult).then_inc(v_s, 1)

            @block.scalar
            def _(act):
                for t in range(NT):
                    norm.act_std(act, t)
                    if t >= 1:
                        norm.act_hi(act, t - 1)
                norm.act_hi(act, NT - 1)
                stack_hi(act, e.lr1, lr_raw, lr_in, lr_hi)
                for n, (b, h) in enumerate(units):
                    act.wait_ge(k_s, n + 1)
                    act.activation(xk_hi[:, h, b * S:(b + 1) * S], xk[:, n % 2, :], ACT.Copy).then_inc(k_hi_s, 1)
                    act.wait_ge(v_s, n + 1)
                    act.activation(e.v_hi[:, n, :], vt[:, n % 2, :], ACT.Copy).then_inc(v_hi_s, 1)
                for n, (b, h) in enumerate(units):
                    for j in range(NJ):
                        m = NJ * n + j
                        w = S - j * P
                        act.wait_ge(sc_mm, m + 1)
                        act.activation(e.aT[:, n, BLK[j]:BLK[j] + w], e.bank[m % 4][:, 0:w], ACT.Tanh,
                                       scale=2.0 * P ** -0.5).then_inc(th_s, 1)

            @block.vector
            def _(dve):
                steps = [0]

                def step(ins):
                    ins.then_inc(bstep, 1)
                    steps[0] += 1
                    dve.wait_ge(bstep, steps[0])

                norm.dve_stats(dve, 0)
                for t in range(NT):
                    if t + 1 < NT:
                        norm.dve_stats(dve, t + 1)
                    norm.dve_norm(dve, t)
                    if t >= 1:
                        norm.dve_lo(dve, t - 1)
                    if t == 1:
                        dve.wait_ge(bv_in, 16)
                        step(dve.tensor_scalar(bsgn[:, :], bv[:, :], 0.0, 2.0, ALU.is_ge, ALU.mult))
                        step(dve.tensor_scalar(bzero[:, :], bsgn[:, :], -1.0, None, ALU.add))
                        step(dve.tensor_tensor(babs[:, :], bv[:, :], bzero[:, :], ALU.mult))
                        step(dve.reduce_sum(alpha[:, :], babs[:, :], axis=AXX))
                        step(dve.tensor_scalar(bsum[:, :], bzero[:, :], alpha[:, 0:1], None, ALU.mult))
                        step(dve.tensor_scalar(bhard[:, :], bsum[:, :], 1.0 / P, None, ALU.mult))
                        step(dve.tensor_tensor(bdif[:, :], bhard[:, :], bv[:, :], ALU.subtract))
                        step(dve.tensor_tensor(bind[:, :], bdif[:, :], bv[:, :], ALU.add))
                norm.dve_lo(dve, NT - 1)
                dve.wait_ge(b_t, 1)
                step(dve.tensor_copy(cols[:, :], e.bank[6][:, 0:2 * 32]))
                dve.tensor_tensor(qk[:, :], cols[:, 0:H1], cols[:, 32:32 + H1], ALU.mult).then_inc(b_cols, 1)
                dve.wait_ge(b_cols, 1)
                for n, (b, h) in enumerate(units):
                    tok = slice(b * S, (b + 1) * S)
                    if n >= 2:
                        dve.wait_ge(k_lo_s, n - 1)
                    dve.tensor_tensor(xk[:, n % 2, :], f32(e.xT_hi[:, h, tok]), f32(e.xT_lo[:, h, tok]), ALU.add).then_inc(bstep, 1)
                    steps[0] += 1
                    dve.wait_ge(bstep, steps[0])
                    dve.tensor_scalar(xk[:, n % 2, :], xk[:, n % 2, :], qk[:, h:h + 1], None, ALU.mult).then_inc(k_s, 1)
                    dve.wait_ge(k_hi_s, n + 1)
                    dve.tensor_tensor(xk_lo[:, h, tok], xk[:, n % 2, :], f32(xk_hi[:, h, tok]), ALU.subtract).then_inc(k_lo_s, 1)
                    dve.wait_ge(v_hi_s, n + 1)
                    dve.tensor_tensor(e.v_lo[:, n, :], vt[:, n % 2, :], f32(e.v_hi[:, n, :]), ALU.subtract).then_inc(v_lo_s, 1)
                stack_lo(dve, e.lr1, lr_raw, 2 * D, lr_hi)
                for n in range(len(units)):
                    dve.wait_ge(th_s, NJ * (n + 1))
                    dve.tensor_scalar(e.aT[:, n, :], e.aT[:, n, :], 1.0, 0.5, ALU.add, ALU.mult).then_inc(a_s, 1)

            @block.tensor
            def _(pe):
                for t in range(NT):
                    norm.pe_transpose(pe, t)
                pe.wait_ge(bstep, 8)
                pe.transpose(e.bank[6][:, 0:64], bind[0:64, :], e.ident[0:64, 0:64]).then_inc(b_t, 1)
                for n, (b, h) in enumerate(units):
                    pe.wait_ge(k_lo_s, n + 1)
                    for j in range(NJ):
                        m = NJ * n + j
                        w = S - j * P
                        if m >= 4:
                            pe.wait_ge(th_s, m - 3)
                        keys = slice(b * S + j * P, b * S + (j + 1) * P)
                        qs = slice(b * S + j * P, (b + 1) * S)
                        three_pass(pe, e.bank[m % 4][:, 0:w], xk_hi[:, h, keys], xk_lo[:, h, keys], e.xT_hi[:, h, qs],
                                   e.xT_lo[:, h, qs], True, True).then_inc(sc_mm, 1)


def up1_stage(nc, e, d):
    with ExitStack() as ctx:
        sem = lambda n: nc.alloc_semaphore(n)
        up = Up(nc, ctx, "up1", CH1, (ALU.mult, 2.0, ALU.add), e.bank[0:3], d["w_gate_up1"], e.xT_hi, e.xT_lo, e.lr1, e.hid1)
        with nc.Block() as block:
            @block.sync
            def _(sp):
                for o in range(CH1):
                    up.sp_load(sp, o)

            @block.gpsimd
            def _(pool):
                for n in range(B * H1):
                    for j in range(NJ):
                        diag = e.aT[:, n, BLK[j]:BLK[j] + P]
                        pool.affine_select(out=diag, in_=diag, compare_op=ALU.is_ge, fill=0.0, base=0,
                                           pattern=[[1, P]], channel_multiplier=-1)
                    if n == 0:
                        for k in range(2):
                            up.pool_lo(pool, 0, k)
                    if n + 1 < CH1:
                        for k in range(2):
                            up.pool_lo(pool, n + 1, k)
                for o in range(B * H1 + 1, CH1):
                    for k in range(2):
                        up.pool_lo(pool, o, k)

            @block.scalar
            def _(act):
                for k in range(2):
                    up.act_hi(act, 0, k)
                for o in range(CH1):
                    for r in range(16):
                        up.act_step(act, o, r)

            @block.vector
            def _(dve):
                for k in range(2):
                    up.dve_combine(dve, 0, k)
                for o in range(CH1):
                    for r in range(16):
                        up.dve_step(dve, o, r)
                up.dve_hidden(dve, CH1 - 1, 1)

            @block.tensor
            def _(pe):
                for k in range(2):
                    up.pe_factor(pe, 0, k)
                for o in range(CH1):
                    for r in range(16):
                        up.pe_step(pe, o, r)


def down1_stage(nc, e, d, out):
    with ExitStack() as ctx:
        sb = lambda n, s, dt=F32: ctx.enter_context(nc.sbuf_tensor(n, s, dt))
        sem = lambda n: nc.alloc_semaphore(n)
        lrd1 = sb("lrd1", [96, CH1 * P + D], F32R)
        with ExitStack() as early:
            raw = early.enter_context(nc.sbuf_tensor("lrd1_raw", [96, CH1 * P + D], F32))
            lr_in, lr_hi = sem("lrd1_loaded"), sem("lrd1_hi")
            with nc.Block() as block:
                @block.sync
                def _(sp):
                    sp.dma_start(raw[:, :], d["lrd1"]).then_inc(lr_in, 16)

                @block.scalar
                def _(act):
                    stack_hi(act, lrd1, raw, lr_in, lr_hi)

                @block.vector
                def _(dve):
                    stack_lo(dve, lrd1, raw, CH1 * P, lr_hi)

        down = Down(nc, ctx, "down1", CH1, (ALU.mult, 2.0, ALU.add), e.bank, d["w_down1"], lrd1, e.hid1)
        res = sb("res1", [P, 2, D])
        res_in, stored = [sem("res1_in0"), sem("res1_in1")], [sem("stored0"), sem("stored1")]
        NA = 3
        a_hi = sb("a1_hi", [P, NA, S], F32R)
        a_lo = sb("a1_lo", [P, NA, S], F32R)
        a_hi_s, a_lo_s, a_mm = sem("a1_hi_ready"), sem("a1_lo_ready"), sem("a1_mm")
        NU = NT * H1

        def cols_of(u):
            t, h = u // H1, u % H1
            b, i = t // NJ, t % NJ
            n = b * H1 + h
            return [e.aT[:, n, BLK[j] + (i - j) * P:BLK[j] + (i - j + 1) * P] for j in range(i + 1)]

        before = [sum((v // H1) % NJ + 1 for v in range(u)) for u in range(NU + 1)]

        with nc.Block() as block:
            @block.sync
            def _(sp):
                def load(t):
                    if t >= 2:
                        sp.wait_ge(stored[t % 2], 16 * (t // 2))
                    sp.dma_start(res[:, t % 2, :], e.x1_dram[t * P:(t + 1) * P, :]).then_inc(res_in[t % 2], 16)

                down.sp_load(sp, 0)
                down.sp_load(sp, 1)
                load(0)
                load(1)
                for o in range(2, CH1):
                    down.sp_load(sp, o)
                for t in range(NT):
                    sp.wait_ge(down.sum, t + 1)
                    sp.dma_start(out[t * P:(t + 1) * P, :], res[:, t % 2, :]).then_inc(stored[t % 2], 16)
                    if t + 2 < NT:
                        load(t + 2)
                for k in range(2):
                    sp.wait_ge(stored[k], 16 * NT // 2)

            @block.gpsimd
            def _(pool):
                for b in range(B):
                    for o in range(CH1):
                        down.pool_hlo(pool, b, o)

            @block.scalar
            def _(act):
                for b in range(B):
                    for o in range(CH1):
                        down.act_hhi(act, b, o)
                        if b == 0:
                            down.act_whi(act, o)
                    for u in range(b * NU // B, (b + 1) * NU // B):
                        if u >= NA:
                            act.wait_ge(a_mm, u - NA + 1)
                        for j, a in enumerate(cols_of(u)):
                            act.activation(a_hi[:, u % NA, j * P:(j + 1) * P], a, ACT.Copy).then_inc(a_hi_s, 1)

            @block.vector
            def _(dve):
                for o in range(CH1):
                    down.dve_combine(dve, o)
                    down.dve_wlo(dve, o)

                def total(t):
                    dve.wait_ge(a_mm, H1 * (t + 1))
                    dve.wait_ge(res_in[t % 2], 16 * (t // 2 + 1))
                    dve.tensor_tensor(res[:, t % 2, :], res[:, t % 2, :], down.acc(t)[:, :], ALU.add).then_inc(down.sum, 1)

                for t in range(NT):
                    for u in range(t * H1, (t + 1) * H1):
                        for j, a in enumerate(cols_of(u)):
                            dve.wait_ge(a_hi_s, before[u] + j + 1)
                            dve.tensor_tensor(a_lo[:, u % NA, j * P:(j + 1) * P], a,
                                              f32(a_hi[:, u % NA, j * P:(j + 1) * P]), ALU.subtract).then_inc(a_lo_s, 1)
                    if t >= 1:
                        total(t - 1)
                total(NT - 1)

            @block.tensor
            def _(pe):
                for o in range(2):
                    down.pe_factor(pe, o)
                for b in range(B):
                    for o in range(CH1):
                        down.pe_chunk(pe, b, o, False)
                    for u in range(b * NU // B, (b + 1) * NU // B):
                        t, h = u // H1, u % H1
                        pe.wait_ge(a_lo_s, before[u + 1])
                        for j in range(t % NJ + 1):
                            last = three_pass(pe, down.acc(t)[:, h * P:(h + 1) * P],
                                              a_hi[:, u % NA, j * P:(j + 1) * P], a_lo[:, u % NA, j * P:(j + 1) * P],
                                              e.v_hi[:, b * NJ + j, h * P:(h + 1) * P], e.v_lo[:, b * NJ + j, h * P:(h + 1) * P],
                                              False, h == H1 - 1 and j == t % NJ)
                        last.then_inc(a_mm, 1)


def build(nc, d, out):
    e = Env()
    with ExitStack() as ctx:
        def holder(stack, side):
            return lambda n, s, dt=F32: stack.enter_context(nc.sbuf_tensor(n, s, dt, side=side))

        sb = holder(ctx, "left")
        sem = lambda n: nc.alloc_semaphore(n)
        dram = lambda n, s: nc.dram_tensor(n, s, F32, kind="Internal").ap()
        e.bank = [ctx.enter_context(nc.psum_tensor(f"bank{n}", [P, 512], F32)) for n in range(8)]
        e.ident = sb("ident", [P, P])
        e.ident_in, e.mask_in = sem("ident_in"), sem("mask_in")
        e.x_loaded = [sem(f"x_loaded{t}") for t in range(NT)]
        e.q_hi, e.q_lo = dram("q_hi", (B, 2, FR, HEADS, S)), dram("q_lo", (B, 2, FR, HEADS, S))
        e.k_hi, e.k_lo = dram("k_hi", (B, 2, FR, KV, S)), dram("k_lo", (B, 2, FR, KV, S))
        e.att_dram = dram("att", (B, KV, P, S))
        e.x1_dram = dram("x1", (T, D))
        e.vrow_dram = dram("v_row", (H1, P))
        with ExitStack() as to_down0, ExitStack() as hidden0:
            e.lrd0 = holder(to_down0, "right")("lrd0", [96, CH0 * P + D], F32R)
            with ExitStack() as to_up0:
                sb0 = holder(to_up0, "right")
                e.lr0 = sb0("lr0", [96, 2 * D + 2 * CH0 * P], F32R)
                e.mask = sb0("mask", [P, REP, P], BF16)
                e.identb = sb0("identb", [P, P], BF16)
                e.v = sb0("v_ones", [P, B, NJ, KV, 32])
                e.xT_hi = sb0("x0T_hi", [P, NC, T], F32R)
                e.xT_lo = sb0("x0T_lo", [P, NC, T], F32R)
                qkv_stage(nc, e, d)
                e.hid = holder(hidden0, "left")("hidden0", [P, CH0, T])
                attention_stage(nc, e, d)
            down0_stage(nc, e, d)
        with ExitStack() as to_down1, ExitStack() as hidden1:
            sb1 = holder(to_down1, "right")
            e.v_hi = sb1("v1_hi", [P, NT, D], F32R)
            e.v_lo = sb1("v1_lo", [P, NT, D], F32R)
            e.aT = sb1("weights1_T", [P, B * H1, CAUSAL])
            with ExitStack() as to_up1:
                sb2 = holder(to_up1, "right")
                e.lr1 = sb2("lr1", [96, 2 * D + 2 * CH1 * P], F32R)
                e.xT_hi = sb2("x1T_hi", [P, NC, T], F32R)
                e.xT_lo = sb2("x1T_lo", [P, NC, T], F32R)
                sigmoid_stage(nc, e, d)
                e.hid1 = holder(hidden1, "left")("hidden1", [P, CH1, T])
                up1_stage(nc, e, d)
            down1_stage(nc, e, d, out)


def _stacked(left, right):
    a = np.zeros((96, left.shape[1] + right.shape[1]), left.dtype)
    for g in range(3):
        a[32 * g:32 * g + left.shape[0], :left.shape[1]] = left
        a[32 * g:32 * g + left.shape[0], left.shape[1]:] = right
    return a


def _chunked(gate, up, n):
    a = np.zeros((2, n * P, D), gate.dtype)
    a[0, :gate.shape[0]] = gate
    a[1, :up.shape[0]] = up
    return np.ascontiguousarray(a.reshape(2, n, P, NC, P).transpose(1, 4, 0, 3, 2))


def _rope_tables():
    inv = (np.float32(1.0) / np.float32(10000.0) ** (np.arange(0, HD, 2, dtype=np.float32) / np.float32(HD))).astype(np.float32)
    angle = (np.arange(S, dtype=np.float32)[:, None] * inv[None, :]).astype(np.float32)
    rep = lambda a: np.ascontiguousarray(np.tile(a.astype(np.float32).T, (P // FR, 1)))
    return rep(np.cos(angle)), rep(np.sin(angle))


def _padded(a, shape):
    out = np.zeros(shape, a.dtype)
    out[tuple(slice(0, n) for n in a.shape)] = a
    return out


def kernel(**inputs):
    import ml_dtypes
    import concourse.bacc as _bacc
    from concourse.bass_utils import run_bass_kernel_spmd as _run

    i = {k: np.asarray(v) for k, v in inputs.items()}
    wq = i["L0_attn_w_qkv"]
    q = wq[:, :HEADS * HD].reshape(D, HEADS, FR, 2)
    k = wq[:, HEADS * HD:(HEADS + KV) * HD].reshape(D, KV, FR, 2)
    w_qkv = np.concatenate([q[..., 0].reshape(D, -1), q[..., 1].reshape(D, -1), k[..., 0].reshape(D, -1),
                            k[..., 1].reshape(D, -1), wq[:, (HEADS + KV) * HD:]], axis=1)
    bind = np.zeros((96, P), np.float32)
    for n, name in enumerate(("q", "k", "v")):
        bind[32 * n:32 * n + H1] = i[f"L1_attn_bv_{name}"]
    cos, sin = _rope_tables()
    after = np.arange(P)[None, :] > np.arange(P)[:, None]
    mask = np.where(after, np.float32(NEG), np.float32(0.0))
    heads = np.zeros((HEADS, NC, P), np.float32)
    for c in range(NC):
        for p in range(P):
            heads[c * (P // HD) + p // HD, c, p] = 1.0
    cat = lambda *a: np.concatenate(a, axis=1)
    n1 = CH1 * P
    arrays = {
        "x": np.ascontiguousarray(i["L0_attn_x"].reshape(T, D)),
        "w_qkv": np.ascontiguousarray(w_qkv),
        "w_o": np.ascontiguousarray(i["L0_attn_w_o"]),
        "cos": cos, "sin": sin, "head_rows": heads,
        "ident": np.eye(P, dtype=np.float32),
        "identb": np.eye(P).astype(ml_dtypes.bfloat16),
        "mask": np.ascontiguousarray(np.broadcast_to(mask[:, None, :], (P, REP, P))).astype(ml_dtypes.bfloat16),
        "w_gate_up0": _chunked(i["L0_ffn_gate_w"], i["L0_ffn_up_w"], CH0),
        "w_gate_up1": _chunked(i["L1_ffn_w1"], i["L1_ffn_w3"], CH1),
        "w_down0": np.ascontiguousarray(i["L0_ffn_down_w"].T),
        "w_down1": _padded(i["L1_ffn_w2"].T, (n1, D)),
        "lr0": _stacked(cat(i["L0_ffn_gate_sv"], i["L0_ffn_up_sv"]), cat(i["L0_ffn_gate_su"].T, i["L0_ffn_up_su"].T)),
        "lrd0": _stacked(i["L0_ffn_down_sv"], i["L0_ffn_down_su"].T),
        "lr1": _stacked(cat(i["L1_ffn_lora_A1"], i["L1_ffn_lora_A3"]),
                        cat(_padded(i["L1_ffn_lora_B1"].T, (16, n1)), _padded(i["L1_ffn_lora_B3"].T, (16, n1)))),
        "lrd1": _stacked(_padded(i["L1_ffn_lora_A2"], (16, n1)), i["L1_ffn_lora_B2"].T),
        "binders": bind,
    }
    nc = _bacc.Bacc("TRN2", target_bir_lowering=False, num_devices=1)
    d = {n: nc.dram_tensor(f"in_{n}", a.shape, mybir.dt.from_np(a.dtype), kind="ExternalInput").ap() for n, a in arrays.items()}
    out = nc.dram_tensor("out", (T, D), F32, kind="ExternalOutput").ap()
    build(nc, d, out)
    r = _run(nc, [{f"in_{n}": a for n, a in arrays.items()}], core_ids=[0])
    return r.results[0]["out"].reshape(B, S, D)
```

```python
import concourse.bass as bass
from concourse import mybir
from contextlib import ExitStack
import numpy as np

F32 = mybir.dt.float32
F32R = mybir.dt.float32r
ALU = mybir.AluOpType
ACT = mybir.ActivationFunctionType
AXX = mybir.AxisListType.X

P = 128
B, S, D = 2, 512, 512
T = B * S
NT = T // P
NJ = S // P
NC = D // P
HEADS, KV, HD = 32, 8, 16
REP = HEADS // KV
FR = HD // 2
GROUPS = B * KV
STK = 3 * HD + 1
H1 = 4
EPS = 1e-5
NEG = -1.0e30
QW = (HEADS + 2 * KV) * HD
CH0, CH1 = 1792 // P, 11
S1_PIECES = [(0, 0, 4), (1, 0, 2), (1, 2, 2)] + [(i, h, 1) for i in (2, 3) for h in range(4)]
S1_END = [4, 6, 8, 9, 10, 11, 12, 13, 14, 15, 16]
S2_PIECES = [(j, h, 1) for j in (0, 1) for h in range(4)] + [(2, 0, 2), (2, 2, 2), (3, 0, 4)]
S2_END = [4, 8, 10, 11]
STEPS = 16 * CH0
G_STEPS = 13
VALUES_AT = [9, 12, 14, 15]


class Env:
    pass


def three_pass(pe, out, w_hi, w_lo, m_hi, m_lo, first, last):
    pe.matmul(out, w_hi, m_hi, start=first, stop=False, skip_group_check=True)
    pe.matmul(out, w_lo, m_hi, start=False, stop=False, skip_group_check=True)
    return pe.matmul(out, w_hi, m_lo, start=False, stop=last, skip_group_check=True)


def f32(ap):
    return ap.bitcast(F32)


class Norm:

    def __init__(self, nc, ctx, tag, src, dst, need, bank, ident, xT_hi, xT_lo, side="left"):
        sb = lambda n, s, d=F32: ctx.enter_context(nc.sbuf_tensor(f"{tag}_{n}", s, d, side=side))
        sem = lambda n: nc.alloc_semaphore(f"{tag}_{n}")
        self.src, self.dst, self.need, self.bank = src, dst, need, bank
        self.stats = sb("stats", [P, NT, 6])
        self.mv = sb("mv", [P, NT, 2])
        self.std = sb("std", [P, NT])
        self.rstd = sb("rstd", [P, NT])
        self.ident, self.xT_hi, self.xT_lo = ident, xT_hi, xT_lo
        self.raw = sem("stats_raw")
        self.stat = sem("stats_ready")
        self.stdd = sem("std_ready")
        self.rst = sem("rstd_ready")
        self.normed = sem("normed")
        self.transposed = sem("transposed")
        self.hi = sem("xT_hi_ready")
        self.lo = sem("xT_lo_ready")

    def dve_stats(self, dve, t):
        dve.wait_ge(*self.need(t))
        dve.bn_stats(self.stats[:, t, :], self.src[:, t, :]).then_inc(self.raw, 1)
        dve.wait_ge(self.raw, t + 1)
        dve.bn_aggr(self.mv[:, t, :], self.stats[:, t, :]).then_inc(self.stat, 1)

    def act_std(self, act, t):
        act.wait_ge(self.stat, t + 1)
        act.activation(self.std[:, t:t + 1], self.mv[:, t, 1:2], ACT.Sqrt, bias=EPS, scale=1.0).then_inc(self.stdd, 1)

    def dve_norm(self, dve, t):
        dve.wait_ge(self.stdd, t + 1)
        dve.reciprocal(self.rstd[:, t:t + 1], self.std[:, t:t + 1]).then_inc(self.rst, 1)
        dve.wait_ge(self.rst, t + 1)
        dve.tensor_scalar(self.dst[:, t, :], self.src[:, t, :], self.mv[:, t, 0:1], self.rstd[:, t:t + 1],
                          ALU.subtract, ALU.mult).then_inc(self.normed, 1)

    def pe_transpose(self, pe, t, bank_used_by):
        pe.wait_ge(self.normed, t + 1)
        if bank_used_by >= 0:
            pe.wait_ge(self.lo, bank_used_by + 1)
        for c in range(NC):
            last = pe.transpose(self.bank(t)[:, c * P:(c + 1) * P], self.dst[:, t, c * P:(c + 1) * P], self.ident[:, :])
        last.then_inc(self.transposed, 1)

    def act_hi(self, act, t):
        act.wait_ge(self.transposed, t + 1)
        act.activation(self.xT_hi[:, :, t * P:(t + 1) * P], self.bank(t)[:, :].rearrange("p (c s) -> p c s", c=NC),
                       ACT.Copy).then_inc(self.hi, 1)

    def dve_lo(self, dve, t):
        dve.wait_ge(self.hi, t + 1)
        dve.tensor_tensor(self.xT_lo[:, :, t * P:(t + 1) * P], self.bank(t)[:, :].rearrange("p (c s) -> p c s", c=NC),
                          f32(self.xT_hi[:, :, t * P:(t + 1) * P]), ALU.subtract).then_inc(self.lo, 1)


def stack_hi(act, stack, raw, cols, loaded, value, done):
    act.wait_ge(loaded, value)
    act.activation(stack[:, cols], raw[:, cols], ACT.Copy).then_inc(done, 1)


def stack_lo(dve, stack, raw, left, right, hi_done, value, done):
    dve.wait_ge(hi_done, value)
    for rows, cols in ((slice(64, 96), left), (slice(32, 64), right)):
        if cols.stop > cols.start:
            dve.tensor_tensor(stack[rows, cols], raw[rows, cols], f32(stack[rows, cols]), ALU.subtract).then_inc(done, 1)


class Up:
    def __init__(self, nc, ctx, tag, n, combine, banks, w_dram, xT_hi, xT_lo, lr, hid, early):
        sb = lambda nm, s, d=F32: ctx.enter_context(nc.sbuf_tensor(f"{tag}_{nm}", s, d))
        sem = lambda nm: nc.alloc_semaphore(f"{tag}_{nm}")
        self.n, self.combine, self.banks, self.w_dram = n, combine, banks, w_dram
        self.xT_hi, self.xT_lo, self.lr, self.hid = xT_hi, xT_lo, lr, hid
        self.w_raw, self.raw = early
        self.w_eff = sb("w_eff", [P, 2, NC, P])
        self.w_hi = sb("w_hi", [P, 2, 2, NC, P], F32R)
        self.w_lo = sb("w_lo", [P, 2, 2, NC, P], F32R)
        self.th = sb("tanh", [P, 2, S])
        self.ut = sb("gated", [P, 2, S])
        self.fac = sem("factor_mm")
        self.eff = [sem("gate_eff"), sem("up_eff")]
        self.whi = sem("w_hi_ready")
        self.wlo = sem("w_lo_ready")
        self.mm = sem("gate_up_mm")
        self.tanh = sem("tanh_ready")
        self.u = sem("gated_ready")
        self.h = sem("hidden_ready")
        self.hid_free = None

    def sp_load(self, sp, o):
        if o >= 2:
            sp.wait_ge(self.eff[1], o - 1)
        sp.dma_start(self.w_raw[:, o % 2], self.w_dram[o]).then_inc(self.raw[o % 2], 16)

    def pe_factor(self, pe, o, k):
        if k == 0 and o >= 2:
            pe.wait_ge(self.h, 2 * (o - 2) + 1)
        if k == 1 and o >= 2:
            pe.wait_ge(self.u, 2 * (o - 2) + 2)
        if k == 1 and o == 1:
            pe.wait_ge(self.eff[0], 1)
        unit = (0 if o == 0 else 6 * (o - 1) + 2) + k
        at = 2 * D + (2 * o + k) * P
        for c in range(NC):
            last = pe.matmul(self.banks[unit % 3][:, c * P:(c + 1) * P],
                             self.lr[0:96, k * D + c * P:k * D + (c + 1) * P],
                             self.lr[0:96, at:at + P],
                             start=True, stop=True)
        last.then_inc(self.fac, 1)

    def factor_bank(self, o, k):
        return self.banks[((0 if o == 0 else 6 * (o - 1) + 2) + k) % 3]

    def dve_combine(self, dve, o, k):
        dve.wait_ge(self.fac, 2 * o + k + 1)
        dve.wait_ge(self.raw[o % 2], 16 * (o // 2 + 1))
        if o >= 1:
            dve.wait_ge(self.wlo, 2 * (o - 1) + k + 1)
        op0, scale, op1 = self.combine
        dve.scalar_tensor_tensor(out=self.w_eff[:, k].rearrange("p c m -> p (c m)"), in0=self.factor_bank(o, k)[:, :],
                                 scalar=scale, in1=self.w_raw[:, o % 2, k].rearrange("p c m -> p (c m)"),
                                 op0=op0, op1=op1).then_inc(self.eff[k], 1)

    def act_hi(self, act, o, k):
        act.wait_ge(self.eff[k], o + 1)
        if o >= 2:
            act.wait_ge(self.mm, 4 * (o - 1))
        act.activation(self.w_hi[:, o % 2, k], self.w_eff[:, k], ACT.Copy).then_inc(self.whi, 1)

    def pool_lo(self, pool, o, k):
        pool.wait_ge(self.whi, 2 * o + k + 1)
        pool.tensor_tensor(self.w_lo[:, o % 2, k], self.w_eff[:, k], f32(self.w_hi[:, o % 2, k]),
                           ALU.subtract).then_inc(self.wlo, 1)

    def pe_product(self, pe, o, b, k, c):
        more = o + 1 < self.n
        if c == 0:
            if b == 0:
                pe.wait_ge(self.wlo, 2 * o + k + 1)
            if (b, k) == (0, 0):
                if o >= 1:
                    pe.wait_ge(self.h, 2 * o)
                else:
                    pe.wait_ge(self.eff[1], 1)
            if (b, k) == (0, 1) and more:
                pe.wait_ge(self.eff[0], o + 2)
            if (b, k) == (1, 0) and more:
                pe.wait_ge(self.eff[1], o + 2)
            if (b, k) == (1, 1):
                pe.wait_ge(self.u, 2 * o + 1)
        last = three_pass(pe, self.product_bank(o, b, k)[:, :], self.w_hi[:, o % 2, k, c, :], self.w_lo[:, o % 2, k, c, :],
                          self.xT_hi[:, c, b * S:(b + 1) * S], self.xT_lo[:, c, b * S:(b + 1) * S],
                          c == 0, c == NC - 1)
        if c == NC - 1:
            last.then_inc(self.mm, 1)

    def pe_factors(self, pe, o, r):
        if r == 0 and o + 1 < self.n:
            self.pe_factor(pe, o + 1, 0)
            self.pe_factor(pe, o + 1, 1)

    def pe_step(self, pe, o, r):
        self.pe_product(pe, o, r // 8, r // 4 % 2, r % 4)

    def dve_step(self, dve, o, r):
        if r == 0 and o >= 1:
            self.dve_hidden(dve, o - 1, 1)
        if r in (1, 2) and o + 1 < self.n:
            self.dve_combine(dve, o + 1, r - 1)
        if r in (5, 13):
            self.dve_gate(dve, o, r // 8)
        if r == 8:
            self.dve_hidden(dve, o, 0)

    def act_step(self, act, o, r):
        if r in (2, 3) and o + 1 < self.n:
            self.act_hi(act, o + 1, r - 2)
        if r in (4, 12):
            self.act_tanh(act, o, r // 8)

    def pool_step(self, pool, o, r):
        if r in (3, 4) and o + 1 < self.n:
            self.pool_lo(pool, o + 1, r - 3)

    def product_bank(self, o, b, k):
        return self.banks[(6 * o + 4 + 2 * b + k) % 3]

    def act_tanh(self, act, o, b):
        act.wait_ge(self.mm, 4 * o + 2 * b + 1)
        if o >= 1:
            act.wait_ge(self.u, 2 * (o - 1) + b + 1)
        act.activation(self.th[:, b, :], self.product_bank(o, b, 0)[:, :], ACT.Tanh, scale=0.5).then_inc(self.tanh, 1)

    def dve_gate(self, dve, o, b):
        dve.wait_ge(self.tanh, 2 * o + b + 1)
        if o >= 1:
            dve.wait_ge(self.h, 2 * (o - 1) + b + 1)
        dve.scalar_tensor_tensor(out=self.ut[:, b, :], in0=self.th[:, b, :], scalar=1.0,
                                 in1=self.product_bank(o, b, 0)[:, :], op0=ALU.add, op1=ALU.mult).then_inc(self.u, 1)

    def dve_hidden(self, dve, o, b):
        dve.wait_ge(self.mm, 4 * o + 2 * b + 2)
        dve.wait_ge(self.u, 2 * o + b + 1)
        if o == 0 and b == 0 and self.hid_free:
            dve.wait_ge(*self.hid_free)
        dve.scalar_tensor_tensor(out=self.hid[:, o, b * S:(b + 1) * S], in0=self.ut[:, b, :], scalar=0.5,
                                 in1=self.product_bank(o, b, 1)[:, :], op0=ALU.mult, op1=ALU.mult).then_inc(self.h, 1)


class Down:
    def __init__(self, nc, ctx, tag, n, combine, bank, w_dram, lr, hid, ends, early):
        sb = lambda nm, s, d=F32: ctx.enter_context(nc.sbuf_tensor(f"{tag}_{nm}", s, d))
        sem = lambda nm: nc.alloc_semaphore(f"{tag}_{nm}")
        self.n, self.combine, self.bank, self.w_dram, self.lr, self.hid = n, combine, bank, w_dram, lr, hid
        self.ends = ends
        self.w_raw, self.raw = early
        self.w_eff = sb("w_eff", [P, D])
        self.w_hi = sb("w_hi", [P, n, D], F32R)
        self.w_lo = sb("w_lo", [P, n, D], F32R)
        self.h_hi = sb("h_hi", [P, 2, S], F32R)
        self.h_lo = sb("h_lo", [P, 2, S], F32R)
        self.fac = sem("factor_mm")
        self.eff = sem("w_eff_ready")
        self.whi = sem("w_hi_ready")
        self.wlo = sem("w_lo_ready")
        self.hhi = sem("h_hi_ready")
        self.hlo = sem("h_lo_ready")
        self.mm = sem("down_mm")
        self.full = sem("tile_mm")

    def acc(self, t):
        return self.bank[t]

    def sp_load(self, sp, o):
        if o >= 2:
            sp.wait_ge(self.eff, o - 1)
        sp.dma_start(self.w_raw[:, o % 2, :], self.w_dram[o * P:(o + 1) * P, :]).then_inc(self.raw[o % 2], 16)

    def pe_factor(self, pe, o):
        if o >= 2:
            pe.wait_ge(self.eff, o - 1)
        pe.matmul(self.bank[4 + o % 2][:, :], self.lr[0:96, o * P:(o + 1) * P],
                  self.lr[0:96, self.n * P:self.n * P + D], start=True, stop=True).then_inc(self.fac, 1)

    def dve_combine(self, dve, o):
        dve.wait_ge(self.fac, o + 1)
        dve.wait_ge(self.raw[o % 2], 16 * (o // 2 + 1))
        if o >= 1:
            dve.wait_ge(self.wlo, o)
        op0, scale, op1 = self.combine
        dve.scalar_tensor_tensor(out=self.w_eff[:, :], in0=self.bank[4 + o % 2][:, :], scalar=scale,
                                 in1=self.w_raw[:, o % 2, :], op0=op0, op1=op1).then_inc(self.eff, 1)

    def act_whi(self, act, o):
        act.wait_ge(self.eff, o + 1)
        act.activation(self.w_hi[:, o, :], self.w_eff[:, :], ACT.Copy).then_inc(self.whi, 1)

    def dve_wlo(self, dve, o):
        dve.wait_ge(self.whi, o + 1)
        dve.tensor_tensor(self.w_lo[:, o, :], self.w_eff[:, :], f32(self.w_hi[:, o, :]), ALU.subtract).then_inc(self.wlo, 1)

    def act_hhi(self, act, b, o):
        k = self.n * b + o
        if k >= 2:
            b2, o2 = divmod(k - 2, self.n)
            if self.ends and o2 == self.n - 1:
                act.wait_ge(self.full, NJ * (b2 + 1))
            else:
                act.wait_ge(self.mm, k - 1 - (b2 if self.ends else 0))
        act.activation(self.h_hi[:, k % 2, :], self.hid[:, o, b * S:(b + 1) * S], ACT.Copy).then_inc(self.hhi, 1)

    def pool_hlo(self, pool, b, o):
        k = self.n * b + o
        pool.wait_ge(self.hhi, k + 1)
        pool.tensor_tensor(self.h_lo[:, k % 2, :], self.hid[:, o, b * S:(b + 1) * S], f32(self.h_hi[:, k % 2, :]),
                           ALU.subtract).then_inc(self.hlo, 1)

    def pe_chunk(self, pe, b, o):
        k = self.n * b + o
        last_of_tile = self.ends and o == self.n - 1
        if b == 0 and o + 2 < self.n:
            self.pe_factor(pe, o + 2)
        pe.wait_ge(self.hlo, k + 1)
        if b == 0:
            pe.wait_ge(self.wlo, o + 1)
        for i in range(NJ):
            own = slice(i * P, (i + 1) * P)
            last = three_pass(pe, self.acc(NJ * b + i)[:, :], self.h_hi[:, k % 2, own], self.h_lo[:, k % 2, own],
                              self.w_hi[:, o, :], self.w_lo[:, o, :], o == 0, last_of_tile)
            if last_of_tile:
                last.then_inc(self.full, 1)
        if not last_of_tile:
            last.then_inc(self.mm, 1)


def qkv_stage(nc, e, d):
    with ExitStack() as ctx:
        sb = lambda n, s, dt=F32: ctx.enter_context(nc.sbuf_tensor(n, s, dt))
        sem = lambda n: nc.alloc_semaphore(n)
        x_sb = sb("x", [P, NT, D])
        x_loaded = [sem(f"x_loaded{t}") for t in range(NT)]
        norm = Norm(nc, ctx, "norm0", x_sb, x_sb, lambda t: (x_loaded[t], 16), lambda t: e.bank[4 + t % 2], e.ident,
                    e.xT_hi, e.xT_lo)
        w_raw = sb("wqkv_raw", [P, NC, QW])
        w_hi = sb("wqkv_hi", [P, NC, QW], F32R)
        w_lo = sb("wqkv_lo", [P, NC, QW], F32R)
        cos = sb("cos", [P, S])
        sin = sb("sin", [P, S])
        prod = sb("rope_products", [P, 2, 4, S])
        rot = sb("rope_sum", [P, 2, 2, S])
        rot_hi = sb("rope_hi", [P, 2, 2, S], F32R)
        rot_lo = sb("rope_lo", [P, 2, 2, S], F32R)
        lr_raw = sb("lr0_raw", [96, e.lr0.shape[1]])
        lrd_raw = sb("lrd0_raw", [96, e.lrd0.shape[1]])
        w_loaded = [sem(f"wqkv_loaded{c}") for c in range(NC)]
        consts = sem("rope_tables_loaded")
        lr_in, lrd_in, lr_hi, lrd_hi = sem("lr0_loaded"), sem("lrd0_loaded"), sem("lr0_hi"), sem("lrd0_hi")
        lr_lo = sem("lr0_lo")
        w_hi_ready, w_lo_ready = sem("wqkv_hi_ready"), sem("wqkv_lo_ready")
        v_mm, v_ones = sem("v_mm"), sem("v_ones")
        pair_mm, products, summed, hi_ready, lo_ready = (sem("pair_mm"), sem("rope_prod_ready"), sem("rope_summed"),
                                                         sem("rope_hi_ready"), sem("rope_lo_ready"))
        stored = [sem("rope_stored0"), sem("rope_stored1")]
        pairs = [(0, 0), (0, 1), (0, 2), (1, 1), (1, 2), (1, 0)]
        rows = [KV * FR, P, P]
        cols = [(4 * P, 4 * P + KV * FR), (0, 2 * P), (P, 3 * P)]

        with nc.Block() as block:
            @block.sync
            def _(sp):
                sp.dma_start(e.ident[:, :], d["ident"]).then_inc(e.ident_in, 16)
                for t in range(NJ):
                    sp.dma_start(x_sb[:, t, :], d["x"][t * P:(t + 1) * P, :]).then_inc(x_loaded[t], 16)
                for c in range(NC):
                    sp.dma_start(w_raw[:, c, :], d["w_qkv"][c * P:(c + 1) * P, :]).then_inc(w_loaded[c], 16)
                for t in range(NJ, NT):
                    sp.dma_start(x_sb[:, t, :], d["x"][t * P:(t + 1) * P, :]).then_inc(x_loaded[t], 16)
                sp.dma_start(cos[:, :], d["cos"]).then_inc(consts, 16)
                sp.dma_start(sin[:, :], d["sin"]).then_inc(consts, 16)
                sp.dma_start(lr_raw[:, :], d["lr0"]).then_inc(lr_in, 16)
                sp.dma_start(lrd_raw[:, :], d["lrd0"]).then_inc(lrd_in, 16)
                sp.dma_start(e.mask[:, :], d["mask"]).then_inc(e.mask_in, 16)
                for o in range(2):
                    sp.dma_start(e.up0_raw[0][:, o], d["w_gate_up0"][o]).then_inc(e.up0_raw[1][o], 16)
                for n, (b, k) in enumerate(pairs):
                    sp.wait_ge(lo_ready, n + 1)
                    dst = [e.k_hi, e.k_lo] if k == 0 else [e.q_hi, e.q_lo]
                    h0, nh = (0, KV) if k == 0 else (16 * (k - 1), 16)
                    for part, src in enumerate((rot_hi, rot_lo)):
                        for r in range(2):
                            sp.dma_start(dst[part][b, r, :, h0:h0 + nh, :].rearrange("f h s -> h f s"),
                                         f32(src[0:rows[k], n % 2, r, :])).then_inc(stored[n % 2], 16)
                for s in stored:
                    sp.wait_ge(s, 64 * (len(pairs) // 2))

            @block.gpsimd
            def _(pool):
                for b in range(B):
                    pool.memset(e.v[:, b], 1.0).then_inc(v_ones, 1)
                for c in range(NC):
                    pool.wait_ge(w_hi_ready, c + 1)
                    pool.tensor_tensor(w_lo[:, c, :], w_raw[:, c, :], f32(w_hi[:, c, :]), ALU.subtract).then_inc(w_lo_ready, 1)
                for n, (b, k) in enumerate(pairs):
                    pool.wait_ge(products, 4 * (n + 1))
                    if n >= 2:
                        pool.wait_ge(lo_ready, n - 1)
                    R = rows[k]
                    pool.tensor_tensor(rot[0:R, n % 2, 0, :], prod[0:R, n % 2, 0, :], prod[0:R, n % 2, 1, :],
                                       ALU.subtract).then_inc(summed, 1)
                    pool.tensor_tensor(rot[0:R, n % 2, 1, :], prod[0:R, n % 2, 2, :], prod[0:R, n % 2, 3, :],
                                       ALU.add).then_inc(summed, 1)

            @block.scalar
            def _(act):
                for b in range(B):
                    for t in range(NJ * b, NJ * (b + 1)):
                        norm.act_std(act, t)
                        if t > NJ * b:
                            norm.act_hi(act, t - 1)
                    norm.act_hi(act, NJ * (b + 1) - 1)
                    if b == 0:
                        for c in range(NC):
                            act.wait_ge(w_loaded[c], 16)
                            act.activation(w_hi[:, c, :], w_raw[:, c, :], ACT.Copy).then_inc(w_hi_ready, 1)
                stack_hi(act, e.lr0, lr_raw, slice(0, 2 * D + 2 * CH0 * P), lr_in, 16, lr_hi)
                stack_hi(act, e.lrd0, lrd_raw, slice(0, CH0 * P + D), lrd_in, 16, lrd_hi)
                act.wait_ge(v_ones, B)
                for n, (b, k) in enumerate(pairs):
                    act.wait_ge(summed, 2 * (n + 1))
                    if n >= 2:
                        act.wait_ge(stored[n % 2], 64 * (n // 2))
                    act.activation(rot_hi[0:rows[k], n % 2], rot[0:rows[k], n % 2], ACT.Copy).then_inc(hi_ready, 1)
                    if n == 3 or n == len(pairs) - 1:
                        bv = 0 if n == 3 else 1
                        act.wait_ge(v_mm, bv + 1)
                        act.activation(e.v[:, bv, :, :, 0:HD],
                                       e.bank[6 + bv][:, :].rearrange("p (j g x) -> p j g x", j=NJ, g=KV), ACT.Copy)

            @block.vector
            def _(dve):
                norm.dve_stats(dve, 0)
                for t in range(NT):
                    if t + 1 < NT:
                        norm.dve_stats(dve, t + 1)
                    norm.dve_norm(dve, t)
                    if t >= 1:
                        norm.dve_lo(dve, t - 1)
                norm.dve_lo(dve, NT - 1)
                dve.wait_ge(consts, 32)

                def rest(n):
                    R = rows[pairs[n][1]]
                    dve.wait_ge(hi_ready, n + 1)
                    dve.tensor_tensor(rot_lo[0:R, n % 2], rot[0:R, n % 2], f32(rot_hi[0:R, n % 2]),
                                      ALU.subtract).then_inc(lo_ready, 1)

                for n, (b, k) in enumerate(pairs):
                    dve.wait_ge(pair_mm, n + 1)
                    if n >= 2:
                        dve.wait_ge(summed, 2 * (n - 1))
                    R = rows[k]
                    scale = 1.0 if k == 0 else HD ** -0.5
                    for m, (src, table) in enumerate(((0, cos), (1, sin), (0, sin), (1, cos))):
                        dve.scalar_tensor_tensor(out=prod[0:R, n % 2, m, :], in0=e.bank[2 * (n % 2) + src][0:R, :],
                                                 scalar=scale, in1=table[0:R, :], op0=ALU.mult,
                                                 op1=ALU.mult).then_inc(products, 1)
                    if n >= 1:
                        rest(n - 1)
                    if n == 2:
                        stack_lo(dve, e.lr0, lr_raw, slice(0, 2 * D), slice(2 * D, 2 * D + 2 * CH0 * P), lr_hi, 1, lr_lo)
                    if n == 4:
                        stack_lo(dve, e.lrd0, lrd_raw, slice(0, CH0 * P), slice(CH0 * P, CH0 * P + D), lrd_hi, 1, lr_lo)
                rest(len(pairs) - 1)

            @block.tensor
            def _(pe):
                pe.wait_ge(e.ident_in, 16)

                def products_of(b):
                    pe.wait_ge(norm.lo, NJ * (b + 1))
                    if b == 0:
                        pe.wait_ge(w_lo_ready, NC)
                    for n in range(3 * b, 3 * b + 3):
                        k = pairs[n][1]
                        if n >= 2:
                            pe.wait_ge(products, 4 * (n - 1))
                        for r in range(2):
                            c0 = cols[k][r]
                            for c in range(NC):
                                last = three_pass(pe, e.bank[2 * (n % 2) + r][0:rows[k], :], w_hi[:, c, c0:c0 + rows[k]],
                                                  w_lo[:, c, c0:c0 + rows[k]], e.xT_hi[:, c, b * S:(b + 1) * S],
                                                  e.xT_lo[:, c, b * S:(b + 1) * S], c == 0, c == NC - 1)
                        last.then_inc(pair_mm, 1)
                    for j in range(NJ):
                        tok = slice(b * S + j * P, b * S + (j + 1) * P)
                        for c in range(NC):
                            last = three_pass(pe, e.bank[6 + b][:, j * P:(j + 1) * P], e.xT_hi[:, c, tok], e.xT_lo[:, c, tok],
                                              w_hi[:, c, 5 * P:6 * P], w_lo[:, c, 5 * P:6 * P], c == 0, c == NC - 1)
                    last.then_inc(v_mm, 1)

                for t in range(NT):
                    norm.pe_transpose(pe, t, t - 2)
                for b in range(B):
                    products_of(b)


def attention_stage(nc, e, d):
    with ExitStack() as ctx:
        sb = lambda n, s, dt=F32: ctx.enter_context(nc.sbuf_tensor(n, s, dt))
        sem = lambda n: nc.alloc_semaphore(n)
        up = Up(nc, ctx, "up0", CH0, (ALU.mult, 1.0, ALU.mult), e.bank[0:3], d["w_gate_up0"], e.xT_hi, e.xT_lo, e.lr0, e.hid,
                e.up0_raw)
        qst = sb("q_stack", [64 + STK, 2, REP, S], F32R)
        kst = sb("k_stack", [64 + STK, 2, S], F32R)
        pt = sb("probs", [P, 2, REP, S])
        rmax = sb("row_max", [P, REP, NJ])
        negm = sb("minus_max", [P, REP * NJ])
        negrow = sb("minus_max_rows", [REP * NJ, P], F32R)
        att = sb("att_T", [P, 2, S])
        ones = sem("k_ones")
        stk = [sem(f"stack_loaded{n}") for n in range(4)]
        s1_mm, reduced, neg_done = sem("max_scores_mm"), sem("maxima"), sem("minus_max_ready")
        neg_mm, neg_copied, neg_row = sem("minus_max_mm"), sem("minus_max_copied"), sem("minus_max_row")
        s2_mm, exp_done, masked, pv_mm, att_out = (sem("scores_mm"), sem("exp_done"), sem("masked"), sem("pv_mm"),
                                                   sem("att_out"))
        att_stored = [sem("att_stored0"), sem("att_stored1")]
        LOADS = 16 * 6

        def rows_of(g):
            return 64 * (g % 2), (g // 2) % 2

        with nc.Block() as block:
            @block.sync
            def _(sp):
                def load_stack(g):
                    b, kv = g // KV, g % KV
                    r, slot = rows_of(g)
                    if g >= 4:
                        sp.wait_ge(s2_mm, 11 * (g - 3))
                    qh, ql, kh, kl = (x[b].rearrange("r f h s -> (r f) h s") for x in (e.q_hi, e.q_lo, e.k_hi, e.k_lo))
                    qs = lambda x: x[:, REP * kv:REP * (kv + 1), :]
                    for part, (q, k) in enumerate(((qh, kh), (qh, kl), (ql, kh))):
                        at = slice(r + part * HD, r + (part + 1) * HD)
                        sp.dma_start(f32(qst[at, slot, :, :]), qs(q)).then_inc(stk[g % 4], 16)
                        sp.dma_start(f32(kst[at, slot, :]), k[:, kv, :]).then_inc(stk[g % 4], 16)

                sp.wait_ge(ones, 4)
                load_stack(0)
                load_stack(1)
                load_stack(2)
                for g in range(GROUPS):
                    if g + 2 < CH0:
                        up.sp_load(sp, g + 2)
                    if g + 3 < GROUPS:
                        load_stack(g + 3)
                    if g >= 1:
                        sp.wait_ge(att_out, g)
                        sp.dma_start(e.att_dram[(g - 1) // KV, (g - 1) % KV], att[:, (g - 1) % 2, :]).then_inc(att_stored[(g - 1) % 2], 16)
                sp.wait_ge(up.eff[1], CH0 - 1)
                for o in range(2):
                    sp.dma_start(e.down0_raw[0][:, o, :], d["w_down0"][o * P:(o + 1) * P, :]).then_inc(e.down0_raw[1][o], 16)
                sp.wait_ge(att_out, GROUPS)
                sp.dma_start(e.att_dram[B - 1, KV - 1], att[:, (GROUPS - 1) % 2, :]).then_inc(att_stored[(GROUPS - 1) % 2], 16)
                for s in att_stored:
                    sp.wait_ge(s, 16 * (GROUPS // 2))

            @block.gpsimd
            def _(pool):
                for g in range(4):
                    r, slot = rows_of(g)
                    pool.memset(f32(kst[r:r + STK, slot, :]), 1.0).then_inc(ones, 1)
                pool.wait_ge(ones, 4)
                for k in range(2):
                    up.pool_lo(pool, 0, k)

                def mask_keys(g, j):
                    jj = NJ * g + j
                    pool.wait_ge(exp_done, 11 * g + S2_END[j])
                    diag = pt[:, jj % 2, :, 0:P]
                    pool.affine_select(out=diag, in_=diag, compare_op=ALU.is_ge, fill=0.0, base=0,
                                       pattern=[[0, REP], [1, P]], channel_multiplier=-1).then_inc(masked, 1)

                for step in range(STEPS):
                    g, s = step // G_STEPS - 1, step % G_STEPS
                    up.pool_step(pool, step // 16, step % 16)
                    for j in range(NJ):
                        if s == S2_END[j] + 2 and 0 <= g < GROUPS:
                            mask_keys(g, j)
                        if s == S2_END[j] + 2 - G_STEPS and g >= 1:
                            mask_keys(g - 1, j)

            @block.scalar
            def _(act):
                def minus_max_row(g):
                    r, slot = rows_of(g)
                    act.wait_ge(neg_mm, g + 1)
                    if g >= 1:
                        act.wait_ge(neg_row, 16 * g)
                    act.activation(negrow[:, :], e.bank[4][0:REP * NJ, 0:P], ACT.Copy).then_inc(neg_copied, 1)
                    act.wait_ge(neg_copied, g + 1)
                    if g >= 4:
                        act.wait_ge(s2_mm, 11 * (g - 3))
                    act.dma_start(f32(qst[r + STK - 1:r + STK, slot]).rearrange("o h (i s) -> o (h i) s", i=NJ),
                                  f32(negrow[:, :])).then_inc(neg_row, 16)

                def exp_piece(g, n):
                    j, h, nh = S2_PIECES[n]
                    n += 11 * g
                    jj = NJ * g + j
                    act.wait_ge(s2_mm, n + 1)
                    if jj >= 2:
                        act.wait_ge(pv_mm, jj - 1)
                    w = S - j * P
                    act.activation(pt[:, jj % 2, h:h + nh, 0:w],
                                   e.bank[5 + n % 2][:, 0:nh * w].rearrange("p (h s) -> p h s", h=nh),
                                   ACT.Exp).then_inc(exp_done, 1)

                for k in range(2):
                    up.act_hi(act, 0, k)
                for step in range(STEPS):
                    g, s = step // G_STEPS - 1, step % G_STEPS
                    up.act_step(act, step // 16, step % 16)
                    if s == 12 and g + 1 < GROUPS:
                        minus_max_row(g + 1)
                    if s >= 2 and 0 <= g < GROUPS:
                        exp_piece(g, s - 2)

            @block.vector
            def _(dve):
                def maxima(g, p):
                    i, h, nh = S1_PIECES[p]
                    dve.wait_ge(s1_mm, 11 * g + p + 1)
                    if p == 0 and g >= 1:
                        dve.wait_ge(neg_done, g)
                    w = (i + 1) * P
                    for n in range(nh):
                        own = e.bank[3 + p % 2][:, n * w:(n + 1) * w]
                        dve.tensor_tensor_reduce(out=own, in0=own,
                                                 in1=e.mask[:, S - w:S], scale=1.0, scalar=NEG, op0=ALU.add, op1=ALU.max,
                                                 accum_out=rmax[:, h + n, i:i + 1]).then_inc(reduced, 1)

                def negate(g):
                    dve.wait_ge(reduced, NJ * REP * (g + 1))
                    if g >= 1:
                        dve.wait_ge(neg_mm, g)
                    dve.tensor_scalar(negm[:, :], rmax[:, :, :].rearrange("p h i -> p (h i)"), -1.0, None,
                                      ALU.mult).then_inc(neg_done, 1)

                def evacuate(g):
                    dve.wait_ge(pv_mm, NJ * (g + 1))
                    if g >= 2:
                        dve.wait_ge(att_stored[g % 2], 16 * (g // 2))
                    dve.tensor_copy(att[:, g % 2, :], e.bank[7][:, :]).then_inc(att_out, 1)

                for k in range(2):
                    up.dve_combine(dve, 0, k)
                dve.wait_ge(e.mask_in, 16)
                for step in range(STEPS):
                    g, s = step // G_STEPS - 1, step % G_STEPS
                    up.dve_step(dve, step // 16, step % 16)
                    if g + 1 < GROUPS:
                        if s < 11:
                            maxima(g + 1, s)
                        if s == 10:
                            negate(g + 1)
                    if s == 3 and 1 <= g < GROUPS:
                        evacuate(g - 1)
                up.dve_hidden(dve, CH0 - 1, 1)
                evacuate(GROUPS - 1)

            @block.tensor
            def _(pe):
                def max_scores(g, p):
                    r, slot = rows_of(g)
                    if p == 0:
                        pe.wait_ge(stk[g % 4], LOADS * (g // 4 + 1))
                    K = slice(r, r + STK - 1)
                    i, h, nh = S1_PIECES[p]
                    if p >= 2:
                        pe.wait_ge(reduced, NJ * REP * g + S1_END[p - 2])
                    elif p == 0 and g >= 1:
                        pe.wait_ge(reduced, NJ * REP * g)
                    elif p == 1 and g >= 1:
                        pe.wait_ge(neg_copied, g)
                    w = (i + 1) * P
                    bank = e.bank[3 + p % 2]
                    for n in range(nh):
                        last = pe.matmul(bank[:, n * w:(n + 1) * w], qst[K, slot, h + n, i * P:(i + 1) * P], kst[K, slot, 0:w],
                                         start=(n == 0), stop=(n == nh - 1), skip_group_check=True)
                    last.then_inc(s1_mm, 1)

                def minus_max(g):
                    pe.wait_ge(neg_done, g + 1)
                    pe.transpose(e.bank[4][0:REP * NJ, 0:P], negm[:, :], e.ident[:, :]).then_inc(neg_mm, 1)

                def scores(g, n):
                    r, slot = rows_of(g)
                    j, h, nh = S2_PIECES[n]
                    if n == 0:
                        pe.wait_ge(neg_row, 16 * (g + 1))
                    K = slice(r, r + STK)
                    n += 11 * g
                    if n >= 2:
                        pe.wait_ge(exp_done, n - 1)
                    w = S - j * P
                    pe.matmul(e.bank[5 + n % 2][:, 0:nh * w], kst[K, slot, j * P:(j + 1) * P],
                              qst[K, slot, h:h + nh, j * P:], start=True, stop=True).then_inc(s2_mm, 1)

                def values(g, j):
                    jj = NJ * g + j
                    pe.wait_ge(masked, jj + 1)
                    if j == 0 and g >= 1:
                        pe.wait_ge(att_out, g)
                    b, kv = g // KV, g % KV
                    for h in range(REP):
                        last = pe.matmul(e.bank[7][32 * h:32 * (h + 1), j * P:], e.v[:, b, j, kv, :],
                                         pt[:, jj % 2, h, 0:S - j * P], start=(j == 0), stop=(j == NJ - 1),
                                         skip_group_check=True)
                    last.then_inc(pv_mm, 1)

                for k in range(2):
                    up.pe_factor(pe, 0, k)
                for step in range(STEPS):
                    g, s = step // G_STEPS - 1, step % G_STEPS
                    up.pe_factors(pe, step // 16, step % 16)
                    if g + 1 < GROUPS:
                        if s < 11:
                            max_scores(g + 1, s)
                    up.pe_step(pe, step // 16, step % 16)
                    if g + 1 < GROUPS and s == 11:
                        minus_max(g + 1)
                    if s >= 2 and 0 <= g < GROUPS:
                        scores(g, s - 2)
                    for j in range(NJ):
                        if s == VALUES_AT[j] and 0 <= g < GROUPS:
                            values(g, j)
                        if g >= 1 and s == VALUES_AT[j] - G_STEPS:
                            values(g - 1, j)


def down0_stage(nc, e, d):
    with ExitStack() as ctx:
        sb = lambda n, s, dt=F32: ctx.enter_context(nc.sbuf_tensor(n, s, dt))
        sem = lambda n: nc.alloc_semaphore(n)
        down = Down(nc, ctx, "down0", CH0, (ALU.mult, 1.0, ALU.mult), e.bank, d["w_down0"], e.lrd0, e.hid, False,
                    e.down0_raw)
        res = e.acc
        att = e.xn[:, :, :].rearrange("p (b c) s -> p b c s", b=B)
        den = e.den[0:HEADS].rearrange("p (b s) -> p b s", b=B)
        sel = sb("head_rows", [HEADS, NC, P])
        wo_hi = sb("wo_hi", [P, NC, D], F32R)
        wo_lo = sb("wo_lo", [P, NC, D], F32R)
        a_hi = sb("att_hi", [P, 2, S], F32R)
        a_lo = sb("att_lo", [P, 2, S], F32R)
        att_in, den_in, sel_in, wo_in = sem("att_in"), sem("den_in"), sem("sel_in"), [sem("wo_in0"), sem("wo_in1")]
        wo_hi_s, wo_lo_s, res_in = sem("wo_hi_ready"), sem("wo_lo_ready"), sem("res_in")
        rden_s, bc_mm, att_n = sem("rden_ready"), sem("broadcast_mm"), sem("att_normalised")
        a_hi_s, a_lo_s, o_mm = sem("att_hi_ready"), sem("att_lo_ready"), sem("att_out_mm")
        UNITS = [(b, c) for b in range(B) for c in range(NC)]
        bv = sb("bv", [3 * 32, P])
        sign, bind = sb("bind_sign", [3 * 32, P]), sb("bind", [3 * 32, P])
        alpha = sb("alpha", [3 * 32, 1])
        cols = sb("bind_cols", [P, 2 * 32])
        bv_in, bstep, b_t, b_cols, vrow_st, vrow_in = (sem("bv_in"), sem("bind_steps"), sem("bind_transposed"),
                                                       sem("bind_cols_ready"), sem("v_row_stored"), sem("v_row_in"))
        BIND_STEPS = 8
        norm = e.norm1

        with nc.Block() as block:
            @block.sync
            def _(sp):
                for b in range(B):
                    sp.dma_start(den[:, b, :], e.att_dram[b].rearrange("g (h r) s -> (g h) r s", h=REP)[:, HD, :]).then_inc(den_in, 16)
                sp.dma_start(sel[:, :, :], d["head_rows"]).then_inc(sel_in, 16)
                for b, c in UNITS:
                    for k in range(2):
                        sp.dma_start(att[64 * k:64 * (k + 1), b, c, :],
                                     e.att_dram[b, 2 * c + k].rearrange("(h r) s -> h r s", h=REP)[:, 0:HD, :]).then_inc(att_in, 16)
                for o in range(2, CH0):
                    down.sp_load(sp, o)
                    if o == 4:
                        sp.dma_start(res[:, :, :], d["x"].rearrange("(t p) n -> p t n", p=P)).then_inc(res_in, 16)
                for c in range(NC):
                    o = CH0 + c
                    if c < 2:
                        sp.wait_ge(down.eff, o - 1)
                    else:
                        sp.wait_ge(wo_lo_s, c - 1)
                    sp.dma_start(down.w_raw[:, o % 2, :], d["w_o"][c * P:(c + 1) * P, :]).then_inc(wo_in[c % 2], 16)
                    if c == 0:
                        sp.dma_start(bv[:, :], d["binders"]).then_inc(bv_in, 16)
                sp.dma_start(e.lr1_right[:, :], d["lr1"][:, 2 * D:LR1_FIRST]).then_inc(e.lr1_in, 16)
                sp.wait_ge(bc_mm, len(UNITS))
                sp.dma_start(e.den[:, :], d["lr1"][:, 0:2 * D]).then_inc(e.lr1_in, 16)
                sp.dma_start(e.up1_raw[0][:, 1], d["w_gate_up1"][1]).then_inc(e.up1_raw[1][1], 16)
                sp.wait_ge(wo_lo_s, NC)
                sp.dma_start(e.up1_raw[0][:, 0], d["w_gate_up1"][0]).then_inc(e.up1_raw[1][0], 16)
                sp.wait_ge(bstep, BIND_STEPS)
                sp.dma_start(e.vrow_dram, bind[64:64 + H1, :]).then_inc(vrow_st, 16)
                sp.wait_ge(vrow_st, 16)
                sp.dma_start(e.vrow[:, :], e.vrow_dram.rearrange("h p -> (h p)").partition_broadcast(P)).then_inc(vrow_in, 16)
                sp.wait_ge(vrow_in, 16)

            @block.gpsimd
            def _(pool):
                for b in range(B):
                    for o in range(CH0):
                        down.pool_hlo(pool, b, o)
                    for c in range(NC):
                        n = NC * b + c
                        pool.wait_ge(a_hi_s, n + 1)
                        pool.tensor_tensor(a_lo[:, n % 2, :], att[:, b, c, :], f32(a_hi[:, n % 2, :]),
                                           ALU.subtract).then_inc(a_lo_s, 1)

            @block.scalar
            def _(act):
                for b in range(B):
                    for o in range(CH0):
                        down.act_hhi(act, b, o)
                        if b == 0:
                            down.act_whi(act, o)
                        elif 4 <= o < 4 + NJ:
                            norm.act_std(act, o - 4)
                    for c in range(NC):
                        if b == 0:
                            act.wait_ge(wo_in[c % 2], 16 * (c // 2 + 1))
                            act.activation(wo_hi[:, c, :], down.w_raw[:, (CH0 + c) % 2, :], ACT.Copy).then_inc(wo_hi_s, 1)
                        n = NC * b + c
                        act.wait_ge(att_n, n + 1)
                        if n >= 2:
                            pb, pc = UNITS[n - 2]
                            if pc < NC - 1:
                                act.wait_ge(o_mm, (NC - 1) * pb + pc + 1)
                            else:
                                act.wait_ge(down.full, NJ * (pb + 1))
                        act.activation(a_hi[:, n % 2, :], att[:, b, c, :], ACT.Copy).then_inc(a_hi_s, 1)

            @block.vector
            def _(dve):
                def normalise(n):
                    b, c = UNITS[n]
                    dve.wait_ge(bc_mm, n + 1)
                    dve.tensor_tensor(att[:, b, c, :], att[:, b, c, :], e.bank[6 + n % 2][:, :],
                                      ALU.mult).then_inc(att_n, 1)

                for o in range(CH0):
                    down.dve_combine(dve, o)
                    down.dve_wlo(dve, o)
                    if o in (2, 5):
                        dve.wait_ge(den_in, 32)
                        b = o // 4
                        dve.reciprocal(den[:, b, :], den[:, b, :]).then_inc(rden_s, 1)
                    if o == 6:
                        dve.wait_ge(att_in, 16 * len(UNITS) * 2)
                    if o >= 6:
                        normalise(o - 6)
                for c in range(NC):
                    dve.wait_ge(wo_hi_s, c + 1)
                    dve.tensor_tensor(wo_lo[:, c, :], down.w_raw[:, (CH0 + c) % 2, :], f32(wo_hi[:, c, :]),
                                      ALU.subtract).then_inc(wo_lo_s, 1)
                steps = [0]

                def step(ins):
                    ins.then_inc(bstep, 1)
                    steps[0] += 1
                    dve.wait_ge(bstep, steps[0])

                dve.wait_ge(bv_in, 16)
                step(dve.tensor_scalar(sign[:, :], bv[:, :], 0.0, 2.0, ALU.is_ge, ALU.mult))
                step(dve.tensor_scalar(sign[:, :], sign[:, :], -1.0, None, ALU.add))
                step(dve.tensor_tensor(bind[:, :], bv[:, :], sign[:, :], ALU.mult))
                step(dve.reduce_sum(alpha[:, :], bind[:, :], axis=AXX))
                step(dve.tensor_scalar(bind[:, :], sign[:, :], alpha[:, 0:1], None, ALU.mult))
                step(dve.tensor_scalar(bind[:, :], bind[:, :], 1.0 / P, None, ALU.mult))
                step(dve.tensor_tensor(bind[:, :], bind[:, :], bv[:, :], ALU.subtract))
                step(dve.tensor_tensor(bind[:, :], bind[:, :], bv[:, :], ALU.add))

                dve.wait_ge(b_t, 1)
                step(dve.tensor_copy(cols[:, :], e.bank[6][:, 0:2 * 32]))
                step(dve.tensor_tensor(e.qk[:, :], cols[:, 0:H1], cols[:, 32:32 + H1], ALU.mult))

                def total(t):
                    dve.wait_ge(down.full, t + 1)
                    dve.tensor_tensor(res[:, t, :], res[:, t, :], down.acc(t)[:, :], ALU.add).then_inc(e.sum0, 1)

                dve.wait_ge(res_in, 16)
                for t in range(NJ):
                    total(t)
                    norm.dve_stats(dve, t)
                dve.wait_ge(a_lo_s, NC)
                for t in range(NJ):
                    norm.dve_norm(dve, t)
                for t in range(NJ, NT):
                    total(t)

            @block.tensor
            def _(pe):
                for o in range(2):
                    down.pe_factor(pe, o)
                for b in range(B):
                    if b == 1:
                        pe.wait_ge(bstep, BIND_STEPS + 1)
                    for o in range(CH0):
                        down.pe_chunk(pe, b, o)
                        if b == 0 and o >= 5 and o - 5 < len(UNITS):
                            n = o - 5
                            ub, c = UNITS[n]
                            if n == 0:
                                pe.wait_ge(sel_in, 16)
                            if c == 0:
                                pe.wait_ge(rden_s, ub + 1)
                            if n >= 2:
                                pe.wait_ge(att_n, n - 1)
                            pe.matmul(e.bank[6 + n % 2][:, :], sel[:, c, :], den[:, ub, :], start=True, stop=True).then_inc(bc_mm, 1)
                    for c in range(NC):
                        n = NC * b + c
                        pe.wait_ge(a_lo_s, n + 1)
                        if b == 0:
                            pe.wait_ge(wo_lo_s, c + 1)
                        for i in range(NJ):
                            own = slice(i * P, (i + 1) * P)
                            last = three_pass(pe, down.acc(NJ * b + i)[:, :], a_hi[:, n % 2, own], a_lo[:, n % 2, own],
                                              wo_hi[:, c, :], wo_lo[:, c, :], False, c == NC - 1)
                            if c == NC - 1:
                                last.then_inc(down.full, 1)
                        if c < NC - 1:
                            last.then_inc(o_mm, 1)
                    if b == 0:
                        pe.wait_ge(att_n, len(UNITS))
                        pe.wait_ge(bstep, BIND_STEPS)
                        pe.transpose(e.bank[6][:, 0:64], bind[0:64, :], e.ident[0:64, 0:64]).then_inc(b_t, 1)
                for t in range(NJ):
                    pe.wait_ge(e.sum0, t + 1)
                    norm.pe_transpose(pe, t, -1)


U_STEPS = 22
SCORES_AT = [0, 4, 8, 12]
TANH_AT, MASK_AT, HI_AT, LO_AT = 1, 2, 3, 4
VALUES1_AT = [6, 10, 14, 18]


LR1_FIRST = 2 * D + 4 * P


def layer1_stage(nc, e, d, outer):
    with ExitStack() as ctx:
        sb = lambda n, s, dt=F32: ctx.enter_context(nc.sbuf_tensor(n, s, dt))
        sem = lambda n: nc.alloc_semaphore(n)
        norm, units = e.norm1, [(b, h) for b in range(B) for h in range(H1)]
        NL = 2 * D + 2 * CH1 * P
        FIRST = LR1_FIRST
        TRANSPOSE_AT, SPLIT_AT = {1: NJ, 2: NJ + 1, 3: NJ + 2, 5: NJ + 3}, {2: NJ, 3: NJ + 1, 4: NJ + 2, 6: NJ + 3}
        with ExitStack() as before_hidden:
            lr_raw = before_hidden.enter_context(nc.sbuf_tensor("lr1_raw", [96, NL], F32))
        e.hid1 = outer.enter_context(nc.sbuf_tensor("hidden1", [P, CH1, T], F32))
        lr1 = sb("lr1", [96, NL], F32R)
        up = Up(nc, ctx, "up1", CH1, (ALU.mult, 2.0, ALU.add), e.bank[0:3], d["w_gate_up1"], e.xT_hi, e.xT_lo, lr1, e.hid1,
                e.up1_raw)
        lr_in, lr_hi, lr_lo = sem("lr1_loaded"), sem("lr1_hi"), sem("lr1_lo")
        lrd_in, lrd_hi, lrd_lo = sem("lrd1_loaded"), sem("lrd1_hi"), sem("lrd1_lo")
        up.hid_free = (lr_lo, 3)
        lrd_raw = up.w_raw[0:96].rearrange("p a k c m -> p (a k c m)")[:, 0:CH1 * P + D]
        xk = sb("xk_scaled", [P, S])
        xk_hi = sb("xk_hi", [P, 2, S], F32R)
        xk_lo = sb("xk_lo", [P, 2, S], F32R)
        vt = sb("v_scaled", [P, NJ, P])
        v_hi = sb("v1_hi", [P, 2, NJ, P], F32R)
        v_lo = sb("v1_lo", [P, 2, NJ, P], F32R)
        th = sb("weights1_T", [P, 2, S])
        a_hi = sb("weights1_hi", [P, 2, S], F32R)
        a_lo = sb("weights1_lo", [P, 2, S], F32R)
        x_sum, k_s, k_hi_s, k_lo_s = sem("xk_sum"), sem("xk_ready"), sem("xk_hi_ready"), sem("xk_lo_ready")
        v_s, v_hi_s, v_lo_s = sem("v1_ready"), sem("v1_hi_ready"), sem("v1_lo_ready")
        sc_mm, th_s, mask_s = sem("scores1_mm"), sem("tanh1_ready"), sem("masked1")
        a_hi_s, a_lo_s, pv_mm, acc_s = sem("weights1_hi_ready"), sem("weights1_lo_ready"), sem("values1_mm"), sem("attention1_added")

        def width(j):
            return S - j * P

        def dve_key(dve, n):
            b, h = units[n]
            tok = slice(b * S, (b + 1) * S)
            dve.wait_ge(norm.lo, NJ * (b + 1))
            if n >= 1:
                dve.wait_ge(k_lo_s, n)
            dve.tensor_tensor(xk[:, :], f32(e.xT_hi[:, h, tok]), f32(e.xT_lo[:, h, tok]), ALU.add).then_inc(x_sum, 1)
            dve.wait_ge(x_sum, n + 1)
            dve.tensor_scalar(xk[:, :], xk[:, :], e.qk[:, h:h + 1], None, ALU.mult).then_inc(k_s, 1)

        def act_key(act, n):
            act.wait_ge(k_s, n + 1)
            if n >= 2:
                act.wait_ge(sc_mm, NJ * (n - 1))
            act.activation(xk_hi[:, n % 2, :], xk[:, :], ACT.Copy).then_inc(k_hi_s, 1)

        def dve_key_lo(dve, n):
            dve.wait_ge(k_hi_s, n + 1)
            dve.tensor_tensor(xk_lo[:, n % 2, :], xk[:, :], f32(xk_hi[:, n % 2, :]), ALU.subtract).then_inc(k_lo_s, 1)

        def pool_value(pool, n):
            b, h = units[n]
            pool.wait_ge(norm.normed, NJ * (b + 1))
            if n >= 1:
                pool.wait_ge(v_lo_s, n)
            cols = e.vrow[:, h * P:(h + 1) * P]
            pool.tensor_tensor(vt[:, :, :], e.xn[:, b * NJ:(b + 1) * NJ, h * P:(h + 1) * P],
                               cols.unsqueeze(1).to_broadcast([P, NJ, P]), ALU.mult).then_inc(v_s, 1)

        def act_value(act, n):
            act.wait_ge(v_s, n + 1)
            if n >= 2:
                act.wait_ge(pv_mm, NJ * (n - 1))
            act.activation(v_hi[:, n % 2], vt[:, :, :], ACT.Copy, scale=0.5).then_inc(v_hi_s, 1)

        def dve_value_lo(dve, n):
            dve.wait_ge(v_hi_s, n + 1)
            dve.scalar_tensor_tensor(out=v_lo[:, n % 2], in0=vt[:, :, :], scalar=0.5, in1=f32(v_hi[:, n % 2]),
                                     op0=ALU.mult, op1=ALU.subtract).then_inc(v_lo_s, 1)

        def pe_scores(pe, n, j):
            b, h = units[n]
            m = NJ * n + j
            if j == 0:
                pe.wait_ge(k_lo_s, n + 1)
            if m >= 2:
                pe.wait_ge(th_s, m - 1)
            three_pass(pe, e.bank[3 + m % 2][:, 0:width(j)], xk_hi[:, n % 2, j * P:(j + 1) * P],
                       xk_lo[:, n % 2, j * P:(j + 1) * P], e.xT_hi[:, h, b * S + j * P:(b + 1) * S],
                       e.xT_lo[:, h, b * S + j * P:(b + 1) * S], True, True).then_inc(sc_mm, 1)

        def act_tanh(act, n, j):
            m = NJ * n + j
            act.wait_ge(sc_mm, m + 1)
            if m >= 2:
                act.wait_ge(a_lo_s, m - 1)
            act.activation(th[:, m % 2, 0:width(j)], e.bank[3 + m % 2][:, 0:width(j)], ACT.Tanh,
                           scale=2.0 * P ** -0.5).then_inc(th_s, 1)

        def pool_mask(pool, n, j):
            m = NJ * n + j
            pool.wait_ge(th_s, m + 1)
            diag = th[:, m % 2, 0:P]
            pool.affine_select(out=diag, in_=diag, compare_op=ALU.is_ge, fill=-1.0, base=0, pattern=[[1, P]],
                               channel_multiplier=-1).then_inc(mask_s, 1)

        def act_weight(act, n, j):
            m = NJ * n + j
            act.wait_ge(mask_s, m + 1)
            if m >= 2:
                act.wait_ge(pv_mm, m - 1)
            act.activation(a_hi[:, m % 2, 0:width(j)], th[:, m % 2, 0:width(j)], ACT.Copy, bias=1.0).then_inc(a_hi_s, 1)

        def dve_weight_lo(dve, n, j):
            m = NJ * n + j
            dve.wait_ge(a_hi_s, m + 1)
            dve.scalar_tensor_tensor(out=a_lo[:, m % 2, 0:width(j)], in0=th[:, m % 2, 0:width(j)], scalar=1.0,
                                     in1=f32(a_hi[:, m % 2, 0:width(j)]), op0=ALU.add, op1=ALU.subtract).then_inc(a_lo_s, 1)

        def pe_values(pe, n, j):
            m = NJ * n + j
            pe.wait_ge(a_lo_s, m + 1)
            if j == 0:
                pe.wait_ge(v_lo_s, n + 1)
                if n >= 1:
                    pe.wait_ge(acc_s, n)
            for i in range(j, NJ):
                own = slice((i - j) * P, (i - j + 1) * P)
                last = three_pass(pe, e.bank[5][:, i * P:(i + 1) * P], a_hi[:, m % 2, own], a_lo[:, m % 2, own],
                                  v_hi[:, n % 2, j, :], v_lo[:, n % 2, j, :], i == 0 and j == 0, j == NJ - 1)
            last.then_inc(pv_mm, 1)

        def dve_add(dve, n):
            b, h = units[n]
            dve.wait_ge(pv_mm, NJ * (n + 1))
            own = e.acc[:, b * NJ:(b + 1) * NJ, h * P:(h + 1) * P]
            dve.tensor_tensor(own, own, e.bank[5][:, :].rearrange("p (i s) -> p i s", i=NJ), ALU.add).then_inc(acc_s, 1)

        with nc.Block() as block:
            @block.sync
            def _(sp):
                sp.dma_start(lr_raw[:, FIRST:], d["lr1"][:, FIRST:]).then_inc(lr_in, 16)
                for o in range(2, CH1):
                    up.sp_load(sp, o)
                sp.wait_ge(up.eff[1], CH1)
                sp.dma_start(lrd_raw, d["lrd1"]).then_inc(lrd_in, 16)

            @block.gpsimd
            def _(pool):
                for k in range(2):
                    up.pool_lo(pool, 0, k)
                pool_value(pool, 0)
                for o in range(CH1):
                    for r in range(16):
                        up.pool_step(pool, o, r)
                        n, s = divmod(16 * o + r, U_STEPS)
                        for j in range(NJ):
                            if s == SCORES_AT[j] + MASK_AT:
                                pool_mask(pool, n, j)
                        if s == 16 and n + 1 < len(units):
                            pool_value(pool, n + 1)

            @block.scalar
            def _(act):
                act.wait_ge(e.lr1_in, 32)
                act.activation(lr1[:, 0:2 * D], e.den[:, :], ACT.Copy).then_inc(lr_hi, 1)
                act.activation(lr1[:, 2 * D:FIRST], e.lr1_right[:, :], ACT.Copy).then_inc(lr_hi, 1)
                for t in range(NJ):
                    norm.act_hi(act, t)
                for k in range(2):
                    up.act_hi(act, 0, k)
                act_key(act, 0)
                for t in range(NJ, NT):
                    norm.act_std(act, t)
                act_value(act, 0)
                for o in range(CH1):
                    for r in range(16):
                        if o == 0 and r in SPLIT_AT:
                            norm.act_hi(act, SPLIT_AT[r])
                        if (o, r) == (0, 5):
                            stack_hi(act, lr1, lr_raw, slice(FIRST, NL), lr_in, 16, lr_hi)
                        up.act_step(act, o, r)
                        n, s = divmod(16 * o + r, U_STEPS)
                        for j in range(NJ):
                            if s == SCORES_AT[j] + TANH_AT:
                                act_tanh(act, n, j)
                            if s == SCORES_AT[j] + HI_AT:
                                act_weight(act, n, j)
                        if s == 17 and n + 1 < len(units):
                            act_key(act, n + 1)
                        if s == 19 and n + 1 < len(units):
                            act_value(act, n + 1)
                        if o == CH1 - 1 and r == 13:
                            stack_hi(act, e.lrd1, lrd_raw, slice(0, CH1 * P + D), lrd_in, 16, lrd_hi)

            @block.vector
            def _(dve):
                dve.wait_ge(lr_hi, 1)
                dve.tensor_tensor(lr1[64:96, 0:2 * D], e.den[64:96, :], f32(lr1[64:96, 0:2 * D]), ALU.subtract).then_inc(lr_lo, 1)
                dve.wait_ge(lr_hi, 2)
                dve.tensor_tensor(lr1[32:64, 2 * D:FIRST], e.lr1_right[32:64, :], f32(lr1[32:64, 2 * D:FIRST]),
                                  ALU.subtract).then_inc(lr_lo, 1)
                norm.dve_lo(dve, 0)
                norm.dve_lo(dve, 1)
                for k in range(2):
                    up.dve_combine(dve, 0, k)
                    norm.dve_lo(dve, 2 + k)
                norm.dve_stats(dve, NJ)
                norm.dve_stats(dve, NJ + 1)
                dve_key(dve, 0)
                norm.dve_stats(dve, NJ + 2)
                dve_key_lo(dve, 0)
                norm.dve_stats(dve, NJ + 3)
                for t in range(NJ, NT):
                    norm.dve_norm(dve, t)
                dve_value_lo(dve, 0)
                for o in range(CH1):
                    for r in range(16):
                        if o == 0 and r in SPLIT_AT:
                            norm.dve_lo(dve, SPLIT_AT[r])
                        if (o, r) == (0, 7):
                            stack_lo(dve, lr1, lr_raw, slice(0, 0), slice(FIRST, NL), lr_hi, 3, lr_lo)
                        up.dve_step(dve, o, r)
                        n, s = divmod(16 * o + r, U_STEPS)
                        for j in range(NJ):
                            if s == SCORES_AT[j] + LO_AT:
                                dve_weight_lo(dve, n, j)
                        if n + 1 < len(units):
                            if s == 15:
                                dve_key(dve, n + 1)
                            if s == 18:
                                dve_key_lo(dve, n + 1)
                            if s == 20:
                                dve_value_lo(dve, n + 1)
                        if s == 20:
                            dve_add(dve, n)
                        if o == CH1 - 1 and r == 14:
                            stack_lo(dve, e.lrd1, lrd_raw, slice(0, CH1 * P), slice(CH1 * P, CH1 * P + D), lrd_hi, 1, lrd_lo)
                up.dve_hidden(dve, CH1 - 1, 1)

            @block.tensor
            def _(pe):
                pe.wait_ge(lr_lo, 2)
                for k in range(2):
                    pe.wait_ge(norm.lo, k + 1)
                    up.pe_factor(pe, 0, k)
                for o in range(CH1):
                    for r in range(16):
                        if (o, r) == (0, 0):
                            pe.wait_ge(norm.lo, NJ)
                        if (o, r) == (1, 0):
                            pe.wait_ge(lr_lo, 3)
                        if o == 0 and r in TRANSPOSE_AT:
                            t = TRANSPOSE_AT[r]
                            norm.pe_transpose(pe, t, t - 2 if t >= NJ + 2 else -1)
                        if (o, r) == (0, 8):
                            pe.wait_ge(norm.lo, NT)
                        up.pe_factors(pe, o, r)
                        n, s = divmod(16 * o + r, U_STEPS)
                        if (o, r) == (0, 0):
                            up.pe_step(pe, o, r)
                        for j in range(NJ):
                            if s == SCORES_AT[j]:
                                pe_scores(pe, n, j)
                        if (o, r) != (0, 0):
                            up.pe_step(pe, o, r)
                        for j in range(NJ):
                            if s == VALUES1_AT[j]:
                                pe_values(pe, n, j)


def down1_stage(nc, e, d, out):
    with ExitStack() as ctx:
        sem = lambda n: nc.alloc_semaphore(n)
        down = Down(nc, ctx, "down1", CH1, (ALU.mult, 2.0, ALU.add), e.bank, d["w_down1"], e.lrd1, e.hid1, True,
                    e.down1_raw)
        out_s, stored = sem("out_ready"), sem("stored")

        with nc.Block() as block:
            @block.sync
            def _(sp):
                for o in range(CH1):
                    down.sp_load(sp, o)
                for t in range(NT):
                    sp.wait_ge(out_s, t + 1)
                    sp.dma_start(out[t * P:(t + 1) * P, :], e.acc[:, t, :]).then_inc(stored, 16)
                sp.wait_ge(stored, 16 * NT)

            @block.gpsimd
            def _(pool):
                for b in range(B):
                    for o in range(CH1):
                        down.pool_hlo(pool, b, o)

            @block.scalar
            def _(act):
                for b in range(B):
                    for o in range(CH1):
                        down.act_hhi(act, b, o)
                        if b == 0:
                            down.act_whi(act, o)

            @block.vector
            def _(dve):
                for o in range(CH1):
                    down.dve_combine(dve, o)
                    down.dve_wlo(dve, o)
                for t in range(NT):
                    dve.wait_ge(down.full, t + 1)
                    dve.tensor_tensor(e.acc[:, t, :], e.acc[:, t, :], down.acc(t)[:, :], ALU.add).then_inc(out_s, 1)

            @block.tensor
            def _(pe):
                for o in range(2):
                    down.pe_factor(pe, o)
                for b in range(B):
                    for o in range(CH1):
                        down.pe_chunk(pe, b, o)


def build(nc, d, out):
    e = Env()
    with ExitStack() as ctx:
        def holder(stack, side):
            return lambda n, s, dt=F32: stack.enter_context(nc.sbuf_tensor(n, s, dt, side=side))

        sb = holder(ctx, "left")
        sem = lambda n: nc.alloc_semaphore(n)
        dram = lambda n, s: nc.dram_tensor(n, s, F32, kind="Internal").ap()
        e.bank = [ctx.enter_context(nc.psum_tensor(f"bank{n}", [P, 512], F32)) for n in range(8)]
        e.ident = sb("ident", [P, P])
        e.ident_in, e.mask_in, e.sum0 = sem("ident_in"), sem("mask_in"), sem("x1_ready")
        e.q_hi, e.q_lo = dram("q_hi", (B, 2, FR, HEADS, S)), dram("q_lo", (B, 2, FR, HEADS, S))
        e.k_hi, e.k_lo = dram("k_hi", (B, 2, FR, KV, S)), dram("k_lo", (B, 2, FR, KV, S))
        e.att_dram = dram("att", (B, KV, P, S))
        e.vrow_dram = dram("v_row", (H1, P))
        raw = sb("w_raw", [P, 4, D])
        chunked = raw[:, :, :].rearrange("p (a k) (c m) -> p a k c m", a=2, c=NC)
        e.up0_raw, e.up1_raw = ((chunked, [sem(f"up{n}_w_raw{k}") for k in range(2)]) for n in range(2))
        e.down0_raw, e.down1_raw = ((raw, [sem(f"down{n}_w_raw{k}") for k in range(2)]) for n in range(2))
        e.qk = sb("qk_cols", [P, H1])
        e.vrow = sb("v_rows", [P, D])
        with ExitStack() as layer0, ExitStack() as to_down1:
            e.lrd0 = holder(layer0, "left")("lrd0", [96, CH0 * P + D], F32R)
            with ExitStack() as to_up0:
                sb0 = holder(to_up0, "right")
                e.lr0 = sb0("lr0", [96, 2 * D + 2 * CH0 * P], F32R)
                e.mask = sb0("mask", [P, S])
                e.v = sb0("v_ones", [P, B, NJ, KV, 32])
                e.xT_hi = sb0("x0T_hi", [P, NC, T], F32R)
                e.xT_lo = sb0("x0T_lo", [P, NC, T], F32R)
                qkv_stage(nc, e, d)
                e.hid = holder(layer0, "left")("hidden0", [P, CH0, T])
                attention_stage(nc, e, d)
            e.acc = holder(to_down1, "right")("acc", [P, NT, D])
            with ExitStack() as to_up1:
                e.xn = holder(to_up1, "right")("attention_or_xn", [P, NT, D])
                e.norm1 = Norm(nc, to_up1, "norm1", e.acc, e.xn, lambda t: (e.sum0, t + 1),
                               lambda t: e.bank[t if t < NJ else 6 + t % 2], e.ident, None, None, "right")
                e.den = holder(to_up1, "right")("den_or_left_factors", [96, 2 * D])
                e.lr1_right = holder(to_up1, "right")("right_factors", [96, LR1_FIRST - 2 * D])
                e.lr1_in = sem("lr1_first_loaded")
                down0_stage(nc, e, d)
                layer0.close()
                sb2 = holder(to_up1, "right")
                e.norm1.xT_hi = e.xT_hi = sb2("x1T_hi", [P, NC, T], F32R)
                e.norm1.xT_lo = e.xT_lo = sb2("x1T_lo", [P, NC, T], F32R)
                e.lrd1 = holder(to_down1, "left")("lrd1", [96, CH1 * P + D], F32R)
                layer1_stage(nc, e, d, to_down1)
            down1_stage(nc, e, d, out)


def _stacked(left, right):
    a = np.zeros((96, left.shape[1] + right.shape[1]), left.dtype)
    for g in range(3):
        a[32 * g:32 * g + left.shape[0], :left.shape[1]] = left
        a[32 * g:32 * g + left.shape[0], left.shape[1]:] = right
    return a


def _paired(gate, up, n):
    a = np.zeros((gate.shape[0], n, 2, P), gate.dtype)
    for k, f in enumerate((gate, up)):
        a[:, :, k] = _padded(f, (f.shape[0], n * P)).reshape(-1, n, P)
    return a.reshape(gate.shape[0], -1)


def _chunked(gate, up, n):
    a = np.zeros((2, n * P, D), gate.dtype)
    a[0, :gate.shape[0]] = gate
    a[1, :up.shape[0]] = up
    return np.ascontiguousarray(a.reshape(2, n, P, NC, P).transpose(1, 4, 0, 3, 2))


def _rope_tables():
    inv = (np.float32(1.0) / np.float32(10000.0) ** (np.arange(0, HD, 2, dtype=np.float32) / np.float32(HD))).astype(np.float32)
    angle = (np.arange(S, dtype=np.float32)[:, None] * inv[None, :]).astype(np.float32)
    rep = lambda a: np.ascontiguousarray(np.tile(a.astype(np.float32).T, (P // FR, 1)))
    return rep(np.cos(angle)), rep(np.sin(angle))


def _padded(a, shape):
    out = np.zeros(shape, a.dtype)
    out[tuple(slice(0, n) for n in a.shape)] = a
    return out


def kernel(**inputs):
    import concourse.bacc as _bacc
    from concourse.bass_utils import run_bass_kernel_spmd as _run

    i = {k: np.asarray(v) for k, v in inputs.items()}
    wq = i["L0_attn_w_qkv"]
    q = wq[:, :HEADS * HD].reshape(D, HEADS, FR, 2)
    k = wq[:, HEADS * HD:(HEADS + KV) * HD].reshape(D, KV, FR, 2)
    w_qkv = np.concatenate([q[..., 0].reshape(D, -1), q[..., 1].reshape(D, -1), k[..., 0].reshape(D, -1),
                            k[..., 1].reshape(D, -1), wq[:, (HEADS + KV) * HD:]], axis=1)
    bind = np.zeros((96, P), np.float32)
    for n, name in enumerate(("q", "k", "v")):
        bind[32 * n:32 * n + H1] = i[f"L1_attn_bv_{name}"]
    cos, sin = _rope_tables()
    after = np.arange(P)[None, :] > np.arange(P)[:, None]
    mask = np.where(after, np.float32(NEG), np.float32(0.0))
    heads = np.zeros((HEADS, NC, P), np.float32)
    for c in range(NC):
        for p in range(P):
            heads[c * (P // HD) + p // HD, c, p] = 1.0
    cat = lambda *a: np.concatenate(a, axis=1)
    n1 = CH1 * P
    arrays = {
        "x": np.ascontiguousarray(i["L0_attn_x"].reshape(T, D)),
        "w_qkv": np.ascontiguousarray(w_qkv),
        "w_o": np.ascontiguousarray(i["L0_attn_w_o"]),
        "cos": cos, "sin": sin, "head_rows": heads,
        "ident": np.eye(P, dtype=np.float32),
        "mask": cat(np.zeros((P, S - P), np.float32), mask),
        "w_gate_up0": _chunked(i["L0_ffn_gate_w"], i["L0_ffn_up_w"], CH0),
        "w_gate_up1": _chunked(i["L1_ffn_w1"], i["L1_ffn_w3"], CH1),
        "w_down0": np.ascontiguousarray(i["L0_ffn_down_w"].T),
        "w_down1": _padded(i["L1_ffn_w2"].T, (n1, D)),
        "lr0": _stacked(cat(i["L0_ffn_gate_sv"], i["L0_ffn_up_sv"]), _paired(i["L0_ffn_gate_su"].T, i["L0_ffn_up_su"].T, CH0)),
        "lrd0": _stacked(i["L0_ffn_down_sv"], i["L0_ffn_down_su"].T),
        "lr1": _stacked(cat(i["L1_ffn_lora_A1"], i["L1_ffn_lora_A3"]),
                        _paired(i["L1_ffn_lora_B1"].T, i["L1_ffn_lora_B3"].T, CH1)),
        "lrd1": _stacked(_padded(i["L1_ffn_lora_A2"], (16, n1)), i["L1_ffn_lora_B2"].T),
        "binders": bind,
    }
    nc = _bacc.Bacc("TRN2", target_bir_lowering=False, num_devices=1)
    d = {n: nc.dram_tensor(f"in_{n}", a.shape, mybir.dt.from_np(a.dtype), kind="ExternalInput").ap() for n, a in arrays.items()}
    out = nc.dram_tensor("out", (T, D), F32, kind="ExternalOutput").ap()
    build(nc, d, out)
    r = _run(nc, [{f"in_{n}": a for n, a in arrays.items()}], core_ids=[0])
    return r.results[0]["out"].reshape(B, S, D)
```
